# Optimizing a Trainium2 kernel written in Bass

```python
import numpy as np
import jax
import jax.numpy as jnp

def _softmax(x, axis=-1):
    return jax.nn.softmax(x, axis=axis)

def _gelu(x):
    return jax.nn.gelu(x, approximate=True)

def _silu(x):
    return jax.nn.silu(x)

def _sigmoid(x):
    return jax.nn.sigmoid(x)

def _layernorm(x, axis=-1, eps=1e-05):
    m = jnp.mean(x, axis=axis, keepdims=True)
    v = jnp.var(x, axis=axis, keepdims=True)
    return (x - m) / jnp.sqrt(v + eps)

def _scatter_add(tgt, idx, src, axis=0):
    return tgt.at[idx].add(src)

def _segment_sum(src, seg, n):
    return jax.ops.segment_sum(src, seg, n)
kernel_name = 'mk_gnn_preln_d4_gnn_r8_016533'

def setup_inputs(seed: int=0):
    np.random.seed(seed)
    _w = jnp.asarray

    def _rec_inputs():
        import jax
        import jax.numpy as jnp
        _gk = jax.random.key(seed)
        x = -0.0002928 + 1 * jax.random.normal(jax.random.fold_in(_gk, 1), (6250, 256), jnp.float32)
        src = jax.random.randint(jax.random.fold_in(_gk, 2), (100000,), 0, 6250, jnp.int32)
        dst = jnp.minimum((6250 * jax.random.uniform(jax.random.fold_in(_gk, 3), (100000,)) ** 2.0).astype(jnp.int32), 49999)
        _o = jnp.argsort(dst, stable=True)
        src = src[_o]
        dst = dst[_o]
        edge_attr_4 = 0.00117183 + 1.0004 * jax.random.normal(jax.random.fold_in(_gk, 12), (100000, 4), jnp.float32)
        edge_attr_8 = -0.000615933 + 0.999959 * jax.random.normal(jax.random.fold_in(_gk, 13), (100000, 8), jnp.float32)
        node_vec1 = jax.random.uniform(jax.random.fold_in(_gk, 15), (6250, 1), jnp.float32, 0.0, 1)
        return (x, src, dst, edge_attr_4, edge_attr_8, node_vec1)
    x, src, dst, edge_attr_4, edge_attr_8, node_vec1 = _rec_inputs()

    def _L0_gnn_setup():
        import jax, jax.numpy as jnp
        import numpy as np
        N_NODES = 2048
        N_EDGES = 32768
        D_IN = 256
        D = 256
        H = 512
        E = 64
        TOP_K = 2
        CAP = 1024
        BN_EPS = 1e-05

        def _moe_ff(x, Wg, bg, w1, b1, w2, b2):
            N = x.shape[0]
            logits = x @ Wg + bg
            vals, idx = jax.lax.top_k(logits, TOP_K)
            gates = jax.nn.softmax(vals, axis=-1)
            e_flat = idx.reshape(-1)
            g_flat = gates.reshape(-1)
            tok = jnp.arange(N * TOP_K) // TOP_K
            order = jnp.argsort(e_flat)
            e_s, tok_s, g_s = (e_flat[order], tok[order], g_flat[order])
            counts = jnp.bincount(e_flat, length=E)
            offs = jnp.concatenate([jnp.zeros((1,), counts.dtype), jnp.cumsum(counts)[:-1]])
            rank = jnp.arange(N * TOP_K) - offs[e_s]
            valid = rank < CAP
            slot = jnp.where(valid, e_s * CAP + rank, E * CAP)
            buf = jnp.zeros((E * CAP + 1, D), x.dtype).at[slot].set(x[tok_s])
            h = buf[:E * CAP].reshape(E, CAP, D)
            h1 = jax.nn.gelu(jnp.einsum('ecd,edh->ech', h, w1) + b1[:, None, :], approximate=False)
            h2 = jnp.einsum('ech,ehd->ecd', h1, w2) + b2[:, None, :]
            out_buf = h2.reshape(E * CAP, D)
            y_s = jnp.where(valid[:, None], out_buf[jnp.minimum(slot, E * CAP - 1)], 0.0)
            return jnp.zeros((N, D), x.dtype).at[tok_s].add(g_s[:, None] * y_s)

        def _forward(feats, W_gc, b_gc, W_res, b_res, Wg, bg, w1, b1, w2, b2, gamma, beta, src, dst):
            n = feats.shape[0]
            ones = jnp.ones((src.shape[0],), feats.dtype)
            deg_out = jnp.clip(jax.ops.segment_sum(ones, src, num_segments=n), 1.0)
            deg_in = jnp.clip(jax.ops.segment_sum(ones, dst, num_segments=n), 1.0)
            h = feats * jax.lax.rsqrt(deg_out)[:, None]
            m = jax.ops.segment_sum(h[src], dst, num_segments=n) * jax.lax.rsqrt(deg_in)[:, None]
            gc = m @ W_gc + b_gc
            x = gc + (feats @ W_res + b_res)
            core = _moe_ff(x, Wg, bg, w1, b1, w2, b2)
            y = x + core
            mean = jnp.mean(y, axis=0)
            var = jnp.mean((y - mean) ** 2, axis=0)
            return (y - mean) * jax.lax.rsqrt(var + BN_EPS) * gamma + beta
        key = jax.random.key(seed)
        ks = jax.random.split(key, 16)
        s = lambda d: 1.0 / np.sqrt(d)
        inp = {'feats': jax.random.normal(ks[0], (N_NODES, D_IN), jnp.float32), 'W_gc': jax.random.normal(ks[1], (D_IN, D), jnp.float32) * s(D_IN), 'b_gc': jnp.zeros((D,), jnp.float32), 'W_res': jax.random.normal(ks[2], (D_IN, D), jnp.float32) * s(D_IN), 'b_res': jnp.zeros((D,), jnp.float32), 'Wg': jax.random.normal(ks[3], (D, E), jnp.float32) * s(D), 'bg': jnp.zeros((E,), jnp.float32), 'w1': jax.random.normal(ks[4], (E, D, H), jnp.float32) * s(D), 'b1': jnp.zeros((E, H), jnp.float32), 'w2': jax.random.normal(ks[5], (E, H, D), jnp.float32) * s(H), 'b2': jnp.zeros((E, D), jnp.float32), 'gamma': jnp.ones((D,), jnp.float32), 'beta': jnp.zeros((D,), jnp.float32), 'src': jax.random.randint(ks[6], (N_EDGES,), 0, N_NODES), 'dst': jax.random.randint(ks[7], (N_EDGES,), 0, N_NODES)}
        return inp
    _L0_gnn_all = _L0_gnn_setup()
    _L0_gnn_in = {k: v for k, v in _L0_gnn_all.items() if k in ('W_gc', 'b_gc', 'W_res', 'b_res', 'Wg', 'bg', 'w1', 'b1', 'w2', 'b2', 'gamma', 'beta')}
    del _L0_gnn_all

    def _L1_gnn_setup():
        import jax, jax.numpy as jnp
        import numpy as np
        N_NODES = 12500
        N_EDGES = 200000
        D_IN = 256
        D_OUT = 256
        key = jax.random.key(seed)
        k1, k2, k3, k4, k5 = jax.random.split(key, 5)
        feat = jax.random.normal(k1, (N_NODES, D_IN), dtype=jnp.float32)
        src = jax.random.randint(k2, (N_EDGES,), 0, N_NODES, dtype=jnp.int32)
        dst = jax.random.randint(k3, (N_EDGES,), 0, N_NODES, dtype=jnp.int32)
        gain = float(np.sqrt(2.0))
        limit = gain * float(np.sqrt(6.0 / (D_IN + D_OUT)))
        w_neigh = jax.random.uniform(k4, (D_OUT, D_IN), minval=-limit, maxval=limit, dtype=jnp.float32)
        w_self = jax.random.uniform(k5, (D_OUT, D_IN), minval=-limit, maxval=limit, dtype=jnp.float32)
        b_self = jnp.zeros((D_OUT,), dtype=jnp.float32)
        return {'feat': feat, 'src': src, 'dst': dst, 'w_neigh': w_neigh, 'w_self': w_self, 'b_self': b_self}
    _L1_gnn_all = _L1_gnn_setup()
    _L1_gnn_in = {k: v for k, v in _L1_gnn_all.items() if k in ('w_neigh', 'w_self', 'b_self')}
    del _L1_gnn_all

    def _L2_gnn_setup():
        import jax, jax.numpy as jnp
        import numpy as np
        N_NODES = 6250

        def _gcn_conv(x, edge_index, W, b):
            n = x.shape[0]
            loop = jnp.arange(n, dtype=edge_index.dtype)
            src = jnp.concatenate([edge_index[0], loop])
            dst = jnp.concatenate([edge_index[1], loop])
            h = x @ W
            deg = jax.ops.segment_sum(jnp.ones_like(dst, dtype=h.dtype), dst, num_segments=n)
            dinv = jnp.where(deg > 0, jax.lax.rsqrt(deg), 0.0)
            norm = dinv[src] * dinv[dst]
            msg = h[src] * norm[:, None]
            out = jax.ops.segment_sum(msg, dst, num_segments=n)
            return out + b
        key = jax.random.key(seed)
        k1, k2, k3, k4 = jax.random.split(key, 4)
        in_c, hid = (256, 128)
        x = jax.random.normal(k1, (N_NODES, in_c), dtype=jnp.float32)
        edge_index = jax.random.randint(k2, (2, 100000), 0, N_NODES, dtype=jnp.int32)
        W_conv = jax.random.normal(k3, (in_c, hid), dtype=jnp.float32) * (1.0 / np.sqrt(in_c))
        b_conv = jnp.zeros((hid,), dtype=jnp.float32)
        limit = np.sqrt(6.0 / (hid + in_c))
        W_lin = jax.random.uniform(k4, (hid, in_c), dtype=jnp.float32, minval=-limit, maxval=limit)
        b_lin = jnp.zeros((in_c,), dtype=jnp.float32)
        return {'x': x, 'edge_index': edge_index, 'W_conv': W_conv, 'b_conv': b_conv, 'W_lin': W_lin, 'b_lin': b_lin}
    _L2_gnn_all = _L2_gnn_setup()
    _L2_gnn_in = {k: v for k, v in _L2_gnn_all.items() if k in ('W_conv', 'b_conv', 'W_lin', 'b_lin')}
    del _L2_gnn_all

    def _L3_gnn_setup():
        import jax, jax.numpy as jnp
        import numpy as np
        import math
        N = 3750
        E = 75000
        MUL = 64
        NES = 8
        FCN = 64
        NUM_NEIGHBORS = 20.0
        SILU_NORM = 1.679
        INV_SQRT3 = 1.0 / math.sqrt(3.0)

        def _split(x):
            return (x[:, :MUL], x[:, MUL:].reshape(-1, MUL, 3))
        key = jax.random.key(seed)
        ks = jax.random.split(key, 16)
        inp = {'node_input': jax.random.normal(ks[0], (N, 4 * MUL), jnp.float32), 'node_attr': jnp.ones((N, 1), jnp.float32), 'edge_src': jax.random.randint(ks[1], (E,), 0, N), 'edge_dst': jax.random.randint(ks[2], (E,), 0, N), 'edge_attr': jax.random.normal(ks[3], (E, 4), jnp.float32), 'edge_scalars': jax.random.normal(ks[4], (E, NES), jnp.float32), 'sc_w0': jax.random.normal(ks[5], (MUL, MUL), jnp.float32), 'sc_w1': jax.random.normal(ks[6], (MUL, MUL), jnp.float32), 'lin1_w0': jax.random.normal(ks[7], (MUL, MUL), jnp.float32), 'lin1_w1': jax.random.normal(ks[8], (MUL, MUL), jnp.float32), 'fc_w1': jax.random.normal(ks[9], (NES, FCN), jnp.float32), 'fc_w2': jax.random.normal(ks[10], (FCN, 4 * MUL), jnp.float32), 'lin2_w00': jax.random.normal(ks[11], (MUL, MUL), jnp.float32), 'lin2_w01': jax.random.normal(ks[12], (MUL, MUL), jnp.float32), 'lin2_w10': jax.random.normal(ks[13], (MUL, MUL), jnp.float32), 'lin2_w11': jax.random.normal(ks[14], (MUL, MUL), jnp.float32)}
        return inp
    _L3_gnn_all = _L3_gnn_setup()
    _L3_gnn_in = {k: v for k, v in _L3_gnn_all.items() if k in ('sc_w0', 'sc_w1', 'lin1_w0', 'lin1_w1', 'fc_w1', 'fc_w2', 'lin2_w00', 'lin2_w01', 'lin2_w10', 'lin2_w11')}
    del _L3_gnn_all
    return {'x': x, 'src': src, 'dst': dst, 'edge_attr_4': edge_attr_4, 'edge_attr_8': edge_attr_8, 'node_vec1': node_vec1, 'L0_gnn_W_gc': _L0_gnn_in['W_gc'], 'L0_gnn_b_gc': _L0_gnn_in['b_gc'], 'L0_gnn_W_res': _L0_gnn_in['W_res'], 'L0_gnn_b_res': _L0_gnn_in['b_res'], 'L0_gnn_Wg': _L0_gnn_in['Wg'], 'L0_gnn_bg': _L0_gnn_in['bg'], 'L0_gnn_w1': _L0_gnn_in['w1'], 'L0_gnn_b1': _L0_gnn_in['b1'], 'L0_gnn_w2': _L0_gnn_in['w2'], 'L0_gnn_b2': _L0_gnn_in['b2'], 'L0_gnn_gamma': _L0_gnn_in['gamma'], 'L0_gnn_beta': _L0_gnn_in['beta'], 'L1_gnn_w_neigh': _L1_gnn_in['w_neigh'], 'L1_gnn_w_self': _L1_gnn_in['w_self'], 'L1_gnn_b_self': _L1_gnn_in['b_self'], 'L2_gnn_W_conv': _L2_gnn_in['W_conv'], 'L2_gnn_b_conv': _L2_gnn_in['b_conv'], 'L2_gnn_W_lin': _L2_gnn_in['W_lin'], 'L2_gnn_b_lin': _L2_gnn_in['b_lin'], 'L3_gnn_sc_w0': _L3_gnn_in['sc_w0'], 'L3_gnn_sc_w1': _L3_gnn_in['sc_w1'], 'L3_gnn_lin1_w0': _L3_gnn_in['lin1_w0'], 'L3_gnn_lin1_w1': _L3_gnn_in['lin1_w1'], 'L3_gnn_fc_w1': _L3_gnn_in['fc_w1'], 'L3_gnn_fc_w2': _L3_gnn_in['fc_w2'], 'L3_gnn_lin2_w00': _L3_gnn_in['lin2_w00'], 'L3_gnn_lin2_w01': _L3_gnn_in['lin2_w01'], 'L3_gnn_lin2_w10': _L3_gnn_in['lin2_w10'], 'L3_gnn_lin2_w11': _L3_gnn_in['lin2_w11']}

def reference(x, src, dst, edge_attr_4, edge_attr_8, node_vec1, L0_gnn_W_gc, L0_gnn_b_gc, L0_gnn_W_res, L0_gnn_b_res, L0_gnn_Wg, L0_gnn_bg, L0_gnn_w1, L0_gnn_b1, L0_gnn_w2, L0_gnn_b2, L0_gnn_gamma, L0_gnn_beta, L1_gnn_w_neigh, L1_gnn_w_self, L1_gnn_b_self, L2_gnn_W_conv, L2_gnn_b_conv, L2_gnn_W_lin, L2_gnn_b_lin, L3_gnn_sc_w0, L3_gnn_sc_w1, L3_gnn_lin1_w0, L3_gnn_lin1_w1, L3_gnn_fc_w1, L3_gnn_fc_w2, L3_gnn_lin2_w00, L3_gnn_lin2_w01, L3_gnn_lin2_w10, L3_gnn_lin2_w11):
    import jax
    import jax.numpy as jnp

    def _L0_gnn_ref(feats, W_gc, b_gc, W_res, b_res, Wg, bg, w1, b1, w2, b2, gamma, beta, src, dst):
        import jax, jax.numpy as jnp
        import numpy as np
        N_NODES = 2048
        N_EDGES = 32768
        D_IN = 256
        D = 256
        H = 512
        E = 64
        TOP_K = 2
        CAP = 1024
        BN_EPS = 1e-05

        def _moe_ff(x, Wg, bg, w1, b1, w2, b2):
            N = x.shape[0]
            logits = x @ Wg + bg
            vals, idx = jax.lax.top_k(logits, TOP_K)
            gates = jax.nn.softmax(vals, axis=-1)
            e_flat = idx.reshape(-1)
            g_flat = gates.reshape(-1)
            tok = jnp.arange(N * TOP_K) // TOP_K
            order = jnp.argsort(e_flat)
            e_s, tok_s, g_s = (e_flat[order], tok[order], g_flat[order])
            counts = jnp.bincount(e_flat, length=E)
            offs = jnp.concatenate([jnp.zeros((1,), counts.dtype), jnp.cumsum(counts)[:-1]])
            rank = jnp.arange(N * TOP_K) - offs[e_s]
            valid = rank < CAP
            slot = jnp.where(valid, e_s * CAP + rank, E * CAP)
            buf = jnp.zeros((E * CAP + 1, D), x.dtype).at[slot].set(x[tok_s])
            h = buf[:E * CAP].reshape(E, CAP, D)
            h1 = jax.nn.gelu(jnp.einsum('ecd,edh->ech', h, w1) + b1[:, None, :], approximate=False)
            h2 = jnp.einsum('ech,ehd->ecd', h1, w2) + b2[:, None, :]
            out_buf = h2.reshape(E * CAP, D)
            y_s = jnp.where(valid[:, None], out_buf[jnp.minimum(slot, E * CAP - 1)], 0.0)
            return jnp.zeros((N, D), x.dtype).at[tok_s].add(g_s[:, None] * y_s)

        def _forward(feats, W_gc, b_gc, W_res, b_res, Wg, bg, w1, b1, w2, b2, gamma, beta, src, dst):
            n = feats.shape[0]
            ones = jnp.ones((src.shape[0],), feats.dtype)
            deg_out = jnp.clip(jax.ops.segment_sum(ones, src, num_segments=n), 1.0)
            deg_in = jnp.clip(jax.ops.segment_sum(ones, dst, num_segments=n), 1.0)
            h = feats * jax.lax.rsqrt(deg_out)[:, None]
            m = jax.ops.segment_sum(h[src], dst, num_segments=n) * jax.lax.rsqrt(deg_in)[:, None]
            gc = m @ W_gc + b_gc
            x = gc + (feats @ W_res + b_res)
            core = _moe_ff(x, Wg, bg, w1, b1, w2, b2)
            y = x + core
            mean = jnp.mean(y, axis=0)
            var = jnp.mean((y - mean) ** 2, axis=0)
            return (y - mean) * jax.lax.rsqrt(var + BN_EPS) * gamma + beta
        return _forward(feats, W_gc, b_gc, W_res, b_res, Wg, bg, w1, b1, w2, b2, gamma, beta, src, dst)

    def _L1_gnn_ref(feat, src, dst, w_neigh, w_self, b_self):
        import jax, jax.numpy as jnp
        import numpy as np
        N_NODES = 12500
        N_EDGES = 200000
        D_IN = 256
        D_OUT = 256
        n = feat.shape[0]
        summed = jax.ops.segment_sum(feat[src], dst, num_segments=n)
        deg = jax.ops.segment_sum(jnp.ones_like(dst, dtype=feat.dtype), dst, num_segments=n)
        h_neigh_raw = summed / jnp.maximum(deg, 1.0)[:, None]
        h_neigh = h_neigh_raw @ w_neigh.T
        rst = feat @ w_self.T + b_self + h_neigh
        return rst

    def _L2_gnn_ref(x, edge_index, W_conv, b_conv, W_lin, b_lin):
        import jax, jax.numpy as jnp
        import numpy as np
        N_NODES = 6250

        def _gcn_conv(x, edge_index, W, b):
            n = x.shape[0]
            loop = jnp.arange(n, dtype=edge_index.dtype)
            src = jnp.concatenate([edge_index[0], loop])
            dst = jnp.concatenate([edge_index[1], loop])
            h = x @ W
            deg = jax.ops.segment_sum(jnp.ones_like(dst, dtype=h.dtype), dst, num_segments=n)
            dinv = jnp.where(deg > 0, jax.lax.rsqrt(deg), 0.0)
            norm = dinv[src] * dinv[dst]
            msg = h[src] * norm[:, None]
            out = jax.ops.segment_sum(msg, dst, num_segments=n)
            return out + b
        h = _gcn_conv(x, edge_index, W_conv, b_conv)
        return h @ W_lin + b_lin

    def _L3_gnn_ref(node_input, node_attr, edge_src, edge_dst, edge_attr, edge_scalars, sc_w0, sc_w1, lin1_w0, lin1_w1, fc_w1, fc_w2, lin2_w00, lin2_w01, lin2_w10, lin2_w11):
        import jax, jax.numpy as jnp
        import numpy as np
        import math
        N = 3750
        E = 75000
        MUL = 64
        NES = 8
        FCN = 64
        NUM_NEIGHBORS = 20.0
        SILU_NORM = 1.679
        INV_SQRT3 = 1.0 / math.sqrt(3.0)

        def _split(x):
            return (x[:, :MUL], x[:, MUL:].reshape(-1, MUL, 3))
        n = node_input.shape[0]
        inv_mul = 1.0 / math.sqrt(MUL)
        x0, x1 = _split(node_input)
        a = node_attr
        s0 = x0 @ sc_w0 * a * inv_mul
        s1 = jnp.einsum('nuc,uv->nvc', x1, sc_w1) * a[:, :, None] * inv_mul
        y0 = x0 @ lin1_w0 * a * inv_mul
        y1 = jnp.einsum('nuc,uv->nvc', x1, lin1_w1) * a[:, :, None] * inv_mul
        h = jax.nn.silu(edge_scalars @ fc_w1 * (1.0 / math.sqrt(NES))) * SILU_NORM
        w = h @ fc_w2 * (1.0 / math.sqrt(FCN))
        w_a, w_b, w_c, w_d = (w[:, :MUL], w[:, MUL:2 * MUL], w[:, 2 * MUL:3 * MUL], w[:, 3 * MUL:])
        xg0 = y0[edge_src]
        xg1 = y1[edge_src]
        ea0 = edge_attr[:, :1]
        ea1 = edge_attr[:, 1:4]
        mid0 = w_a * xg0 * ea0
        mid1 = w_b * jnp.einsum('euc,ec->eu', xg1, ea1) * INV_SQRT3
        mid2 = (w_c * xg0)[:, :, None] * ea1[:, None, :]
        mid3 = (w_d * ea0)[:, :, None] * xg1
        mids = jnp.concatenate([mid0, mid1, mid2.reshape(-1, 3 * MUL), mid3.reshape(-1, 3 * MUL)], axis=1)
        agg = jax.ops.segment_sum(mids, edge_dst, num_segments=n)
        agg = agg * (1.0 / math.sqrt(NUM_NEIGHBORS))
        z0a = agg[:, :MUL]
        z0b = agg[:, MUL:2 * MUL]
        z1a = agg[:, 2 * MUL:5 * MUL].reshape(n, MUL, 3)
        z1b = agg[:, 5 * MUL:].reshape(n, MUL, 3)
        inv2 = 1.0 / math.sqrt(2 * MUL)
        o0 = (z0a @ lin2_w00 + z0b @ lin2_w01) * a * inv2
        o1 = (jnp.einsum('nuc,uv->nvc', z1a, lin2_w10) + jnp.einsum('nuc,uv->nvc', z1b, lin2_w11)) * a[:, :, None] * inv2
        c_s = math.sin(math.pi / 8.0)
        c_x = math.cos(math.pi / 8.0)
        out0 = c_s * s0 + c_x * o0
        out1 = c_s * s1 + c_x * o1
        return jnp.concatenate([out0, out1.reshape(n, 3 * MUL)], axis=1)
    edge_index = jnp.stack([src, dst])
    h = jnp.maximum(_layernorm(x, axis=-1), 0.0)
    x = x + _L0_gnn_ref(h, L0_gnn_W_gc, L0_gnn_b_gc, L0_gnn_W_res, L0_gnn_b_res, L0_gnn_Wg, L0_gnn_bg, L0_gnn_w1, L0_gnn_b1, L0_gnn_w2, L0_gnn_b2, L0_gnn_gamma, L0_gnn_beta, src, dst)
    h = jnp.maximum(_layernorm(x, axis=-1), 0.0)
    x = x + _L1_gnn_ref(h, src, dst, L1_gnn_w_neigh, L1_gnn_w_self, L1_gnn_b_self)
    h = jnp.maximum(_layernorm(x, axis=-1), 0.0)
    x = x + _L2_gnn_ref(h, edge_index, L2_gnn_W_conv, L2_gnn_b_conv, L2_gnn_W_lin, L2_gnn_b_lin)
    h = jnp.maximum(_layernorm(x, axis=-1), 0.0)
    x = x + _L3_gnn_ref(h, node_vec1, src, dst, edge_attr_4, edge_attr_8, L3_gnn_sc_w0, L3_gnn_sc_w1, L3_gnn_lin1_w0, L3_gnn_lin1_w1, L3_gnn_fc_w1, L3_gnn_fc_w2, L3_gnn_lin2_w00, L3_gnn_lin2_w01, L3_gnn_lin2_w10, L3_gnn_lin2_w11)
    return x

_drawn_inputs = setup_inputs


def setup_inputs(seed=0):
    import zlib

    import numpy as np

    out = dict(_drawn_inputs(seed))
    spreads = {'L0_gnn_b_gc': (0.0, 0.1),
     'L0_gnn_b_res': (0.0, 0.1),
     'L0_gnn_bg': (0.0, 0.1),
     'L0_gnn_b1': (0.0, 0.1),
     'L0_gnn_b2': (0.0, 0.1),
     'L0_gnn_gamma': (1.0, 0.2),
     'L0_gnn_beta': (0.0, 0.1),
     'L1_gnn_b_self': (0.0, 0.1),
     'L2_gnn_b_conv': (0.0, 0.1),
     'L2_gnn_b_lin': (0.0, 0.1)}
    factors = {}
    for name, (base, spread) in spreads.items():
        noise = np.random.default_rng([zlib.crc32(name.encode()), seed]).standard_normal(out[name].shape)
        drawn = base * np.exp(spread * noise) if base else spread * noise
        out[name] = jnp.asarray(drawn.astype(out[name].dtype))
    for name, factor in factors.items():
        out[name] = (out[name] * factor).astype(out[name].dtype)
    return out
```

```python
from contextlib import ExitStack

import numpy as np

import concourse.bass as bass
from concourse import mybir

F32 = mybir.dt.float32
I32 = mybir.dt.int32
U32 = mybir.dt.uint32
BF16 = mybir.dt.bfloat16
ALU = mybir.AluOpType
ACT = mybir.ActivationFunctionType
AX_X = mybir.AxisListType.X
ds = bass.ds

N = 6250
E = 100000
D = 256
P = 125
T = N // P
Q = 128
WIN = 2 * Q
WPI = 8
WINDOWS = -(-((E + T * (WIN - 1)) // WIN) // WPI) * WPI
EC = E // P
X_EXP = 64
HID = 512
CAP = 1024
MT = -(-((2 * N + X_EXP * (Q - 1)) // Q) // 6) * 6
TOK_ROWS = MT * Q
MUL = 64
LN_EPS = 1e-5
BN_EPS = 1e-5
assert N == P * T and E == P * EC and T % 2 == 0


class Chain:

    def __init__(self, eng, sem, base=0):
        self.eng, self.sem, self.base, self.n = eng, sem, base, 0

    def __call__(self, ins):
        self.n += 1
        ins.then_inc(self.sem, 1)
        self.eng.wait_ge(self.sem, self.base + self.n)


def for_tiles(eng, count, body, ahead=(), ring=2):
    def step(t, b, first, last_b):
        for lead, f in ahead:
            if last_b is None or last_b + lead < ring:
                f(t + lead, (b + lead) % ring, first and b + lead < ring)
        body(t, b, first)

    for lead in sorted({k for k, _ in ahead}, reverse=True):
        for k, f in ahead:
            if k == lead:
                for t in range(k):
                    f(t, t % ring, True)
    for t in range(ring):
        step(t, t, True, None)
    if count > 2 * ring:
        with eng.Fori(1, count // ring - 1) as i:
            for b in range(ring):
                step(ring * i + b, b, False, None)
    for b in range(ring):
        step(count - ring + b, b, False, b)


def carry_wait(eng, sem):
    eng.sem_inc(sem, 1)


def bc(ap, axis, shape):
    return ap.unsqueeze(axis).broadcast_to(shape)


class Net:

    def __init__(self, nc, ctx, a):
        self.nc, self.a = nc, a

        def sb(name, shape, dt=F32):
            return ctx.enter_context(nc.sbuf_tensor(name, shape, dt))

        self.x = sb("x_res", [P, T, D])
        self.acc_full = sb("acc", [Q, T * 2 * D])
        self.acc = self.acc_full[0:P, :]
        self.src_w = sb("src_w", [Q, 2 * WINDOWS], I32)
        self.dst_w = sb("dst_w", [Q, 2 * WINDOWS])
        self.win_tab = sb("win_tab", [1, 2 * WINDOWS], I32)
        self.ident = sb("ident", [Q, Q])
        self.iota_i = sb("iota_i", [Q, WINDOWS])
        self.part_i = sb("part_i", [Q, 2])
        self.ones = sb("ones", [Q, Q])
        self.tri = sb("tri", [Q, Q])
        self.deg_out = sb("deg_out", [P, T])
        self.deg_in = sb("deg_in", [P, T])
        self.ra = sb("ra", [P, T])
        self.rb = sb("rb", [P, T])
        self.rc = sb("rc", [P, T])
        self.stats = sb("stats", [P, T, 6])
        self.mv = sb("mv", [P, T, 2])
        self.rstd = sb("rstd", [P, T])
        self.nmr = sb("nmr", [P, T])
        self.eps = sb("eps", [Q, 1])
        self.bank = [ctx.enter_context(nc.psum_tensor(f"bank{i}", [Q, 512], F32)) for i in range(8)]
        self.used = []

    def acc_view(self, width):
        return self.acc[:, 0:T * width].rearrange("p (t d) -> p t d", d=width)

    def phase(self, name):
        return Phase(self, name)


class Phase:

    def __init__(self, net, name):
        self.net, self.nc, self.name = net, net.nc, name
        self.ctx = ExitStack()
        if len(net.used) > 120:
            self.nc.clear_and_free_semaphores(net.used)
            self.nc.all_engine_barrier()
            net.used = []

    def __enter__(self):
        return self

    def __exit__(self, *e):
        return self.ctx.__exit__(*e)

    def sb(self, name, shape, dt=F32):
        return self.ctx.enter_context(self.nc.sbuf_tensor(f"{self.name}_{name}", shape, dt))

    def sem(self, name):
        sem = self.nc.alloc_semaphore(f"{self.name}_{name}")
        self.net.used.append(sem)
        return sem

    def block(self):
        return self.nc.Block()



def ceil_div(step, dve, out, x, divisor, whole, over):
    step(dve.tensor_scalar(out, x, 1.0 / divisor, None, ALU.mult))
    step(dve.tensor_copy(whole, out))
    step(dve.tensor_copy(over, whole))
    step(dve.tensor_tensor(out, out, over, ALU.subtract))
    step(dve.tensor_scalar(out, out, 0.0, None, ALU.is_gt))
    step(dve.tensor_tensor(out, out, over, ALU.add))


def split_node(step, dve, ids, tile, lane, whole):
    step(dve.tensor_copy(lane, ids))
    step(dve.tensor_scalar(whole, lane, 1.0 / P, None, ALU.mult))
    step(dve.tensor_copy(tile, whole))
    step(dve.scalar_tensor_tensor(lane, tile, -float(P), lane, ALU.mult, ALU.add))
    low = whole.bitcast(F32)
    step(dve.tensor_scalar(low, lane, 0.0, None, ALU.is_lt))
    step(dve.tensor_tensor(tile, tile, low, ALU.subtract))
    step(dve.scalar_tensor_tensor(lane, low, float(P), lane, ALU.mult, ALU.add))
    step(dve.tensor_scalar(low, lane, float(P), None, ALU.is_ge))
    step(dve.tensor_tensor(tile, tile, low, ALU.add))
    step(dve.scalar_tensor_tensor(lane, low, -float(P), lane, ALU.mult, ALU.add))


def prepare(net):
    nc, a = net.nc, net.a
    COLS = 8
    with net.phase("prep") as ph:
        base = net.acc
        ids = [base[:, k * EC:(k + 1) * EC].bitcast(I32) for k in (0, 1)]
        tiles = [base[:, (2 + k) * EC:(3 + k) * EC] for k in (0, 1)]
        lanes = [base[:, (4 + k) * EC:(5 + k) * EC] for k in (0, 1)]
        whole = [base[:, (6 + k) * EC:(7 + k) * EC].bitcast(I32) for k in (0, 1)]
        lane_hot = [ph.sb(f"lane_hot{k}", [P, COLS, P], BF16) for k in (0, 1)]
        tile_hot = [ph.sb(f"tile_hot{k}", [P, COLS, T], BF16) for k in (0, 1)]
        zero_bf = ph.sb("zero_bf", [P, P], BF16)
        col = ph.sb("col", [T, 8])
        coli = ph.sb("coli", [T, 1], I32)
        past = ph.sb("past", [T, WINDOWS])
        base_row = ph.sb("base_row", [Q, WINDOWS])
        erow = ph.sb("erow", [1, WINDOWS])
        edges_w = ph.sb("edges_w", [Q, 4 * WINDOWS], I32)
        s_const, s_x, s_ids = ph.sem("const"), ph.sem("x"), [ph.sem("src"), ph.sem("dst")]
        s_step, s_hot, s_used, s_hist = ph.sem("step"), ph.sem("hot"), ph.sem("used"), ph.sem("hist")
        s_deg, s_cnt, s_pairs, s_end = ph.sem("deg"), ph.sem("cnt"), ph.sem("pairs"), ph.sem("end")
        s_past, s_sum, s_tab, s_win = ph.sem("past"), ph.sem("sum"), ph.sem("tab"), ph.sem("win")
        s_win2, s_zero = ph.sem("win2"), ph.sem("zero")
        hist = net.bank[0:2]
        tile_h, first_h, base_h = net.bank[2], net.bank[3], net.bank[4]
        small = net.bank[5]
        edge_rows = a["edge_index"]

        with ph.block() as block:
            @block.gpsimd
            def _(pool):
                pool.memset(net.ones[:, :], 1.0).then_inc(s_const, 1)
                pool.memset(net.eps[:, :], LN_EPS).then_inc(s_const, 1)
                pool.iota(net.iota_i[:, :], [[1, WINDOWS]], base=0, channel_multiplier=0,
                          allow_small_or_imprecise_dtypes=True).then_inc(s_const, 1)
                pool.iota(net.part_i[:, :], [[0, 2]], base=0, channel_multiplier=1,
                          allow_small_or_imprecise_dtypes=True).then_inc(s_const, 1)
                pool.wait_ge(s_const, 4)
                pool.affine_select(out=net.ident[:, :], in_=net.ones[:, :], compare_op=ALU.is_equal, fill=0.0,
                                   base=0, pattern=[[-1, Q]], channel_multiplier=1).then_inc(s_const, 1)
                pool.affine_select(out=net.tri[:, :], in_=net.ones[:, :], compare_op=ALU.is_ge, fill=0.0,
                                   base=-1, pattern=[[1, Q]], channel_multiplier=-1).then_inc(s_const, 1)

            def load_windows(eng, first, count, sem):
                eng.wait_ge(s_tab, 2)
                with eng.Fori(first, first + count) as w:
                    e0 = eng.value_load(net.win_tab[0:1, ds(WINDOWS + w, 1)], min_val=0, max_val=E)
                    eng.dma_start(edges_w[:, ds(4 * w, 4)],
                                  edge_rows[ds(e0, WIN), :].rearrange("(p j) w -> p (j w)", j=2)).then_inc(sem, 16)

            @block.sync
            def _(sp):
                for k, name in enumerate(("src", "dst")):
                    sp.dma_start(ids[k], a[name].rearrange("(p c) -> p c", c=EC)).then_inc(s_ids[k], 16)
                xv = a["x"].rearrange("(t p) d -> p t d", p=P)
                sp.dma_start(net.x[:, :, :], xv).then_inc(s_x, 16)
                load_windows(sp, 0, WINDOWS // 2, s_win)
                sp.wait_ge(s_x, 16)

            @block.scalar
            def _(act):
                load_windows(act, WINDOWS // 2, WINDOWS // 2, s_win2)

            @block.vector
            def _(dve):
                step = Chain(dve, s_step)
                dve.memset(zero_bf[:, :], 0.0).then_inc(s_zero, 1)
                dve.wait_ge(s_const, 6)
                for k in (0, 1):
                    dve.wait_ge(s_ids[k], 16)
                    split_node(step, dve, ids[k], tiles[k], lanes[k], whole[k])
                with dve.Fori(0, EC // COLS) as g:
                    for k in (0, 1):
                        dve.wait_ge(s_used, 2 * g + 1 + k)
                        dve.tensor_tensor(lane_hot[k][:, :, :], bc(lanes[k][:, ds(COLS * g, COLS)], 2, [P, COLS, P]),
                                          bc(net.iota_i[0:P, 0:P], 1, [P, COLS, P]), ALU.is_equal).then_inc(s_hot, 1)
                        dve.tensor_tensor(tile_hot[k][:, :, :], bc(tiles[k][:, ds(COLS * g, COLS)], 2, [P, COLS, T]),
                                          bc(net.iota_i[0:P, 0:T], 1, [P, COLS, T]), ALU.is_equal).then_inc(s_hot, 1)
                dve.wait_ge(s_hist, 2)
                dve.tensor_scalar(net.deg_out[:, :], hist[0][0:P, 0:T], 1.0, None, ALU.max)
                dve.tensor_copy(net.deg_in[:, :], hist[1][0:P, 0:T]).then_inc(s_deg, 1)
                dve.wait_ge(s_cnt, 1)
                step(dve.tensor_copy(col[:, 0:1], small[0:T, 0:1]))
                ceil_div(step, dve, col[:, 1:2], col[:, 0:1], WIN, coli[:, :], col[:, 2:3])
                dve.scalar_tensor_tensor(col[:, 3:4], col[:, 1:2], -float(WIN), col[:, 0:1],
                                         ALU.mult, ALU.add).then_inc(s_pairs, 1)
                dve.wait_ge(s_end, 1)
                step(dve.tensor_tensor(col[:, 4:5], small[0:T, 1:2], col[:, 1:2], ALU.add))
                dve.tensor_scalar(past[:, :], net.iota_i[0:T, :], col[:, 4:5], None, ALU.is_ge).then_inc(s_past, 1)
                dve.wait_ge(s_sum, 3)
                dve.tensor_scalar(net.win_tab[0:1, 0:WINDOWS], tile_h[0:1, 0:WINDOWS], float(T - 1), None,
                                  ALU.min).then_inc(s_tab, 1)
                step(dve.scalar_tensor_tensor(erow[:, :], net.iota_i[0:1, :], float(WIN), first_h[0:1, 0:WINDOWS],
                                              ALU.mult, ALU.add))
                dve.tensor_scalar(net.win_tab[0:1, WINDOWS:2 * WINDOWS], erow[:, :], float(E), None,
                                  ALU.min).then_inc(s_tab, 1)
                step(dve.tensor_scalar(base_row[:, :], base_h[:, 0:WINDOWS], float(T - 1), float(P),
                                       ALU.min, ALU.mult))
                dve.wait_ge(s_win, 16 * (WINDOWS // 2))
                dve.wait_ge(s_win2, 16 * (WINDOWS // 2))
                got = edges_w[:, :].rearrange("p (w j k) -> p w j k", j=2, k=2)
                dve.tensor_copy(net.src_w[:, :].rearrange("p (w j) -> p w j", j=2), got[:, :, :, 0])
                dve.tensor_tensor(net.dst_w[:, :].rearrange("p (w j) -> p w j", j=2), got[:, :, :, 1],
                                  bc(base_row[:, :], 2, [Q, WINDOWS, 2]), ALU.subtract)

            @block.tensor
            def _(pe):
                pe.wait_ge(s_zero, 1)
                for k in (0, 1):
                    pe.matmul(hist[k][0:P, 0:T], zero_bf[:, :], zero_bf[:, 0:T], start=True, stop=False,
                              skip_group_check=True).then_inc(s_used, 1)
                with pe.Fori(0, EC // COLS) as g:
                    for k in (0, 1):
                        pe.wait_ge(s_hot, 4 * g + 2 + 2 * k)
                        for j in range(COLS):
                            mm = pe.matmul(hist[k][0:P, 0:T], lane_hot[k][:, j, :], tile_hot[k][:, j, :],
                                           start=False, stop=False, skip_group_check=True)
                        mm.then_inc(s_used, 1)
                for k in (0, 1):
                    pe.matmul(hist[k][0:P, 0:T], zero_bf[:, :], zero_bf[:, 0:T], start=False, stop=True,
                              skip_group_check=True).then_inc(s_hist, 1)
                pe.wait_ge(s_deg, 1)
                pe.matmul(small[0:T, 0:1], net.deg_in[:, :], net.ones[0:P, 0:1], start=True, stop=True).then_inc(s_cnt, 1)
                pe.wait_ge(s_pairs, 1)
                pe.matmul(small[0:T, 1:2], net.tri[0:T, 0:T], col[:, 1:2], start=True, stop=True).then_inc(s_end, 1)
                pe.wait_ge(s_past, 1)
                pe.matmul(tile_h[0:1, 0:WINDOWS], net.ones[0:T, 0:1], past[:, :], start=True, stop=True).then_inc(s_sum, 1)
                pe.matmul(first_h[0:1, 0:WINDOWS], col[:, 3:4], past[:, :], start=True, stop=True).then_inc(s_sum, 1)
                pe.matmul(base_h[:, 0:WINDOWS], net.ones[0:T, :], past[:, :], start=True, stop=True).then_inc(s_sum, 1)



def layer_stats(net, tag, factors):
    with net.phase(tag) as ph:
        s_stat, s_step, s_var, s_root = ph.sem("stat"), ph.sem("step"), ph.sem("var"), ph.sem("root")
        s_own, s_own2 = ph.sem("own"), ph.sem("own2")
        with ph.block() as block:
            @block.vector
            def _(dve):
                with dve.Fori(0, T) as t:
                    dve.bn_stats(net.stats[:, ds(t, 1), :].rearrange("p a b -> p (a b)"),
                                 net.x[:, ds(t, 1), :].rearrange("p a d -> p (a d)")).then_inc(s_stat, 1)
                dve.wait_ge(s_stat, T)
                for t in range(T):
                    dve.bn_aggr(net.mv[:, t, :], net.stats[:, t, :]).then_inc(s_var, 1)
                step = Chain(dve, s_step)
                dve.wait_ge(s_root, 1)
                step(dve.reciprocal(net.rstd[:, :], net.rstd[:, :]))
                step(dve.scalar_tensor_tensor(net.nmr[:, :], net.mv[:, :, 0], -1.0, net.rstd[:, :],
                                              ALU.mult, ALU.mult))
                factors(step, dve, None, s_own, s_own2)

            @block.scalar
            def _(act):
                act.wait_ge(s_var, T)
                act.activation(net.rstd[:, :], net.mv[:, :, 1], ACT.Sqrt, bias=net.eps[0:P, :]).then_inc(s_root, 1)
                factors(None, None, act, s_own, s_own2)


def node_row(view, t):
    return view[:, ds(t, 1), :].rearrange("p a d -> p (a d)")


def write_table(net, tag, table, scale, bias):
    with net.phase(tag) as ph:
        row = [ph.sb(f"row{b}", [P, D]) for b in (0, 1)]
        s_row, s_out = ph.sem("row"), [ph.sem("out0"), ph.sem("out1")]
        with ph.block() as block:
            @block.scalar
            def _(act):
                def body(t, b, first):
                    if not first:
                        act.wait_ge(s_out[b], (t - b) * 8)
                    act.activation(row[b][:, :], node_row(net.x, t), ACT.Relu, bias=bias[:, ds(t, 1)],
                                   scale=scale[:, ds(t, 1)]).then_inc(s_row, 1)
                for_tiles(act, T, body)

            @block.sync
            def _(sp):
                def body(t, b, first):
                    sp.wait_ge(s_row, t + 1)
                    sp.dma_start(table[ds(P * t, P), :], row[b][:, :]).then_inc(s_out[b], 16)
                for_tiles(sp, T, body)
                for b in (0, 1):
                    sp.wait_ge(s_out[b], 16 * (T // 2))



def aggregate(net, tag, table, width, clear=None):
    acc = net.acc_view(width)
    SLOTS = 2 * WPI
    GROUPS = WPI // 2
    STEPS = WINDOWS // WPI
    LEAD = 2
    with net.phase(tag) as ph:
        msg = [ph.sb(f"msg{r}", [Q, width]) for r in range(SLOTS)]
        hot = [ph.sb(f"hot{r}", [Q, P]) for r in range(SLOTS)]
        idx = [ph.sb(f"idx{g}", [Q, 4], I32) for g in range(GROUPS)]
        s_idx, s_idle = ph.sem("idx"), ph.sem("idle")
        s_msg = [ph.sem(f"msg{r}") for r in range(SLOTS)]
        s_hot, s_sum, s_add, s_clear = ph.sem("hot"), ph.sem("sum"), ph.sem("add"), ph.sem("clear")
        if clear is not None:
            zero, s_zero, s_filled = ph.sb("zero", [Q, 6 * D]), ph.sem("zero"), ph.sem("filled")
        with ph.block() as block:
            @block.gpsimd
            def _(pool):
                with pool.Fori(0, STEPS) as i:
                    for g in range(GROUPS):
                        pool.wait_ge(s_idx, GROUPS * i + g + 1)
                        carry_wait(pool, s_idle)
                        for r in range(4 * g, 4 * g + 4):
                            pool.indirect_dma_start(
                                out=msg[r][:, :], out_offset=None, in_=table[:, :],
                                in_offset=bass.IndirectOffsetOnAxis(ap=idx[g][:, r % 4:r % 4 + 1], axis=0),
                            ).then_inc(s_msg[r], 16)

            @block.vector
            def _(dve):
                def stage(i, g):
                    dve.wait_ge(s_sum, WPI * i + 2 * g + 2)
                    dve.tensor_copy(idx[g][:, :].bitcast(F32),
                                    net.src_w[:, ds(2 * WPI * i + 4 * g, 4)].bitcast(F32)).then_inc(s_idx, 1)
                    for r in range(4 * g, 4 * g + 4):
                        dve.tensor_scalar(hot[r][:, :], net.iota_i[:, 0:P],
                                          net.dst_w[:, ds(2 * WPI * i + r, 1)], None,
                                          ALU.is_equal).then_inc(s_hot, 1)

                def add(i, w):
                    tile = dve.value_load(net.win_tab[0:1, ds(WPI * i + w, 1)], min_val=0, max_val=T - 1)
                    dve.wait_ge(s_sum, WPI * i + w + 1 + WPI)
                    dve.wait_ge(s_add, WPI * i + w + 1)
                    row = node_row(acc, tile)
                    dve.tensor_tensor(row, row, net.bank[w][0:P, 0:width], ALU.add).then_inc(s_add, 1)

                def steps(i, last):
                    for g in range(GROUPS):
                        add(i, 2 * g)
                        add(i, 2 * g + 1)
                        if g + LEAD < GROUPS:
                            stage(i, g + LEAD)
                        elif not last:
                            stage(i + 1, g + LEAD - GROUPS)

                dve.memset(net.acc[:, 0:T * width], 0.0).then_inc(s_clear, 1)
                dve.sem_inc(s_add, 1)
                for g in range(LEAD):
                    stage(0, g)
                dve.wait_ge(s_clear, 1)
                with dve.Fori(0, STEPS - 1) as i:
                    steps(i, False)
                steps(STEPS - 1, True)

            @block.tensor
            def _(pe):
                pe.sem_inc(s_sum, WPI)
                with pe.Fori(0, STEPS) as i:
                    for w in range(WPI):
                        for r in (2 * w, 2 * w + 1):
                            pe.wait_ge(s_hot, SLOTS * i + r + 1)
                            pe.wait_ge(s_msg[r], 16 * i + 16)
                            mm = pe.matmul(net.bank[w][0:P, 0:width], hot[r][:, :], msg[r][:, :],
                                           start=(r % 2 == 0), stop=(r % 2 == 1))
                        mm.then_inc(s_sum, 1)

            if clear is not None:
                @block.scalar
                def _(act):
                    act.activation(zero[:, :], net.iota_i[:, 0:1].broadcast_to([Q, 6 * D]), ACT.Copy,
                                   scale=0.0).then_inc(s_zero, 1)

                @block.sync
                def _(sp):
                    sp.wait_ge(s_zero, 1)
                    with sp.Fori(0, MT // 6) as g:
                        sp.dma_start(clear[ds(6 * Q * g, 6 * Q), :].rearrange("(p r) d -> p (r d)", p=Q),
                                     zero[:, :]).then_inc(s_filled, 16)
                    sp.wait_ge(s_filled, 16 * (MT // 6))



def node_stage(net, tag, chunks, load, stage, products, finish, steps=0, store=None):
    with net.phase(tag) as ph:
        rows = [ph.sb(f"rows{b}", [P, chunks * Q]) for b in (0, 1)]
        cols = [ph.sb(f"cols{b}", [Q, chunks, P]) for b in (0, 1)]
        turned, product = net.bank[0:2], net.bank[2:4]
        s_w, s_staged, s_turned, s_copied = ph.sem("w"), ph.sem("staged"), ph.sem("turned"), ph.sem("copied")
        s_product, s_finished, s_step = ph.sem("product"), ph.sem("finished"), ph.sem("step")
        s_stored = [ph.sem("stored0"), ph.sem("stored1")]
        s_init = ph.sem("init")
        loads = load(None, ph, None)
        with ph.block() as block:
            @block.sync
            def _(sp):
                load(sp, ph, s_w)
                if store:
                    def body(t, b, first):
                        sp.wait_ge(s_finished, t + 1)
                        store(sp, t, b).then_inc(s_stored[b], 16)
                    for_tiles(sp, T, body)
                    for b in (0, 1):
                        sp.wait_ge(s_stored[b], 16 * (T // 2))

            @block.scalar
            def _(act):
                def body(t, b, first):
                    if not first:
                        act.wait_ge(s_turned, t - 1)
                    stage(act, t, rows[b]).then_inc(s_staged, 1)
                for_tiles(act, T, body)

            @block.tensor
            def _(pe):
                def turn(t, b, first):
                    pe.wait_ge(s_staged, t + 1)
                    for c in range(chunks):
                        mm = pe.transpose(turned[b][:, c * P:(c + 1) * P], rows[b][:, c * Q:(c + 1) * Q],
                                          net.ident[0:P, 0:P])
                    mm.then_inc(s_turned, 1)

                def body(t, b, first):
                    pe.wait_ge(s_copied, t + 1)
                    if not first:
                        pe.wait_ge(s_finished, t - 1)
                    products(pe, cols[b], product[b]).then_inc(s_product, 1)
                pe.wait_ge(s_w, 16 * loads)
                for_tiles(pe, T, body, ahead=((1, turn),))

            @block.vector
            def _(dve):
                def copy(t, b, first):
                    dve.wait_ge(s_turned, t + 1)
                    dve.tensor_copy(cols[b][:, :, :].rearrange("p c n -> p (c n)"),
                                    turned[b][:, 0:chunks * P]).then_inc(s_copied, 1)

                def body(t, b, first):
                    dve.wait_ge(s_product, t + 1)
                    if store and not first:
                        dve.wait_ge(s_stored[b], (t - b) * 8)
                    step = Chain(dve, s_step, t * steps)
                    finish(dve, step, t, b, product[b]).then_inc(s_finished, 1)
                    assert step.n == steps
                dve.wait_ge(s_w, 16 * loads)
                for_tiles(dve, T, body, ahead=((1, copy),))


def loader(*items):
    def load(sp, ph, sem):
        n = 0
        if sp is None:
            ph.net.got = {}
            for name, shape, _ in items:
                ph.net.got[name] = ph.sb(name, shape)
        for name, _, pairs in items:
            for to, of in pairs(ph.net.got[name]):
                n += 1
                if sp is not None:
                    sp.dma_start(to, of).then_inc(sem, 16)
        return n
    return load


def row_of(vector, parts=P):
    return vector.unsqueeze(0).broadcast_to([parts, vector.shape[0]])


def in_chunks(w):
    return w.rearrange("(c p) n -> p c n", p=Q)



def experts(net, buf, outb, exp_row):
    nc, a = net.nc, net.a
    xm = net.acc_view(D)
    with ExitStack() as ctx:
        def sb(name, shape, dt=F32):
            return ctx.enter_context(nc.sbuf_tensor(f"moe_{name}", shape, dt))

        mask = sb("mask", [P, T, X_EXP])
        val = sb("val", [P, T, 2])
        exp_of = sb("exp_of", [P, T, 2])
        rank = sb("rank", [P, T, 2])
        gate = sb("gate", [P, T, 2])
        valid = sb("valid", [P, T, 2])
        put = sb("put", [P, T, 2], I32)
        get = sb("get", [P, T, 2], I32)
        exp_tab = sb("exp_tab", [1, MT], I32)

        s_idle = nc.alloc_semaphore("route_idle")
        logits, top, top_i = sb("logits", [P, X_EXP]), sb("top", [P, 8]), sb("top_i", [P, 8], U32)

        def stage(act, t, rows):
            return act.activation(rows[:, :], node_row(xm, t), ACT.Copy)

        def products(pe, cols, po):
            for c in (0, 1):
                mm = pe.matmul(po[0:P, 0:X_EXP], cols[:, c, :], net.got["wg"][:, c, :], start=(c == 0), stop=(c == 1))
            return mm

        def finish(dve, step, t, b, po):
            step(dve.tensor_tensor(logits[:, :], po[0:P, 0:X_EXP], net.got["bg"][:, :], ALU.add))
            carry_wait(dve, s_idle)
            step(dve.max(top[:, :], logits[:, :]))
            carry_wait(dve, s_idle)
            step(dve.max_index(top_i[:, :], top[:, :], logits[:, :]))
            dve.tensor_copy(node_row(val, t), top[:, 0:2])
            e = node_row(exp_of, t)
            step(dve.tensor_copy(e, top_i[:, 0:2]))
            m = node_row(mask, t)
            step(dve.tensor_scalar(m, net.iota_i[0:P, 0:X_EXP], exp_of[:, ds(t, 1), 0], None, ALU.is_equal))
            return dve.scalar_tensor_tensor(m, net.iota_i[0:P, 0:X_EXP], exp_of[:, ds(t, 1), 1], m,
                                            ALU.is_equal, ALU.add)

        node_stage(net, "route", 2, loader(
            ("wg", [Q, 2, X_EXP], lambda w: [(w[:, :, :], in_chunks(a["L0_gnn_Wg"]))]),
            ("bg", [P, X_EXP], lambda w: [(w[:, :], row_of(a["L0_gnn_bg"]))])), stage, products, finish, steps=5)

        with net.phase("rank") as ph:
            carry, place, junk = ph.sb("carry", [P, X_EXP]), ph.sb("place", [P, X_EXP]), ph.sb("junk", [P, 2, X_EXP])
            counts, col, coli = ph.sb("counts", [P, X_EXP]), ph.sb("col", [X_EXP, 8]), ph.sb("coli", [X_EXP, 1], I32)
            past, tiles_bc, start = ph.sb("past", [X_EXP, MT]), ph.sb("tiles_bc", [X_EXP, P]), ph.sb("start", [P, X_EXP])
            place_of, diff = ph.sb("place_of", [P, T, 2]), ph.sb("diff", [P, T])
            pick = net.acc[:, T * D:T * D + 2 * T * X_EXP].rearrange("p (n e) -> p n e", e=X_EXP)
            s_rank, s_used, s_step = ph.sem("rank"), ph.sem("used"), ph.sem("step")
            s_counts, s_cnt, s_tiles, s_end, s_past = (ph.sem("counts"), ph.sem("cnt"), ph.sem("tiles"),
                                                       ph.sem("end"), ph.sem("past"))
            s_rows, s_diff, s_exp, s_zero = ph.sem("rows"), ph.sem("diff"), ph.sem("exp"), ph.sem("zero")
            small, exp_h, start_h = net.bank[2], net.bank[3], net.bank[4]
            with ph.block() as block:
                @block.tensor
                def _(pe):
                    def body(t, b, first):
                        if not first:
                            pe.wait_ge(s_used, t - 1)
                        m = node_row(mask, t)
                        pe.matmul(net.bank[b][0:P, 0:X_EXP], net.tri[0:P, 0:P], m, start=True, stop=True)
                        pe.matmul(net.bank[b][0:P, X_EXP:2 * X_EXP], net.ones[0:P, 0:P], m,
                                  start=True, stop=True).then_inc(s_rank, 1)
                    for_tiles(pe, T, body)
                    pe.wait_ge(s_counts, 1)
                    pe.matmul(small[0:X_EXP, 0:1], counts[:, :], net.ones[0:P, 0:1], start=True, stop=True).then_inc(s_cnt, 1)
                    pe.wait_ge(s_tiles, 1)
                    pe.matmul(small[0:X_EXP, 1:2], net.tri[0:X_EXP, 0:X_EXP], col[:, 1:2], start=True, stop=True)
                    pe.matmul(start_h[0:P, 0:X_EXP], tiles_bc[:, :], net.tri[0:X_EXP, 0:X_EXP],
                              start=True, stop=True).then_inc(s_end, 1)
                    pe.wait_ge(s_past, 1)
                    pe.matmul(exp_h[0:1, 0:MT], net.ones[0:X_EXP, 0:1], past[:, :], start=True, stop=True).then_inc(s_rows, 1)

                @block.scalar
                def _(act):
                    act.wait_ge(s_diff, 1)
                    act.activation(gate[:, :, 1], diff[:, :], ACT.Exp).then_inc(s_exp, 1)

                @block.vector
                def _(dve):
                    dve.tensor_tensor(diff[:, :], val[:, :, 1], val[:, :, 0], ALU.subtract).then_inc(s_diff, 1)
                    dve.memset(carry[:, :], 0.0).then_inc(s_zero, 1)
                    dve.wait_ge(s_zero, 1)

                    def body(t, b, first):
                        step = Chain(dve, s_step, t)
                        dve.wait_ge(s_rank, t + 1)
                        if not (isinstance(t, int) and t == 0):
                            dve.wait_ge(s_used, t)
                        step(dve.tensor_tensor(place[:, :], net.bank[b][0:P, 0:X_EXP], carry[:, :], ALU.add))
                        for k in (0, 1):
                            dve.scalar_tensor_tensor(junk[:, k, :], net.iota_i[0:P, 0:X_EXP], exp_of[:, ds(t, 1), k],
                                                     place[:, :], ALU.is_equal, ALU.mult,
                                                     accum_out=rank[:, ds(t, 1), k])
                        dve.tensor_tensor(carry[:, :], net.bank[b][0:P, X_EXP:2 * X_EXP], carry[:, :],
                                          ALU.add).then_inc(s_used, 1)
                    for_tiles(dve, T, body)
                    step = Chain(dve, s_step, T)
                    dve.tensor_reduce(counts[:, :], mask[:, :, :].rearrange("p t e -> p e t"), AX_X, ALU.add).then_inc(s_counts, 1)
                    dve.wait_ge(s_cnt, 1)
                    step(dve.tensor_scalar(col[:, 0:1], small[0:X_EXP, 0:1], float(CAP), None, ALU.min))
                    ceil_div(step, dve, col[:, 1:2], col[:, 0:1], Q, coli[:, :], col[:, 2:3])
                    dve.tensor_scalar(tiles_bc[:, :], net.ones[0:X_EXP, 0:P], col[:, 1:2], None, ALU.mult).then_inc(s_tiles, 1)
                    dve.wait_ge(s_end, 1)
                    step(dve.tensor_tensor(col[:, 4:5], small[0:X_EXP, 1:2], col[:, 1:2], ALU.add))
                    dve.tensor_scalar(past[:, :], net.iota_i[0:X_EXP, 0:MT], col[:, 4:5], None, ALU.is_ge).then_inc(s_past, 1)
                    step(dve.tensor_scalar(start[:, :], start_h[0:P, 0:X_EXP], float(Q), None, ALU.mult))
                    dve.wait_ge(s_rows, 1)
                    dve.tensor_scalar(exp_tab[:, :], exp_h[0:1, 0:MT], float(X_EXP - 1), None, ALU.min)
                    chosen = exp_of[:, :, :].rearrange("p t k -> p (t k)")
                    wide = [P, 2 * T, X_EXP]
                    step(dve.tensor_tensor(pick, bc(chosen, 2, wide), bc(net.iota_i[0:P, 0:X_EXP], 1, wide), ALU.is_equal))
                    step(dve.tensor_tensor(pick, pick, bc(start[:, :], 1, wide), ALU.mult))
                    step(dve.tensor_reduce(place_of[:, :, :].rearrange("p t k -> p (t k)"), pick, AX_X, ALU.add))
                    step(dve.tensor_tensor(place_of[:, :, :], place_of[:, :, :], rank[:, :, :], ALU.add))
                    step(dve.tensor_scalar(valid[:, :, :], rank[:, :, :], float(CAP), None, ALU.is_lt))
                    step(dve.tensor_tensor(get[:, :, :], place_of[:, :, :], valid[:, :, :], ALU.mult))
                    step(dve.tensor_scalar(rank[:, :, :], valid[:, :, :], -1e6, 1e6, ALU.mult, ALU.add))
                    step(dve.tensor_tensor(put[:, :, :], place_of[:, :, :], rank[:, :, :], ALU.add))
                    dve.wait_ge(s_exp, 1)
                    step(dve.tensor_scalar(gate[:, :, 0], gate[:, :, 1], 1.0, None, ALU.add))
                    step(dve.reciprocal(gate[:, :, 0], gate[:, :, 0]))
                    step(dve.tensor_tensor(gate[:, :, 1], gate[:, :, 1], gate[:, :, 0], ALU.mult))
                    dve.tensor_tensor(gate[:, :, :], gate[:, :, :], valid[:, :, :], ALU.mult)

        with net.phase("send") as ph:
            row = [ph.sb(f"row{b}", [P, D]) for b in (0, 1)]
            to = [ph.sb(f"to{b}", [P, 2], I32) for b in (0, 1)]
            s_idle = ph.sem("idle")
            s_row, s_to, s_sent = ph.sem("row"), ph.sem("to"), [ph.sem("sent0"), ph.sem("sent1")]
            with ph.block() as block:
                @block.scalar
                def _(act):
                    def body(t, b, first):
                        if not first:
                            act.wait_ge(s_sent[b], (t - b) * 16)
                        act.activation(row[b][:, :], node_row(xm, t), ACT.Copy).then_inc(s_row, 1)
                    for_tiles(act, T, body)

                @block.vector
                def _(dve):
                    def body(t, b, first):
                        if not first:
                            dve.wait_ge(s_sent[b], (t - b) * 16)
                        dve.tensor_copy(to[b][:, :].bitcast(F32), node_row(put, t).bitcast(F32)).then_inc(s_to, 1)
                    for_tiles(dve, T, body)

                @block.gpsimd
                def _(pool):
                    def body(t, b, first):
                        pool.wait_ge(s_row, t + 1)
                        pool.wait_ge(s_to, t + 1)
                        carry_wait(pool, s_idle)
                        for k in (0, 1):
                            pool.indirect_dma_start(
                                out=buf[:, :], out_offset=bass.IndirectOffsetOnAxis(ap=to[b][:, k:k + 1], axis=0),
                                in_=row[b][:, :], in_offset=None, bounds_check=TOK_ROWS - 1, oob_is_err=False,
                            ).then_inc(s_sent[b], 16)
                    for_tiles(pool, T, body)
                    for b in (0, 1):
                        pool.wait_ge(s_sent[b], 16 * T)

        with net.phase("ffn") as ph:
            R = RING = 6
            KD, KH = D // Q, HID // Q
            free = net.acc_full[:, T * D:2 * T * D]
            w1 = [free[:, r * D * HID // Q:(r + 1) * D * HID // Q].rearrange("p (c n) -> p c n", c=KD) for r in range(R)]
            w2 = [free[:, (R + r) * D * HID // Q:(R + r + 1) * D * HID // Q].rearrange("p (c n) -> p c n", c=KH)
                  for r in range(R)]
            b1 = [ph.sb(f"b1_{r}", [Q, KH]) for r in range(R)]
            b2 = [ph.sb(f"b2_{r}", [Q, D]) for r in range(R)]
            rows = [ph.sb(f"rows{r}", [Q, D]) for r in range(R)]
            cols = [ph.sb(f"cols{r}", [Q, KD, Q]) for r in (0, 1)]
            hid = [ph.sb(f"hid{r}", [Q, KH, Q]) for r in (0, 1)]
            res = [ph.sb(f"res{r}", [Q, D]) for r in (0, 1)]
            turned, hidden, product = net.bank[0:2], net.bank[2:4], net.bank[4:6]
            s_w = [ph.sem(f"w{r}") for r in range(R)]
            s_in = [ph.sem(f"in{r}") for r in range(R)]
            s_turned, s_copied, s_hidden, s_gelu = ph.sem("turned"), ph.sem("copied"), ph.sem("hidden"), ph.sem("gelu")
            s_product, s_res, s_stored = ph.sem("product"), ph.sem("res"), [ph.sem("st0"), ph.sem("st1")]
            with ph.block() as block:
                @block.sync
                def _(sp):
                    def body(t, b, first):
                        e = sp.value_load(exp_tab[0:1, ds(t, 1)], min_val=0, max_val=X_EXP - 1)
                        r = b % R
                        if not (first and b < R):
                            sp.wait_ge(s_product, t - R + 1)
                        sp.dma_start(w1[r][:, :, :].rearrange("p c n -> p (c n)"),
                                     a["L0_gnn_w1"][ds(e, 1)].rearrange("e (p c) n -> p (e c n)", c=KD)).then_inc(s_w[r], 16)
                        sp.dma_start(w2[r][:, :, :].rearrange("p c n -> p (c n)"),
                                     a["L0_gnn_w2"][ds(e, 1)].rearrange("e (p c) n -> p (e c n)", c=KH)).then_inc(s_w[r], 32)
                    for_tiles(sp, MT, body, ring=RING)

                @block.gpsimd
                def _(pool):
                    def body(t, b, first):
                        e = pool.value_load(exp_tab[0:1, ds(t, 1)], min_val=0, max_val=X_EXP - 1)
                        r = b % R
                        if not (first and b < R):
                            pool.wait_ge(s_res, t - R + 1)
                        pool.dma_start(rows[r][:, :], buf[ds(Q * t, Q), :]).then_inc(s_in[r], 16)
                        pool.dma_start(b1[r][:, :], a["L0_gnn_b1"][ds(e, 1)].rearrange("e (p c) -> p (e c)", c=KH)).then_inc(s_in[r], 16)
                        pool.dma_start(b2[r][:, :], a["L0_gnn_b2"][ds(e, 1)].broadcast_to([Q, D])).then_inc(s_in[r], 16)
                    for_tiles(pool, MT, body, ring=RING)

                def loaded(eng, sem, each, t, b):
                    eng.wait_ge(sem[b], each // R * (t - b) + each)

                @block.tensor
                def _(pe):
                    def turn(t, b, first):
                        loaded(pe, s_in, 48, t, b)
                        if not (first and b < 2):
                            pe.wait_ge(s_copied, t - 1)
                        for c in range(KD):
                            mm = pe.transpose(turned[b % 2][:, c * Q:(c + 1) * Q], rows[b % R][:, c:D:KD], net.ident[:, :])
                        mm.then_inc(s_turned, 1)

                    def up(t, b, first):
                        loaded(pe, s_w, 48, t, b)
                        pe.wait_ge(s_copied, t + 1)
                        if not (first and b < 2):
                            pe.wait_ge(s_gelu, t - 1)
                        for j in range(KH):
                            for c in range(KD):
                                mm = pe.matmul(hidden[b % 2][:, j * Q:(j + 1) * Q], w1[b % R][:, c, j:HID:KH],
                                               cols[b % 2][:, c, :], start=(c == 0), stop=(c == KD - 1))
                        mm.then_inc(s_hidden, 1)

                    def down(t, b, first):
                        pe.wait_ge(s_gelu, t + 1)
                        if not (first and b < 2):
                            pe.wait_ge(s_res, t - 1)
                        for j in range(KH):
                            mm = pe.matmul(product[b % 2][:, 0:D], hid[b % 2][:, j, :], w2[b % R][:, j, :],
                                           start=(j == 0), stop=(j == KH - 1))
                        mm.then_inc(s_product, 1)
                    for_tiles(pe, MT, down, ahead=((2, turn), (1, up)), ring=RING)

                @block.scalar
                def _(act):
                    def body(t, b, first):
                        act.wait_ge(s_hidden, t + 1)
                        loaded(act, s_in, 48, t, b)
                        if not (first and b < 2):
                            act.wait_ge(s_product, t - 1)
                        for j in range(KH):
                            ins = act.activation(hid[b % 2][:, j, :], hidden[b % 2][:, j * Q:(j + 1) * Q], ACT.Gelu,
                                                 bias=b1[b % R][:, j:j + 1])
                        ins.then_inc(s_gelu, 1)

                    def store(t, b, first):
                        act.wait_ge(s_res, t + 1)
                        act.dma_start(outb[ds(Q * t, Q), :], res[b % 2][:, :]).then_inc(s_stored[b % 2], 16)
                    for_tiles(act, MT, store, ahead=((1, body),), ring=RING)
                    for b in (0, 1):
                        act.wait_ge(s_stored[b], 16 * (MT // 2))

                @block.vector
                def _(dve):
                    def copy(t, b, first):
                        dve.wait_ge(s_turned, t + 1)
                        if not (first and b < 2):
                            dve.wait_ge(s_hidden, t - 1)
                        dve.tensor_copy(cols[b % 2][:, :, :].rearrange("p c n -> p (c n)"),
                                        turned[b % 2][:, 0:D]).then_inc(s_copied, 1)

                    def body(t, b, first):
                        dve.wait_ge(s_product, t + 1)
                        loaded(dve, s_in, 48, t, b)
                        if not (first and b < 2):
                            dve.wait_ge(s_stored[b % 2], 8 * (t - b % 2))
                        dve.tensor_tensor(res[b % 2][:, :], product[b % 2][:, 0:D], b2[b % R][:, :], ALU.add).then_inc(s_res, 1)
                    for_tiles(dve, MT, body, ahead=((2, copy),), ring=RING)

        with net.phase("take") as ph:
            R = 2
            got = [[ph.sb(f"got{b}{k}", [P, D]) for k in (0, 1)] for b in (0, 1)]
            of = [ph.sb(f"of{b}", [P, 2], I32) for b in (0, 1)]
            s_idle = ph.sem("idle")
            s_of, s_got, s_y, s_step = ph.sem("of"), [ph.sem("got0"), ph.sem("got1")], ph.sem("y"), ph.sem("step")
            with ph.block() as block:
                @block.gpsimd
                def _(pool):
                    def body(t, b, first):
                        pool.wait_ge(s_of, t + 1)
                        carry_wait(pool, s_idle)
                        for k in (0, 1):
                            pool.indirect_dma_start(
                                out=got[b][k][:, :], out_offset=None, in_=outb[:, :],
                                in_offset=bass.IndirectOffsetOnAxis(ap=of[b][:, k:k + 1], axis=0),
                            ).then_inc(s_got[b], 16)
                    for_tiles(pool, T, body)

                @block.vector
                def _(dve):
                    def ahead(t, b, first):
                        if not first:
                            dve.wait_ge(s_y, t - 1)
                        dve.tensor_copy(of[b][:, :].bitcast(F32), node_row(get, t).bitcast(F32)).then_inc(s_of, 1)

                    def body(t, b, first):
                        dve.wait_ge(s_got[b], (t - b) * 16 + 32)
                        step = Chain(dve, s_step, t)
                        y = node_row(xm, t)
                        step(dve.scalar_tensor_tensor(y, got[b][0][:, :], gate[:, ds(t, 1), 0], y, ALU.mult, ALU.add))
                        dve.scalar_tensor_tensor(y, got[b][1][:, :], gate[:, ds(t, 1), 1], y,
                                                 ALU.mult, ALU.add).then_inc(s_y, 1)
                    for_tiles(dve, T, body, ahead=((1, ahead),))


def batch_norm(net):
    a = net.a
    y = net.acc_view(D)
    sq = net.acc[:, T * D:2 * T * D].rearrange("p (t d) -> p t d", d=D)
    by_column = "p t d -> p d t"
    with net.phase("bn") as ph:
        part, mean, scale = ph.sb("part", [P, D]), ph.sb("mean", [P, D]), ph.sb("scale", [P, D])
        gamma, beta = ph.sb("gamma", [P, D]), ph.sb("beta", [P, D])
        s_w, s_part, s_all, s_step, s_yc, s_sq = (ph.sem("w"), ph.sem("part"), ph.sem("all"), ph.sem("step"),
                                                  ph.sem("yc"), ph.sem("sq"))
        s_var, s_root = ph.sem("var"), ph.sem("root")
        wide = [P, T, D]
        with ph.block() as block:
            @block.sync
            def _(sp):
                sp.dma_start(gamma[:, :], row_of(a["L0_gnn_gamma"])).then_inc(s_w, 16)
                sp.dma_start(beta[:, :], row_of(a["L0_gnn_beta"])).then_inc(s_w, 16)

            @block.tensor
            def _(pe):
                for k in (0, 1):
                    pe.wait_ge(s_part, k + 1)
                    pe.matmul(net.bank[k][0:P, 0:D], net.ones[0:P, 0:P], part[:, :], start=True, stop=True).then_inc(s_all, 1)

            @block.scalar
            def _(act):
                act.wait_ge(s_yc, 1)
                act.activation(sq, y, ACT.Square).then_inc(s_sq, 1)
                act.wait_ge(s_var, 1)
                act.activation(scale[:, :], scale[:, :], ACT.Sqrt).then_inc(s_root, 1)

            @block.vector
            def _(dve):
                step = Chain(dve, s_step)
                dve.tensor_reduce(part[:, :], y.rearrange(by_column), AX_X, ALU.add).then_inc(s_part, 1)
                dve.wait_ge(s_all, 1)
                step(dve.tensor_scalar(mean[:, :], net.bank[0][0:P, 0:D], 1.0 / N, None, ALU.mult))
                dve.tensor_tensor(y, y, bc(mean[:, :], 1, wide), ALU.subtract).then_inc(s_yc, 1)
                dve.wait_ge(s_sq, 1)
                dve.tensor_reduce(part[:, :], sq.rearrange(by_column), AX_X, ALU.add).then_inc(s_part, 1)
                dve.wait_ge(s_all, 2)
                dve.tensor_scalar(scale[:, :], net.bank[1][0:P, 0:D], 1.0 / N, BN_EPS, ALU.mult, ALU.add).then_inc(s_var, 1)
                dve.wait_ge(s_root, 1)
                step(dve.reciprocal(scale[:, :], scale[:, :]))
                dve.wait_ge(s_w, 32)
                step(dve.tensor_tensor(scale[:, :], scale[:, :], gamma[:, :], ALU.mult))
                step(dve.tensor_tensor(y, y, bc(scale[:, :], 1, wide), ALU.mult))
                step(dve.tensor_tensor(y, y, bc(beta[:, :], 1, wide), ALU.add))
                step(dve.tensor_tensor(net.x[:, :, :], net.x[:, :, :], y, ALU.add))



BL = 8

def tensor_product_edges(net, table):
    nc, a = net.nc, net.a
    acc = net.acc_view(2 * D)
    R = 8
    HALVES = 2 * WINDOWS
    with net.phase("tp") as ph:
        attr = [ph.sb(f"attr{w}", [Q, 2, 4]) for w in range(R // 2)]
        scal = [ph.sb(f"scal{w}", [8, WIN]) for w in range(R // 2)]
        fc1, fc2 = ph.sb("fc1", [8, MUL]), ph.sb("fc2", [MUL, 4, MUL])
        hid = [ph.sb(f"hid{w}", [MUL, WIN]) for w in (0, 1)]
        src = [ph.sb(f"src{r}", [Q, D]) for r in range(R)]
        idx = [ph.sb(f"idx{w}", [Q, 2], I32) for w in range(R // 2)]
        hot = [ph.sb(f"hot{r}", [Q, P]) for r in range(R)]
        hots = [ph.sb(f"hots{r}", [Q, 4, P]) for r in (0, 1)]
        msg = [ph.sb(f"msg{r}", [Q, BL, MUL]) for r in (0, 1)]
        s_fc, s_fcs, s_attr = ph.sem("fc"), ph.sem("fcs"), [ph.sem(f"attr{w}") for w in range(R // 2)]
        s_idx, s_src, s_idle = ph.sem("idx"), [ph.sem(f"src{r}") for r in range(R)], ph.sem("idle")
        s_z, s_hid, s_w = ph.sem("z"), ph.sem("hid"), ph.sem("w")
        s_hot, s_hots, s_msg, s_half, s_add = ph.sem("hot"), ph.sem("hots"), ph.sem("msg"), ph.sem("half"), ph.sem("add")
        s_zero = ph.sem("zero")
        zb, wb, ab = net.bank[0:2], net.bank[2:4], net.bank[4:6]
        fc2_of = (0, 2, 3, 1)

        def window(h, b):
            return (h - b % 2) // 2

        def fresh(first, b, n):
            return first and b < n

        with ph.block() as block:
            @block.sync
            def _(sp):
                sp.dma_start(fc1[:, :], a["L3_gnn_fc_w1"][:, :]).then_inc(s_fc, 16)
                for k, of in enumerate(fc2_of):
                    sp.dma_start(fc2[:, k, :], a["L3_gnn_fc_w2"][:, of * MUL:(of + 1) * MUL]).then_inc(s_fc, 16)

                def body(h, b, first):
                    if b % 2:
                        return
                    w = b // 2
                    e0 = sp.value_load(net.win_tab[0:1, ds(WINDOWS + window(h, b), 1)], min_val=0, max_val=E)
                    if not fresh(first, b, R):
                        sp.wait_ge(s_half, h - R + 2)
                    sp.dma_start(attr[w][:, :, :].rearrange("p j k -> p (j k)"),
                                 a["edge_attr"][ds(e0, WIN), :].rearrange("(p j) k -> p (j k)", j=2)).then_inc(s_attr[w], 16)
                    sp.dma_start(scal[w][:, :], a["edge_scal_t"][:, ds(e0, WIN)]).then_inc(s_attr[w], 16)
                for_tiles(sp, HALVES, body, ring=R)

            @block.gpsimd
            def _(pool):
                def body(h, b, first):
                    if b % 2 == 0:
                        pool.wait_ge(s_idx, h + 2)
                        carry_wait(pool, s_idle)
                    pool.indirect_dma_start(
                        out=src[b][:, :], out_offset=None, in_=table[:, :],
                        in_offset=bass.IndirectOffsetOnAxis(ap=idx[b // 2][:, b % 2:b % 2 + 1], axis=0)).then_inc(s_src[b], 16)
                for_tiles(pool, HALVES, body, ring=R)

            @block.scalar
            def _(act):
                def hidden(h, b, first):
                    if b % 2:
                        return
                    w = (b // 2) % 2
                    act.wait_ge(s_z, h + 2)
                    if not fresh(first, b, 4):
                        act.wait_ge(s_w, h - 2)
                    act.activation(hid[w][:, :], zb[w][0:MUL, 0:WIN], ACT.Silu, scale=8 ** -0.5).then_inc(s_hid, 2)

                def body(h, b, first):
                    act.wait_ge(s_hot, h + 1)
                    act.wait_ge(s_attr[b // 2], 4 * (h - b) + 32)
                    if not fresh(first, b, 2):
                        act.wait_ge(s_half, h - 1)
                    for c in range(4):
                        ins = act.activation(hots[b % 2][:, c, :], hot[b][:, :], ACT.Copy,
                                             scale=attr[b // 2][:, b % 2, c:c + 1])
                    ins.then_inc(s_hots, 1)
                for_tiles(act, HALVES, body, ahead=((2, hidden),), ring=R)

            @block.tensor
            def _(pe):
                def first_product(h, b, first):
                    if b % 2:
                        return
                    w = b // 2
                    pe.wait_ge(s_attr[w], 4 * (h - b) + 32)
                    if not fresh(first, b, 4):
                        pe.wait_ge(s_hid, h - 2)
                    pe.matmul(zb[w % 2][0:MUL, 0:WIN], fc1[:, :], scal[w][:, :], start=True, stop=True).then_inc(s_z, 2)

                def second_product(h, b, first):
                    j = b % 2
                    pe.wait_ge(s_hid, h - j + 2)
                    if not fresh(first, b, 2):
                        pe.wait_ge(s_msg, h - 1)
                    pe.matmul(wb[j][:, 0:4 * MUL], hid[(b // 2) % 2][:, j:WIN:2], fc2[:, :, :].rearrange("p b n -> p (b n)"),
                              start=True, stop=True).then_inc(s_w, 1)

                def body(h, b, first):
                    j, w = b % 2, (b // 2) % 2
                    if j == 0 and not fresh(first, b, 4):
                        pe.wait_ge(s_add, h - 2)
                    pe.wait_ge(s_msg, h + 1)
                    pe.wait_ge(s_hots, h + 1)
                    m = msg[j]
                    out = ab[w][0:P, :].rearrange("p (b n) -> p b n", n=MUL)
                    pe.matmul(out[:, 0:4, :], hots[j][:, 0, :], m[:, 0:4, :], start=(j == 0), stop=False,
                              skip_group_check=True)
                    for c in range(3):
                        mm = pe.matmul(out[:, 4 + c:8:3 - c, :], hots[j][:, 1 + c, :], m[:, 4:6 + c:1 + c, :],
                                       start=False, stop=(j == 1 and c == 2), skip_group_check=True)
                    mm.then_inc(s_half, 1)
                pe.wait_ge(s_fc, 16 * 5)
                pe.wait_ge(s_fcs, 2)
                for_tiles(pe, HALVES, body, ahead=((4, first_product), (1, second_product)), ring=R)

            @block.vector
            def _(dve):
                dve.memset(net.acc[:, :], 0.0).then_inc(s_zero, 1)
                dve.wait_ge(s_fc, 16 * 5)
                dve.tensor_scalar(fc2[:, 0:3, :], fc2[:, 0:3, :], 1.679 * MUL ** -0.5, None, ALU.mult).then_inc(s_fcs, 1)
                dve.tensor_scalar(fc2[:, 3, :], fc2[:, 3, :], 1.679 * MUL ** -0.5 * 3 ** -0.5, None, ALU.mult).then_inc(s_fcs, 1)

                def stage(h, b, first):
                    if b % 2 == 0:
                        if not fresh(first, b, R):
                            dve.wait_ge(s_half, h - R + 2)
                        dve.tensor_copy(idx[b // 2][:, :].bitcast(F32),
                                        net.src_w[:, ds(h, 2)].bitcast(F32)).then_inc(s_idx, 2)
                    dve.tensor_scalar(hot[b][:, :], net.iota_i[:, 0:P], net.dst_w[:, ds(h, 1)], None,
                                      ALU.is_equal).then_inc(s_hot, 1)

                def add(h, w_index, w, very_first):
                    tile = dve.value_load(net.win_tab[0:1, ds(w_index, 1)], min_val=0, max_val=T - 1)
                    dve.wait_ge(s_half, h + 2)
                    if not very_first:
                        dve.wait_ge(s_add, h)
                    row = node_row(acc, tile)
                    dve.tensor_tensor(row, row, ab[w][0:P, :], ALU.add).then_inc(s_add, 2)

                def body(h, b, first):
                    j = b % 2
                    dve.wait_ge(s_src[b], 2 * (h - b) + 16)
                    dve.wait_ge(s_w, h + 1)
                    if not fresh(first, b, 2):
                        dve.wait_ge(s_half, h - 1)
                    m = msg[j][:, :, :]
                    wv = wb[j][:, 0:4 * MUL].rearrange("p (b n) -> p b n", n=MUL)
                    sv = src[b][:, :].rearrange("p (b n) -> p b n", n=MUL)
                    dve.tensor_tensor(m[:, 0:8:4, :], wv[:, 0:2, :], sv[:, 0:1, :].broadcast_to([Q, 2, MUL]), ALU.mult)
                    quad = m.rearrange("p (g k) n -> p g k n", g=2)[:, :, 1:4, :]
                    dve.tensor_tensor(quad, bc(wv[:, 2:4, :], 2, [Q, 2, 3, MUL]),
                                      bc(sv[:, 1:4, :], 1, [Q, 2, 3, MUL]), ALU.mult).then_inc(s_msg, 1)
                    if j == 0 and not fresh(first, b, 2):
                        add(h - 2, window(h, b) - 1, (b // 2 + 1) % 2, fresh(first, b, 4))
                dve.wait_ge(s_zero, 1)
                for_tiles(dve, HALVES, body, ahead=((4, stage),), ring=R)
                add(2 * WINDOWS - 2, WINDOWS - 1, (WINDOWS - 1) % 2, False)


def dram(nc, name, shape, dt=F32):
    return nc.dram_tensor(name, shape, dt, kind="Internal").ap()


def gnn_kernel(nc, a, out):
    with ExitStack() as ctx:
        net = Net(nc, ctx, a)
        table0, table1 = dram(nc, "table0", [N, D]), dram(nc, "table1", [N, D])
        table2, table3 = dram(nc, "table2", [N, D // 2]), dram(nc, "table3", [N, D])
        buf, outb = dram(nc, "token_rows", [TOK_ROWS, D]), dram(nc, "expert_rows", [TOK_ROWS, D])
        prepare(net)
        acc256, acc128, acc512 = net.acc_view(D), net.acc_view(D // 2), net.acc_view(2 * D)

        def relu_norm(act, t, rows):
            return act.activation(rows, node_row(net.x, t), ACT.Relu, bias=net.nmr[:, ds(t, 1)],
                                  scale=net.rstd[:, ds(t, 1)])

        def four_products(pe, cols, po):
            for c in range(4):
                mm = pe.matmul(po[0:P, 0:D], cols[:, c, :], net.got["w"][:, c, :], start=(c == 0), stop=(c == 3))
            return mm

        def factors0(step, dve, act, s1, s2):
            if act:
                act.activation(net.ra[:, :], net.deg_out[:, :], ACT.Sqrt).then_inc(s1, 1)
                act.wait_ge(s2, 1)
                act.activation(net.rb[:, :], net.rb[:, :], ACT.Sqrt).then_inc(s1, 1)
            else:
                dve.tensor_scalar(net.rb[:, :], net.deg_in[:, :], 1.0, None, ALU.max).then_inc(s2, 1)
                dve.wait_ge(s1, 2)
                step(dve.reciprocal(net.ra[:, :], net.ra[:, :]))
                step(dve.reciprocal(net.rb[:, :], net.rb[:, :]))
                step(dve.tensor_tensor(net.rc[:, :], net.ra[:, :], net.nmr[:, :], ALU.mult))
                step(dve.tensor_tensor(net.ra[:, :], net.ra[:, :], net.rstd[:, :], ALU.mult))
        layer_stats(net, "ln0", factors0)
        write_table(net, "tab0", table0, net.ra, net.rc)

        aggregate(net, "agg0", table0, D, clear=buf)

        def stage0(act, t, rows):
            act.activation(rows[:, 0:D], node_row(acc256, t), ACT.Copy, scale=net.rb[:, ds(t, 1)])
            return relu_norm(act, t, rows[:, D:2 * D])

        def finish0(dve, step, t, b, po):
            row = node_row(acc256, t)
            step(dve.tensor_tensor(row, po[0:P, 0:D], net.got["b1"][:, :], ALU.add))
            return dve.tensor_tensor(row, row, net.got["b2"][:, :], ALU.add)
        node_stage(net, "node0", 4, loader(
            ("w", [Q, 4, D], lambda w: [(w[:, 0:2, :], in_chunks(a["L0_gnn_W_gc"])), (w[:, 2:4, :], in_chunks(a["L0_gnn_W_res"]))]),
            ("b1", [P, D], lambda w: [(w[:, :], row_of(a["L0_gnn_b_gc"]))]),
            ("b2", [P, D], lambda w: [(w[:, :], row_of(a["L0_gnn_b_res"]))])), stage0, four_products, finish0, steps=1)
        experts(net, buf, outb, None)
        batch_norm(net)

        def factors1(step, dve, act, s1, s2):
            if dve:
                step(dve.tensor_scalar(net.rb[:, :], net.deg_in[:, :], 1.0, None, ALU.max))
                step(dve.reciprocal(net.rb[:, :], net.rb[:, :]))
        layer_stats(net, "ln1", factors1)
        write_table(net, "tab1", table1, net.rstd, net.nmr)
        aggregate(net, "agg1", table1, D)

        def finish1(dve, step, t, b, po):
            row = node_row(net.x, t)
            step(dve.tensor_tensor(row, po[0:P, 0:D], row, ALU.add))
            return dve.tensor_tensor(row, row, net.got["b"][:, :], ALU.add)
        node_stage(net, "node1", 4, loader(
            ("w", [Q, 4, D], lambda w: [(w[:, 0:2, :], in_chunks(a["L1_w_neigh_t"])), (w[:, 2:4, :], in_chunks(a["L1_w_self_t"]))]),
            ("b", [P, D], lambda w: [(w[:, :], row_of(a["L1_gnn_b_self"]))])), stage0, four_products, finish1, steps=1)

        half = D // 2
        own = net.acc[:, T * half:2 * T * half].rearrange("p (t d) -> p t d", d=half)

        def factors2(step, dve, act, s1, s2):
            if act:
                act.wait_ge(s2, 1)
                act.activation(net.ra[:, :], net.ra[:, :], ACT.Sqrt).then_inc(s1, 1)
            else:
                dve.tensor_scalar(net.ra[:, :], net.deg_in[:, :], 1.0, None, ALU.add).then_inc(s2, 1)
                dve.wait_ge(s1, 1)
                step(dve.reciprocal(net.ra[:, :], net.ra[:, :]))
        layer_stats(net, "ln2", factors2)
        with ExitStack() as c2:
            row2 = [c2.enter_context(nc.sbuf_tensor(f"row2_{b}", [P, half], F32)) for b in (0, 1)]

            def stage2(act, t, rows):
                return relu_norm(act, t, rows[:, :])

            def products2(pe, cols, po):
                for c in (0, 1):
                    mm = pe.matmul(po[0:P, 0:half], cols[:, c, :], net.got["w"][:, c, :], start=(c == 0), stop=(c == 1))
                return mm

            def finish2(dve, step, t, b, po):
                dve.tensor_scalar(node_row(own, t), po[0:P, 0:half], net.ra[:, ds(t, 1)], None, ALU.mult)
                return dve.tensor_scalar(row2[b][:, :], po[0:P, 0:half], net.ra[:, ds(t, 1)], None, ALU.mult)

            def store2(sp, t, b):
                return sp.dma_start(table2[ds(P * t, P), :], row2[b][:, :])
            node_stage(net, "node2", 2, loader(
                ("w", [Q, 2, half], lambda w: [(w[:, :, :], in_chunks(a["L2_gnn_W_conv"]))])),
                stage2, products2, finish2, steps=0, store=store2)
        aggregate(net, "agg2", table2, half)
        with ExitStack() as c2:
            b_conv = c2.enter_context(nc.sbuf_tensor("b_conv", [P, half], F32))
            scale_and_bias(net, acc128, own, b_conv)

        def stage2b(act, t, rows):
            return act.activation(rows[:, :], node_row(acc128, t), ACT.Copy)

        def products2b(pe, cols, po):
            return pe.matmul(po[0:P, 0:D], cols[:, 0, :], net.got["w"][:, 0, :], start=True, stop=True)
        node_stage(net, "node2b", 1, loader(
            ("w", [Q, 1, D], lambda w: [(w[:, 0, :], a["L2_gnn_W_lin"][:, :])]),
            ("b", [P, D], lambda w: [(w[:, :], row_of(a["L2_gnn_b_lin"]))])), stage2b, products2b, finish1, steps=1)

        inv_mul = MUL ** -0.5
        c_s, c_x = float(np.sin(np.pi / 8)), float(np.cos(np.pi / 8))

        def factors3(step, dve, act, s1, s2):
            if dve:
                step(dve.tensor_scalar(net.ra[:, :], net.rc[:, :], inv_mul, None, ALU.mult))
                step(dve.tensor_scalar(net.rb[:, :], net.rc[:, :], c_s * inv_mul, None, ALU.mult))
                step(dve.tensor_scalar(net.rc[:, :], net.rc[:, :], c_x * (2 * MUL) ** -0.5 * 20.0 ** -0.5, None, ALU.mult))
        load_node_attr(net)
        layer_stats(net, "ln3", factors3)
        parts = "p (u c) -> p c u"
        with ExitStack() as c3:
            row3 = [c3.enter_context(nc.sbuf_tensor(f"row3_{b}", [P, D], F32)) for b in (0, 1)]

            def stage3(act, t, rows):
                relu_norm3 = dict(bias=net.nmr[:, ds(t, 1)], scale=net.rstd[:, ds(t, 1)])
                xr = node_row(net.x, t)
                act.activation(rows[:, 0:MUL], xr[:, 0:MUL], ACT.Relu, **relu_norm3)
                return act.activation(rows[:, MUL:D].rearrange("p (c u) -> p c u", c=3),
                                      xr[:, MUL:D].rearrange(parts, c=3), ACT.Relu, **relu_norm3)

            def products3(pe, cols, po):
                w = net.got["w"]
                for c in (0, 1):
                    pe.matmul(po[0:P, c * Q:(c + 1) * Q], cols[:, c, :], w[:, c, :], start=(c == 0), stop=True,
                              skip_group_check=True)
                    mm = pe.matmul(po[0:P, D + c * Q:D + (c + 1) * Q], cols[:, c, :], w[:, 2 + c, :], start=False,
                                   stop=True, skip_group_check=True)
                return mm

            def finish3(dve, step, t, b, po):
                dve.tensor_scalar(row3[b][:, :], po[0:P, 0:D], net.ra[:, ds(t, 1)], None, ALU.mult)
                xr = node_row(net.x, t)
                dve.scalar_tensor_tensor(xr[:, 0:MUL], po[0:P, D:D + MUL], net.rb[:, ds(t, 1)], xr[:, 0:MUL],
                                         ALU.mult, ALU.add)
                x1 = xr[:, MUL:D].rearrange(parts, c=3)
                return dve.scalar_tensor_tensor(x1, po[0:P, D + MUL:2 * D].rearrange("p (c u) -> p c u", c=3),
                                                net.rb[:, ds(t, 1)], x1, ALU.mult, ALU.add)

            def store3(sp, t, b):
                return sp.dma_start(table3[ds(P * t, P), :], row3[b][:, :])

            node_stage(net, "node3", 2, loader(("w", [Q, 4, Q], lambda w: [
                (w[:, k, :], a["L3_w_pairs"][k]) for k in range(4)])), stage3, products3, finish3, steps=0, store=store3)
        tensor_product_edges(net, table3)

        with ExitStack() as c4:
            row4 = [c4.enter_context(nc.sbuf_tensor(f"row4_{b}", [P, D], F32)) for b in (0, 1)]

            def stage4(act, t, rows):
                of = node_row(acc512, t).rearrange("p (b u) -> p b u", u=MUL)
                to = rows[:, :].rearrange("p (b u) -> p b u", u=MUL)
                act.activation(to[:, 0, :], of[:, 0, :], ACT.Copy)
                act.activation(to[:, 1, :], of[:, 7, :], ACT.Copy)
                act.activation(to[:, 2:8:2, :], of[:, 4:7, :], ACT.Copy)
                return act.activation(to[:, 3:8:2, :], of[:, 1:4, :], ACT.Copy)

            def products4(pe, cols, po):
                w = net.got["w"]
                for c in range(4):
                    mm = pe.matmul(po[0:P, c * MUL:(c + 1) * MUL], cols[:, c, :], w[:, min(c, 1), :], start=(c == 0),
                                   stop=True, skip_group_check=True)
                return mm

            def finish4(dve, step, t, b, po):
                xr = node_row(net.x, t)
                sc = net.rc[:, ds(t, 1)]
                dve.scalar_tensor_tensor(row4[b][:, 0:MUL], po[0:P, 0:MUL], sc, xr[:, 0:MUL], ALU.mult, ALU.add)
                return dve.scalar_tensor_tensor(row4[b][:, MUL:D].rearrange(parts, c=3),
                                                po[0:P, MUL:D].rearrange("p (c u) -> p c u", c=3), sc,
                                                xr[:, MUL:D].rearrange(parts, c=3), ALU.mult, ALU.add)

            def store4(sp, t, b):
                return sp.dma_start(out[ds(P * t, P), :], row4[b][:, :])
            node_stage(net, "node4", 4, loader(("w", [Q, 2, MUL], lambda w: [
                (w[MUL * h:MUL * (h + 1), k, :], a["L3_gnn_lin2_w" + n][:, :])
                for k, h, n in ((0, 0, "00"), (0, 1, "01"), (1, 0, "10"), (1, 1, "11"))])),
                stage4, products4, finish4, steps=0, store=store4)


def scale_and_bias(net, acc, own, b_conv):
    half = D // 2
    with net.phase("gcn") as ph:
        s_w, s_step = ph.sem("w"), ph.sem("step")
        with ph.block() as block:
            @block.sync
            def _(sp):
                sp.dma_start(b_conv[:, :], row_of(net.a["L2_gnn_b_conv"])).then_inc(s_w, 16)

            @block.vector
            def _(dve):
                step = Chain(dve, s_step)
                wide = [P, T, half]
                step(dve.tensor_tensor(acc, acc, own, ALU.add))
                step(dve.tensor_tensor(acc, acc, bc(net.ra[:, :], 2, wide), ALU.mult))
                dve.wait_ge(s_w, 16)
                step(dve.tensor_tensor(acc, acc, bc(b_conv[:, :], 1, wide), ALU.add))


def load_node_attr(net):
    with net.phase("attr") as ph:
        s_w, s_t = ph.sem("w"), ph.sem("t")
        rows = ph.sb("rows", [T, P])
        with ph.block() as block:
            @block.sync
            def _(sp):
                sp.dma_start(rows[:, :], net.a["node_vec1"].rearrange("(t p) k -> t (p k)", p=P)).then_inc(s_w, 16)

            @block.tensor
            def _(pe):
                pe.wait_ge(s_w, 16)
                pe.transpose(net.bank[0][0:P, 0:T], rows[:, :], net.ident[0:T, 0:T]).then_inc(s_t, 1)

            @block.vector
            def _(dve):
                dve.wait_ge(s_t, 1)
                dve.tensor_copy(net.rc[:, :], net.bank[0][0:P, 0:T])


_OUT_SHAPE = (N, D)


def kernel(**inputs):
    import concourse.bacc as _bacc
    from concourse.bass_utils import run_bass_kernel_spmd as _run

    src, dst = np.asarray(inputs["src"]), np.asarray(inputs["dst"])
    arrays = {}
    edge_index = np.full((E + WIN, 2), -1, np.int32)
    edge_index[:E, 0], edge_index[:E, 1] = src, dst
    edge_index[E:, 0] = 0
    arrays["edge_index"] = edge_index
    arrays["edge_attr"] = np.zeros((E + WIN, 4), np.float32)
    arrays["edge_attr"][:E] = inputs["edge_attr_4"]
    arrays["edge_scal_t"] = np.zeros((8, E + WIN), np.float32)
    arrays["edge_scal_t"][:, :E] = np.asarray(inputs["edge_attr_8"]).T
    arrays["L1_w_neigh_t"] = np.ascontiguousarray(np.asarray(inputs["L1_gnn_w_neigh"]).T)
    arrays["L1_w_self_t"] = np.ascontiguousarray(np.asarray(inputs["L1_gnn_w_self"]).T)
    arrays["L3_w_pairs"] = np.zeros((4, 2 * MUL, 2 * MUL), np.float32)
    for k, (top, low) in enumerate((("lin1_w0", "lin1_w1"), ("lin1_w1", "lin1_w1"), ("sc_w0", "sc_w1"), ("sc_w1", "sc_w1"))):
        arrays["L3_w_pairs"][k, :MUL, :MUL] = inputs["L3_gnn_" + top]
        arrays["L3_w_pairs"][k, MUL:, MUL:] = inputs["L3_gnn_" + low]
    laid_out = ("edge_attr_4", "edge_attr_8", "L1_gnn_w_neigh", "L1_gnn_w_self", "L3_gnn_sc_w0", "L3_gnn_sc_w1",
                "L3_gnn_lin1_w0", "L3_gnn_lin1_w1")
    for name in inputs:
        if name not in laid_out:
            arrays[name] = np.ascontiguousarray(inputs[name])
    nc = _bacc.Bacc("TRN2", target_bir_lowering=False, num_devices=1)
    a = {name: nc.dram_tensor(f"in_{name}_dram", v.shape, mybir.dt.from_np(v.dtype), kind="ExternalInput").ap()
         for name, v in arrays.items()}
    out = nc.dram_tensor("out_0_dram", _OUT_SHAPE, F32, kind="ExternalOutput").ap()
    gnn_kernel(nc, a, out)
    r = _run(nc, [{f"in_{k}_dram": v for k, v in arrays.items()}], core_ids=[0])
    return r.results[0]["out_0_dram"]
```

```python
from contextlib import ExitStack

import numpy as np

import concourse.bass as bass
from concourse import mybir

F32 = mybir.dt.float32
I32 = mybir.dt.int32
U32 = mybir.dt.uint32
BF16 = mybir.dt.bfloat16
ALU = mybir.AluOpType
ACT = mybir.ActivationFunctionType
AX_X = mybir.AxisListType.X
ds = bass.ds

N = 6250
E = 100000
D = 256
P = 125
T = N // P
Q = 128
WIN = 128
WPI = 16
WINDOWS = -(-((E + T * (WIN - 1)) // WIN) // WPI) * WPI
STEPS = WINDOWS // WPI
SPLIT = -(-8 * (E + WIN) // (Q * STEPS))
EPAD = SPLIT * STEPS * Q // 8
GROUPS_W = 8
WG = WINDOWS // GROUPS_W
EC = E // P
X_EXP = 64
HID = 512
CAP = 1024
MT = -(-((2 * N + X_EXP * (Q - 1)) // Q) // 6) * 6
TOK_ROWS = MT * Q
MUL = 64
LN_EPS = 1e-5
BN_EPS = 1e-5
assert N == P * T and E == P * EC and T % 2 == 0 and WINDOWS == WG * GROUPS_W and WG <= Q
assert EPAD >= E + WIN and 8 * EPAD == SPLIT * STEPS * Q


class Chain:

    def __init__(self, eng, sem, base=0):
        self.eng, self.sem, self.base, self.n = eng, sem, base, 0

    def __call__(self, ins):
        self.n += 1
        ins.then_inc(self.sem, 1)
        self.eng.wait_ge(self.sem, self.base + self.n)


def for_tiles(eng, count, body, ahead=(), ring=2, turns=False):
    def call(f, t, b, turn):
        f(t, b, turn if turns else is_zero(turn))

    def step(t, b, turn, last_b):
        for lead, f in ahead:
            if last_b is None or last_b + lead < ring:
                call(f, t + lead, (b + lead) % ring, turn + (b + lead) // ring)
        call(body, t, b, turn)

    for lead in sorted({k for k, _ in ahead}, reverse=True):
        for k, f in ahead:
            if k == lead:
                for t in range(k):
                    call(f, t, t % ring, 0)
    for t in range(ring):
        step(t, t, 0, None)
    if count > 2 * ring:
        with eng.Fori(1, count // ring - 1) as i:
            for b in range(ring):
                step(ring * i + b, b, i, None)
    for b in range(ring):
        step(count - ring + b, b, count // ring - 1, b)


def load_values(eng, row, most):
    return eng.bass.values_load_multi_w_load_instructions(row, engines=[eng.engine], min_val=0, max_val=most)[1]


def is_zero(turn):
    return isinstance(turn, int) and turn == 0


def carry_wait(eng, sem):
    eng.sem_inc(sem, 1)


def dram(nc, name, shape, dt=F32):
    return nc.dram_tensor(name, shape, dt, kind="Internal").ap()


def bc(ap, axis, shape):
    return ap.unsqueeze(axis).broadcast_to(shape)


class Net:

    def __init__(self, nc, ctx, a):
        self.nc, self.a = nc, a

        def sb(name, shape, dt=F32):
            return ctx.enter_context(nc.sbuf_tensor(name, shape, dt))

        self.x = sb("x_res", [P, T, D])
        self.acc_full = sb("acc", [Q, T * 2 * D])
        self.acc = self.acc_full[0:P, :]
        self.src_w = sb("src_w", [Q, WINDOWS], I32)
        self.dst_w = sb("dst_w", [Q, WINDOWS])
        self.win_tab = sb("win_tab", [1, 2 * WINDOWS], I32)
        self.ident = sb("ident", [Q, Q])
        self.iota_i = sb("iota_i", [Q, MT])
        self.first_edge = sb("first_edge", [WG, GROUPS_W], I32)
        self.base_col = sb("base_col", [WG, GROUPS_W])
        self.below = sb("below", [P, T])
        self.flag = sb("flag", [1, 1], I32)
        self.edges = dram(nc, "edges", [EPAD, 2], I32)
        self.attr = dram(nc, "attr", [EPAD, 4])
        self.scal_t = dram(nc, "scal_t", [8, EPAD])
        self.scal_parts = dram(nc, "scal_parts", [3, 8, EPAD], BF16)
        self.ones = sb("ones", [Q, Q])
        self.tri = sb("tri", [Q, Q])
        self.deg_out = sb("deg_out", [P, T])
        self.deg_in = sb("deg_in", [P, T])
        self.ra = sb("ra", [P, T])
        self.rb = sb("rb", [P, T])
        self.rc = sb("rc", [P, T])
        self.stats = sb("stats", [P, T, 6])
        self.mv = sb("mv", [P, T, 2])
        self.rstd = sb("rstd", [P, T])
        self.nmr = sb("nmr", [P, T])
        self.eps = sb("eps", [Q, 1])
        self.bank = [ctx.enter_context(nc.psum_tensor(f"bank{i}", [Q, 512], F32)) for i in range(8)]
        self.used = []

    def acc_view(self, width):
        return self.acc[:, 0:T * width].rearrange("p (t d) -> p t d", d=width)

    def phase(self, name):
        return Phase(self, name)


class Phase:

    def __init__(self, net, name):
        self.net, self.nc, self.name = net, net.nc, name
        self.ctx = ExitStack()
        if len(net.used) > 120:
            self.nc.clear_and_free_semaphores(net.used)
            self.nc.all_engine_barrier()
            net.used = []

    def __enter__(self):
        return self

    def __exit__(self, *e):
        return self.ctx.__exit__(*e)

    def sb(self, name, shape, dt=F32):
        return self.ctx.enter_context(self.nc.sbuf_tensor(f"{self.name}_{name}", shape, dt))

    def sem(self, name):
        sem = self.nc.alloc_semaphore(f"{self.name}_{name}")
        self.net.used.append(sem)
        return sem

    def block(self):
        return self.nc.Block()



def ceil_div(step, dve, out, x, divisor, whole, over):
    step(dve.tensor_scalar(out, x, 1.0 / divisor, None, ALU.mult))
    step(dve.tensor_copy(whole, out))
    step(dve.tensor_copy(over, whole))
    step(dve.tensor_tensor(out, out, over, ALU.subtract))
    step(dve.tensor_scalar(out, out, 0.0, None, ALU.is_gt))
    step(dve.tensor_tensor(out, out, over, ALU.add))


def split_node(step, dve, ids, tile, lane, whole):
    step(dve.tensor_copy(lane, ids))
    step(dve.tensor_scalar(whole, lane, 1.0 / P, None, ALU.mult))
    step(dve.tensor_copy(tile, whole))
    step(dve.scalar_tensor_tensor(lane, tile, -float(P), lane, ALU.mult, ALU.add))
    low = whole.bitcast(F32)
    step(dve.tensor_scalar(low, lane, 0.0, None, ALU.is_lt))
    step(dve.tensor_tensor(tile, tile, low, ALU.subtract))
    step(dve.scalar_tensor_tensor(lane, low, float(P), lane, ALU.mult, ALU.add))
    step(dve.tensor_scalar(low, lane, float(P), None, ALU.is_ge))
    step(dve.tensor_tensor(tile, tile, low, ALU.add))
    step(dve.scalar_tensor_tensor(lane, low, -float(P), lane, ALU.mult, ALU.add))


def prepare(net, buf):
    nc, a = net.nc, net.a
    COLS = 8
    with net.phase("prep") as ph:
        base = net.acc
        ids = [base[:, k * EC:(k + 1) * EC].bitcast(I32) for k in (0, 1)]
        next_dst = base[:, 2 * EC:3 * EC].bitcast(I32)
        tiles, lanes = base[:, 3 * EC:4 * EC], base[:, 4 * EC:5 * EC]
        whole = base[:, 5 * EC:6 * EC].bitcast(I32)
        dst_f, next_f = base[:, 6 * EC:7 * EC], base[:, 7 * EC:8 * EC]
        junk = base[:, 8 * EC:9 * EC]
        SCRATCH = 16
        scratch = [base[:, (9 + k) * EC:(10 + k) * EC] for k in range(SCRATCH)]
        tiles_bf, lanes_bf = ph.sb("tiles_bf", [P, EC], BF16), ph.sb("lanes_bf", [P, EC], BF16)
        iota_bf = ph.sb("iota_bf", [P, P], BF16)
        lane_hot = [ph.sb(f"lane_hot{k}", [P, COLS, P], BF16) for k in (0, 1)]
        tile_hot = [ph.sb(f"tile_hot{k}", [P, COLS, T], BF16) for k in (0, 1)]
        zero_bf = ph.sb("zero_bf", [P, P], BF16)
        CLEAR = 18
        zero, s_clear = ph.sb("zero", [Q, CLEAR * D]), ph.sem("clear")
        bounds = ph.sb("bounds", [P, T])
        below, count = net.below, ph.sb("count", [P, T])
        bad = ph.sb("bad", [P, 1])
        col = ph.sb("col", [T, 8])
        coli = ph.sb("coli", [T, 1], I32)
        past = ph.sb("past", [T, WINDOWS])
        edge_row = base[0:1, 9 * EC:9 * EC + WINDOWS]
        first_col = ph.sb("first_col", [WG, GROUPS_W])
        number = ph.sb("number", [WG, GROUPS_W])
        iota_w = ph.sb("iota_w", [T, WINDOWS])
        s_const, s_x, s_ids = ph.sem("const"), ph.sem("x"), [ph.sem("src"), ph.sem("dst")]
        s_step, s_hot, s_used, s_hist = ph.sem("step"), ph.sem("hot"), ph.sem("used"), ph.sem("hist")
        s_below, s_cnt, s_pairs, s_end = ph.sem("below"), ph.sem("cnt"), ph.sem("pairs"), ph.sem("end")
        s_edge = ph.sem("edge")
        s_past, s_sum, s_copies, s_zero = ph.sem("past"), ph.sem("sum"), ph.sem("copies"), ph.sem("zero")
        hist, tile_h, first_h = net.bank[0], net.bank[1:3], net.bank[3:5]
        small, by_window = net.bank[5], net.bank[6]
        HALF = WINDOWS // 2

        with ph.block() as block:
            @block.gpsimd
            def _(pool):
                pool.memset(net.ones[:, :], 1.0).then_inc(s_const, 1)
                pool.memset(net.eps[:, :], LN_EPS).then_inc(s_const, 1)
                pool.memset(zero[:, :], 0.0).then_inc(s_zero, 1)
                pool.iota(iota_w[:, :], [[1, WINDOWS]], base=0, channel_multiplier=0,
                          allow_small_or_imprecise_dtypes=True).then_inc(s_const, 1)
                pool.iota(net.iota_i[:, :], [[1, MT]], base=0, channel_multiplier=0,
                          allow_small_or_imprecise_dtypes=True).then_inc(s_const, 1)
                pool.iota(number[:, :], [[WIN * WG, GROUPS_W]], base=0, channel_multiplier=WIN,
                          allow_small_or_imprecise_dtypes=True).then_inc(s_const, 1)
                pool.wait_ge(s_const, 5)
                pool.affine_select(out=net.ident[:, :], in_=net.ones[:, :], compare_op=ALU.is_equal, fill=0.0,
                                   base=0, pattern=[[-1, Q]], channel_multiplier=1).then_inc(s_const, 1)
                pool.affine_select(out=net.tri[:, :], in_=net.ones[:, :], compare_op=ALU.is_ge, fill=0.0,
                                   base=-1, pattern=[[1, Q]], channel_multiplier=-1).then_inc(s_const, 1)

            @block.sync
            def _(sp):
                dst, tail = a["dst"], (P - 1) * EC
                sp.dma_start(ids[1], dst.rearrange("(p c) -> p c", c=EC)).then_inc(s_ids[1], 16)
                sp.dma_start(next_dst[0:P - 1, :],
                             dst[1:tail + 1].rearrange("(p c) -> p c", c=EC)).then_inc(s_ids[1], 16)
                sp.dma_start(next_dst[P - 1:P, 0:EC - 1], dst[tail + 1:E].unsqueeze(0)).then_inc(s_ids[1], 16)
                sp.dma_start(next_dst[P - 1:P, EC - 1:EC], dst[E - 1:E].unsqueeze(0)).then_inc(s_ids[1], 16)
                sp.dma_start(ids[0], a["src"].rearrange("(p c) -> p c", c=EC)).then_inc(s_ids[0], 16)
                sp.dma_start(net.x[:, :, :], a["x"].rearrange("(t p) d -> p t d", p=P)).then_inc(s_x, 16)
                sp.wait_ge(s_zero, 2)
                for g in range(MT // CLEAR):
                    sp.dma_start(buf[CLEAR * Q * g:CLEAR * Q * (g + 1), :].rearrange("(p r) d -> p (r d)", p=Q),
                                 zero[:, :]).then_inc(s_clear, 16)
                sp.wait_ge(s_clear, 16 * (MT // CLEAR))
                sp.wait_ge(s_x, 16)

            @block.scalar
            def _(act):
                for to, of, rows in ((net.edges, a["edge_index"], 208), (net.attr, a["edge_attr"], 208)):
                    act.dma_start(to.rearrange("(r n) k -> r (n k)", r=rows),
                                  of.rearrange("(r n) k -> r (n k)", r=rows)).then_inc(s_copies, 16)
                act.dma_start(net.scal_t.rearrange("k (r n) -> (k r) n", r=32),
                              a["edge_scal_t"].rearrange("k (r n) -> (k r) n", r=32)).then_inc(s_copies, 16)
                act.wait_ge(s_copies, 48)

            @block.vector
            def _(dve):
                step = Chain(dve, s_step)
                dve.memset(zero_bf[:, :], 0.0).then_inc(s_zero, 1)
                dve.wait_ge(s_const, 7)
                dve.tensor_copy(iota_bf[:, :], net.iota_i[0:P, 0:P])
                step(dve.tensor_scalar(bounds[:, :], net.iota_i[0:P, 0:T], float(P), float(P), ALU.mult, ALU.add))
                dve.wait_ge(s_ids[1], 64)
                dve.tensor_copy(next_f, next_dst)
                step(dve.tensor_copy(dst_f, ids[1]))
                for b in range(T):
                    if b >= SCRATCH:
                        dve.wait_ge(s_below, b - SCRATCH + 1)
                    dve.tensor_scalar(scratch[b % SCRATCH], dst_f, bounds[:, b:b + 1], 0.0, ALU.is_lt, ALU.add,
                                      accum_out=below[:, b:b + 1]).then_inc(s_below, 1)
                dve.wait_ge(s_below, T)
                dve.tensor_copy(count[:, 0:1], below[:, 0:1])
                dve.tensor_tensor(count[:, 1:T], below[:, 1:T], below[:, 0:T - 1], ALU.subtract)
                step(dve.tensor_tensor(junk, dst_f, next_f, ALU.is_gt))
                dve.tensor_reduce(bad[:, :], junk, AX_X, ALU.add).then_inc(s_below, 1)
                dve.wait_ge(s_cnt, 2)
                dve.tensor_copy(net.flag[:, :], small[0:1, 2:3])
                step(dve.tensor_copy(col[:, 0:1], small[0:T, 0:1]))
                ceil_div(step, dve, col[:, 1:2], col[:, 0:1], WIN, coli[:, :], col[:, 2:3])
                dve.scalar_tensor_tensor(col[:, 3:4], col[:, 1:2], -float(WIN), col[:, 0:1],
                                         ALU.mult, ALU.add).then_inc(s_pairs, 1)
                dve.wait_ge(s_end, 1)
                step(dve.tensor_tensor(col[:, 4:5], small[0:T, 1:2], col[:, 1:2], ALU.add))
                dve.tensor_scalar(past[:, :], iota_w[:, :], col[:, 4:5], None, ALU.is_ge).then_inc(s_past, 1)
                dve.wait_ge(s_sum, 4 + 2 * GROUPS_W)
                for k in (0, 1):
                    of = slice(k * HALF, (k + 1) * HALF)
                    dve.tensor_scalar(net.win_tab[0:1, of], tile_h[k][0:1, 0:HALF], float(T - 1), None, ALU.min)
                    dve.scalar_tensor_tensor(edge_row[:, of],
                                             iota_w[0:1, of], float(WIN), first_h[k][0:1, 0:HALF],
                                             ALU.mult, ALU.add).then_inc(s_edge, 1)
                dve.wait_ge(s_edge, 2)
                dve.tensor_scalar(net.win_tab[0:1, WINDOWS:2 * WINDOWS], edge_row[:, :], float(E), None, ALU.min)
                step(dve.tensor_tensor(first_col[:, :], number[:, :], by_window[0:WG, 0:GROUPS_W], ALU.add))
                dve.tensor_scalar(net.first_edge[:, :], first_col[:, :], float(E), None, ALU.min)
                dve.tensor_scalar(net.base_col[:, :], by_window[0:WG, GROUPS_W:2 * GROUPS_W], float(T - 1), float(P),
                                  ALU.min, ALU.mult)
                dve.wait_ge(s_ids[0], 16)
                split_node(step, dve, ids[0], tiles, lanes, whole)
                dve.tensor_copy(tiles_bf[:, :], tiles)
                step(dve.tensor_copy(lanes_bf[:, :], lanes))
                with dve.Fori(0, EC // COLS // 2) as g:
                    for k in (0, 1):
                        dve.wait_ge(s_used, 2 * g + 1 + k)
                        cols = ds(COLS * (2 * g + k), COLS)
                        dve.tensor_tensor(lane_hot[k][:, :, :], bc(lanes_bf[:, cols], 2, [P, COLS, P]),
                                          bc(iota_bf[:, :], 1, [P, COLS, P]), ALU.is_equal).then_inc(s_hot, 1)
                        dve.tensor_tensor(tile_hot[k][:, :, :], bc(tiles_bf[:, cols], 2, [P, COLS, T]),
                                          bc(iota_bf[:, 0:T], 1, [P, COLS, T]), ALU.is_equal).then_inc(s_hot, 1)
                dve.wait_ge(s_hist, 1)
                dve.tensor_scalar(net.deg_out[:, :], hist[0:P, 0:T], 1.0, None, ALU.max)

            @block.tensor
            def _(pe):
                pe.wait_ge(s_const, 7)
                pe.wait_ge(s_below, T + 1)
                pe.matmul(small[0:T, 0:1], count[:, :], net.ones[0:P, 0:1], start=True, stop=True).then_inc(s_cnt, 1)
                pe.matmul(small[0:1, 2:3], bad[:, :], net.ones[0:P, 0:1], start=True, stop=True).then_inc(s_cnt, 1)
                pe.wait_ge(s_pairs, 1)
                pe.matmul(small[0:T, 1:2], net.tri[0:T, 0:T], col[:, 1:2], start=True, stop=True).then_inc(s_end, 1)
                pe.wait_ge(s_past, 1)
                for k in (0, 1):
                    of = past[:, k * HALF:(k + 1) * HALF]
                    pe.matmul(tile_h[k][0:1, 0:HALF], net.ones[0:T, 0:1], of, start=True, stop=True).then_inc(s_sum, 1)
                    pe.matmul(first_h[k][0:1, 0:HALF], col[:, 3:4], of, start=True, stop=True).then_inc(s_sum, 1)
                for g in range(GROUPS_W):
                    of = past[:, WG * g:WG * (g + 1)]
                    pe.matmul(by_window[0:WG, g:g + 1], of, col[:, 3:4], start=True, stop=True).then_inc(s_sum, 1)
                    pe.matmul(by_window[0:WG, GROUPS_W + g:GROUPS_W + g + 1], of, net.ones[0:T, 0:1],
                              start=True, stop=True).then_inc(s_sum, 1)
                pe.wait_ge(s_zero, 2)
                pe.matmul(hist[0:P, 0:T], zero_bf[:, :], zero_bf[:, 0:T], start=True, stop=False,
                          skip_group_check=True).then_inc(s_used, 2)
                with pe.Fori(0, EC // COLS // 2) as g:
                    for k in (0, 1):
                        pe.wait_ge(s_hot, 4 * g + 2 + 2 * k)
                        for j in range(COLS):
                            mm = pe.matmul(hist[0:P, 0:T], lane_hot[k][:, j, :], tile_hot[k][:, j, :],
                                           start=False, stop=False, skip_group_check=True)
                        mm.then_inc(s_used, 1)
                pe.matmul(hist[0:P, 0:T], zero_bf[:, :], zero_bf[:, 0:T], start=False, stop=True,
                          skip_group_check=True).then_inc(s_hist, 1)


def group_edges(net):
    nc, a = net.nc, net.a
    base = net.acc
    dst = base[:, EC:2 * EC].bitcast(I32)
    tiles, lanes = base[:, 2 * EC:3 * EC], base[:, 3 * EC:4 * EC]
    whole, place = base[:, 4 * EC:5 * EC].bitcast(I32), base[:, 5 * EC:6 * EC]
    scal_rows = dram(nc, "scal_rows", [E, 8])
    of_column = "(p c) k -> p c k"
    sources = (a["edge_index"][0:E].rearrange(of_column, c=EC), a["edge_attr"][0:E].rearrange(of_column, c=EC),
               a["edge_attr_8"].rearrange(of_column, c=EC))
    targets = (net.edges, net.attr, scal_rows)
    with net.phase("group") as ph:
        count, offset, junk = ph.sb("count", [P, T]), ph.sb("offset", [P, T]), ph.sb("junk", [P, T])
        to = [ph.sb(f"to{b}", [P, 1], I32) for b in (0, 1)]
        rec = [(ph.sb(f"ids{b}", [P, 2], I32), ph.sb(f"attr{b}", [P, 4]), ph.sb(f"scal{b}", [P, 8])) for b in (0, 1)]
        rows = [ph.sb(f"rows{b}", [P, 8]) for b in (0, 1)]
        cols = [ph.sb(f"cols{b}", [8, P]) for b in (0, 1)]
        s_step, s_count, s_offset, s_place = ph.sem("step"), ph.sem("count"), ph.sem("offset"), ph.sem("place")
        s_rec, s_to, s_sent = [ph.sem("rec0"), ph.sem("rec1")], ph.sem("to"), [ph.sem("sent0"), ph.sem("sent1")]
        s_idle, s_grouped, s_rows = ph.sem("idle"), ph.sem("grouped"), [ph.sem("rows0"), ph.sem("rows1")]
        s_turned, s_flat, s_stored = ph.sem("turned"), ph.sem("flat"), [ph.sem("stored0"), ph.sem("stored1")]

        def unordered(eng):
            return eng.If(eng.value_load(net.flag[0:1, 0:1], min_val=0, max_val=E) > 0)

        with ph.block() as block:
            @block.vector
            def _(dve):
                with unordered(dve):
                    step = Chain(dve, s_step)
                    split_node(step, dve, dst, tiles, lanes, whole)
                    step(dve.tensor_copy(count[:, 0:1], net.below[:, 0:1]))
                    dve.tensor_tensor(count[:, 1:T], net.below[:, 1:T], net.below[:, 0:T - 1],
                                      ALU.subtract).then_inc(s_count, 1)
                    dve.wait_ge(s_offset, 1)
                    dve.tensor_copy(offset[:, :], net.bank[0][0:P, 0:T]).then_inc(s_place, 1)
                    with dve.Fori(0, EC) as c:
                        dve.wait_ge(s_place, 2 * c + 1)
                        dve.scalar_tensor_tensor(junk[:, :], net.iota_i[0:P, 0:T], tiles[:, ds(c, 1)], offset[:, :],
                                                 ALU.is_equal, ALU.mult,
                                                 accum_out=place[:, ds(c, 1)]).then_inc(s_place, 1)
                        dve.wait_ge(s_place, 2 * c + 2)
                        dve.scalar_tensor_tensor(offset[:, :], net.iota_i[0:P, 0:T], tiles[:, ds(c, 1)], offset[:, :],
                                                 ALU.is_equal, ALU.add).then_inc(s_place, 1)
                    dve.wait_ge(s_place, 2 * EC + 1)

                    def stage(t, b, first):
                        if not first:
                            dve.wait_ge(s_sent[b], (t - b) * 24)
                        dve.tensor_copy(to[b][:, :], place[:, ds(t, 1)]).then_inc(s_to, 1)
                    for_tiles(dve, EC, stage)

                    def copy(t, b, first):
                        dve.wait_ge(s_turned, t + 1)
                        if not first:
                            dve.wait_ge(s_stored[b], (t - b) * 8)
                        dve.tensor_copy(cols[b][:, :], net.bank[b][0:8, 0:P]).then_inc(s_flat, 1)
                    for_tiles(dve, EC, copy)

            @block.tensor
            def _(pe):
                with unordered(pe):
                    pe.wait_ge(s_count, 1)
                    pe.matmul(net.bank[0][0:P, 0:T], net.tri[0:P, 0:P], count[:, :], start=True, stop=False,
                              skip_group_check=True)
                    pe.matmul(net.bank[0][0:P, 1:T], net.ones[0:P, 0:P], net.below[:, 0:T - 1], start=False, stop=True,
                              skip_group_check=True).then_inc(s_offset, 1)

                    def turn(t, b, first):
                        pe.wait_ge(s_rows[b], (t - b) * 8 + 16)
                        if not first:
                            pe.wait_ge(s_flat, t - 1)
                        pe.transpose(net.bank[b][0:8, 0:P], rows[b][:, :], net.ident[0:P, 0:P]).then_inc(s_turned, 1)
                    for_tiles(pe, EC, turn)

            @block.sync
            def _(sp):
                with unordered(sp):
                    def load(t, b, first):
                        if not first:
                            sp.wait_ge(s_sent[b], (t - b) * 24)
                        for r, of in zip(rec[b], sources):
                            sp.dma_start(r[:, :], of[:, ds(t, 1), :].rearrange("p c k -> p (c k)")).then_inc(s_rec[b], 16)
                    for_tiles(sp, EC, load)

                    def load_rows(t, b, first):
                        if not first:
                            sp.wait_ge(s_turned, t - 1)
                        sp.dma_start(rows[b][:, :], scal_rows[ds(P * t, P), :]).then_inc(s_rows[b], 16)
                    sp.wait_ge(s_grouped, 1)
                    for_tiles(sp, EC, load_rows)

            @block.gpsimd
            def _(pool):
                with unordered(pool):
                    def send(t, b, first):
                        pool.wait_ge(s_to, t + 1)
                        pool.wait_ge(s_rec[b], (t - b) * 24 + 48)
                        carry_wait(pool, s_idle)
                        for r, target in zip(rec[b], targets):
                            pool.indirect_dma_start(
                                out=target[:, :], out_offset=bass.IndirectOffsetOnAxis(ap=to[b][:, 0:1], axis=0),
                                in_=r[:, :], in_offset=None, bounds_check=E - 1, oob_is_err=False).then_inc(s_sent[b], 16)
                    for_tiles(pool, EC, send)
                    for b in (0, 1):
                        pool.wait_ge(s_sent[b], 24 * EC)
                    pool.sem_inc(s_grouped, 1)

            @block.scalar
            def _(act):
                with unordered(act):
                    def store(t, b, first):
                        act.wait_ge(s_flat, t + 1)
                        act.dma_start(net.scal_t[:, ds(P * t, P)], cols[b][:, :]).then_inc(s_stored[b], 16)
                    for_tiles(act, EC, store)
                    for b in (0, 1):
                        act.wait_ge(s_stored[b], 8 * EC)


def load_windows(net):
    with net.phase("windows") as ph:
        got = [ph.sb(f"got{g}", [WG, 2 * WIN], I32) for g in range(GROUPS_W)]
        src = [ph.sb(f"src{g}", [WG, WIN]) for g in range(GROUPS_W)]
        dst = [ph.sb(f"dst{g}", [WG, WIN]) for g in range(GROUPS_W)]
        s_got, s_flat, s_turned = ph.sem("got"), ph.sem("flat"), ph.sem("turned")
        of_src, of_dst = net.bank[0:2], net.bank[2:4]
        with ph.block() as block:
            @block.gpsimd
            def _(pool):
                for g in range(GROUPS_W):
                    pool.indirect_dma_start(
                        out=got[g][:, :], out_offset=None, in_=net.edges[:, :],
                        in_offset=bass.IndirectOffsetOnAxis(ap=net.first_edge[:, g:g + 1], axis=0)).then_inc(s_got, 16)

            @block.vector
            def _(dve):
                dve.wait_ge(s_got, 16 * GROUPS_W)
                for g in range(GROUPS_W):
                    dve.tensor_copy(src[g][:, :], got[g][:, 0::2]).then_inc(s_flat, 1)
                    dve.tensor_scalar(dst[g][:, :], got[g][:, 1::2], net.base_col[:, g:g + 1], None,
                                      ALU.subtract).then_inc(s_flat, 1)
                dve.wait_ge(s_turned, 2 * GROUPS_W)
                half = WINDOWS // 2
                for k in (0, 1):
                    dve.tensor_copy(net.src_w[:, k * half:(k + 1) * half], of_src[k][:, 0:half])
                    dve.tensor_copy(net.dst_w[:, k * half:(k + 1) * half], of_dst[k][:, 0:half])

            @block.tensor
            def _(pe):
                for g in range(GROUPS_W):
                    pe.wait_ge(s_flat, 2 * g + 2)
                    k, c = divmod(g, GROUPS_W // 2)
                    for of, to in ((src[g], of_src[k]), (dst[g], of_dst[k])):
                        pe.transpose(to[:, WG * c:WG * (c + 1)], of[:, :], net.ident[0:WG, 0:WG]).then_inc(s_turned, 1)



def layer_stats(net, tag, factors):
    with net.phase(tag) as ph:
        s_stat, s_step, s_var, s_root = ph.sem("stat"), ph.sem("step"), ph.sem("var"), ph.sem("root")
        s_own, s_own2 = ph.sem("own"), ph.sem("own2")
        with ph.block() as block:
            @block.vector
            def _(dve):
                with dve.Fori(0, T) as t:
                    dve.bn_stats(net.stats[:, ds(t, 1), :].rearrange("p a b -> p (a b)"),
                                 net.x[:, ds(t, 1), :].rearrange("p a d -> p (a d)")).then_inc(s_stat, 1)
                dve.wait_ge(s_stat, T)
                for t in range(T):
                    dve.bn_aggr(net.mv[:, t, :], net.stats[:, t, :]).then_inc(s_var, 1)
                step = Chain(dve, s_step)
                dve.wait_ge(s_root, 1)
                step(dve.reciprocal(net.rstd[:, :], net.rstd[:, :]))
                step(dve.scalar_tensor_tensor(net.nmr[:, :], net.mv[:, :, 0], -1.0, net.rstd[:, :],
                                              ALU.mult, ALU.mult))
                factors(step, dve, None, s_own, s_own2)

            @block.scalar
            def _(act):
                act.wait_ge(s_var, T)
                act.activation(net.rstd[:, :], net.mv[:, :, 1], ACT.Sqrt, bias=net.eps[0:P, :]).then_inc(s_root, 1)
                factors(None, None, act, s_own, s_own2)


def node_row(view, t):
    return view[:, ds(t, 1), :].rearrange("p a d -> p (a d)")


STORE = 5


def tiles_of(table, first):
    return table[ds(P * first, P * STORE), :].rearrange("(t p) d -> p t d", p=P)


def write_table(net, tag, table, scale, bias):
    with net.phase(tag) as ph:
        row = [ph.sb(f"row{b}", [P, STORE, D]) for b in (0, 1)]
        s_row, s_out = ph.sem("row"), [ph.sem("out0"), ph.sem("out1")]
        with ph.block() as block:
            @block.scalar
            def _(act):
                def body(g, b, first):
                    if not first:
                        act.wait_ge(s_out[b], (g - b) * 8)
                    for k in range(STORE):
                        t = STORE * g + k
                        ins = act.activation(row[b][:, k, :], node_row(net.x, t), ACT.Relu, bias=bias[:, ds(t, 1)],
                                             scale=scale[:, ds(t, 1)])
                    ins.then_inc(s_row, 1)
                for_tiles(act, T // STORE, body)

            @block.sync
            def _(sp):
                def body(g, b, first):
                    sp.wait_ge(s_row, g + 1)
                    sp.dma_start(tiles_of(table, STORE * g), row[b][:, :, :]).then_inc(s_out[b], 16)
                for_tiles(sp, T // STORE, body)
                for b in (0, 1):
                    sp.wait_ge(s_out[b], 16 * (T // STORE // 2))



def aggregate(net, tag, table, width, degrees=False, split=False):
    sums = width + 1 if degrees else width
    acc = net.acc_view(sums)
    GROUPS = 4
    PER = WPI // GROUPS
    LEAD = 2
    BANKS = LEAD * PER
    with net.phase(tag) as ph:
        msg = [ph.sb(f"msg{r}", [Q, sums]) for r in range(WPI)]
        hot = [ph.sb(f"hot{r}", [Q, P]) for r in range(WPI)]
        idx = [ph.sb(f"idx{g}", [Q, PER], I32) for g in range(GROUPS)]
        s_idx, s_idle = ph.sem("idx"), ph.sem("idle")
        s_msg = [ph.sem(f"msg{r}") for r in range(WPI)]
        s_hot, s_sum, s_add, s_clear = ph.sem("hot"), ph.sem("sum"), ph.sem("add"), ph.sem("clear")
        s_ones = ph.sem("ones")
        if split:
            whole = ph.sb("whole", [Q, SPLIT])
            parts = [ph.sb(f"part{k}", [Q, SPLIT], BF16) for k in range(3)]
            s_whole, s_parts, s_split = ph.sem("whole"), ph.sem("parts"), ph.sem("split")
            flat_in = net.scal_t.rearrange("k n -> (k n)").rearrange("(p c) -> p c", p=Q)
            flat_out = [net.scal_parts[k].rearrange("k n -> (k n)").rearrange("(p c) -> p c", p=Q) for k in range(3)]
        with ph.block() as block:
            @block.gpsimd
            def _(pool):
                if degrees:
                    for r in range(WPI):
                        pool.memset(msg[r][:, width:sums], 1.0).then_inc(s_ones, 1)
                with pool.Fori(0, STEPS) as i:
                    for g in range(GROUPS):
                        pool.wait_ge(s_idx, GROUPS * i + g + 1)
                        carry_wait(pool, s_idle)
                        for r in range(PER):
                            pool.indirect_dma_start(
                                out=msg[PER * g + r][:, 0:width], out_offset=None, in_=table[:, :],
                                in_offset=bass.IndirectOffsetOnAxis(ap=idx[g][:, r:r + 1], axis=0),
                            ).then_inc(s_msg[PER * g + r], 16)

            @block.vector
            def _(dve):
                def stage(i, r):
                    g = r // PER
                    if r % PER == 0:
                        dve.wait_ge(s_sum, WPI * i + PER * g + PER)
                        dve.tensor_copy(idx[g][:, :].bitcast(F32),
                                        net.src_w[:, ds(WPI * i + PER * g, PER)].bitcast(F32)).then_inc(s_idx, 1)
                    dve.tensor_scalar(hot[r][:, :], net.iota_i[:, 0:P], net.dst_w[:, ds(WPI * i + r, 1)], None,
                                      ALU.is_equal).then_inc(s_hot, 1)

                def add(i, w, tile):
                    dve.wait_ge(s_sum, WPI * i + w + 1 + WPI)
                    dve.wait_ge(s_add, WPI * i + w + 1)
                    row = node_row(acc, tile)
                    dve.tensor_tensor(row, row, net.bank[w % BANKS][0:P, 0:sums], ALU.add).then_inc(s_add, 1)

                def split_step(i, k):
                    if k == 0:
                        dve.wait_ge(s_whole, 16 * i + 16)
                        dve.wait_ge(s_parts, 48 * i + 48)
                    else:
                        dve.wait_ge(s_split, 5 * i + 5 + k)
                    if k % 2 == 0:
                        ins = dve.tensor_copy(parts[k // 2][:, :], whole[:, :])
                    else:
                        ins = dve.tensor_tensor(whole[:, :], whole[:, :], parts[k // 2][:, :], ALU.subtract)
                    ins.then_inc(s_split, 1)

                def steps(i, last):
                    tiles = load_values(dve, net.win_tab[0:1, ds(WPI * i, WPI)], T - 1)
                    for w in range(WPI):
                        add(i, w, tiles[w])
                        if w + BANKS < WPI:
                            stage(i, w + BANKS)
                        elif not last:
                            stage(i + 1, w + BANKS - WPI)
                        if split and 1 <= w <= 9 and w % 2:
                            split_step(i, w // 2)

                dve.memset(net.acc[:, 0:T * sums], 0.0).then_inc(s_clear, 1)
                dve.sem_inc(s_add, 1)
                for r in range(BANKS):
                    stage(0, r)
                dve.wait_ge(s_clear, 1)
                with dve.Fori(0, STEPS - 1) as i:
                    steps(i, False)
                steps(STEPS - 1, True)

            @block.tensor
            def _(pe):
                if degrees:
                    pe.wait_ge(s_ones, WPI)
                pe.sem_inc(s_sum, WPI)
                with pe.Fori(0, STEPS) as i:
                    for w in range(WPI):
                        pe.wait_ge(s_hot, WPI * i + w + 1)
                        pe.wait_ge(s_msg[w], 16 * i + 16)
                        pe.matmul(net.bank[w % BANKS][0:P, 0:sums], hot[w][:, :], msg[w][:, :],
                                  start=True, stop=True).then_inc(s_sum, 1)

            if split:
                @block.sync
                def _(sp):
                    sp.sem_inc(s_split, 5)
                    sp.sem_inc(s_parts, 48)
                    with sp.Fori(0, STEPS) as i:
                        sp.wait_ge(s_split, 5 * i + 5)
                        sp.dma_start(whole[:, :], flat_in[:, ds(SPLIT * i, SPLIT)]).then_inc(s_whole, 16)

                @block.scalar
                def _(act):
                    with act.Fori(0, STEPS) as i:
                        act.wait_ge(s_split, 5 * i + 10)
                        for k in range(3):
                            act.dma_start(flat_out[k][:, ds(SPLIT * i, SPLIT)], parts[k][:, :]).then_inc(s_parts, 16)
                    act.wait_ge(s_parts, 48 * STEPS + 48)



def node_stage(net, tag, chunks, load, stage, products, finish, steps=0, store=None):
    with net.phase(tag) as ph:
        rows = [ph.sb(f"rows{b}", [P, chunks * Q]) for b in (0, 1)]
        cols = [ph.sb(f"cols{b}", [Q, chunks, P]) for b in (0, 1)]
        turned, product = net.bank[0:2], net.bank[2:4]
        s_w, s_staged, s_turned, s_copied = ph.sem("w"), ph.sem("staged"), ph.sem("turned"), ph.sem("copied")
        s_product, s_finished, s_step = ph.sem("product"), ph.sem("finished"), ph.sem("step")
        s_stored = [ph.sem("stored0"), ph.sem("stored1")]
        s_init = ph.sem("init")
        loads = load(None, ph, None)
        with ph.block() as block:
            @block.sync
            def _(sp):
                load(sp, ph, s_w)
                if store:
                    def body(g, b, first):
                        sp.wait_ge(s_finished, STORE * g + STORE)
                        sp.dma_start(tiles_of(store[0], STORE * g), store[1][b][:, :, :]).then_inc(s_stored[b], 16)
                    for_tiles(sp, T // STORE, body)
                    for b in (0, 1):
                        sp.wait_ge(s_stored[b], 16 * (T // STORE // 2))

            @block.scalar
            def _(act):
                def body(t, b, first):
                    if not first:
                        act.wait_ge(s_turned, t - 1)
                    stage(act, t, rows[b]).then_inc(s_staged, 1)
                for_tiles(act, T, body)

            @block.tensor
            def _(pe):
                def turn(t, b, first):
                    pe.wait_ge(s_staged, t + 1)
                    for c in range(chunks):
                        mm = pe.transpose(turned[b][:, c * P:(c + 1) * P], rows[b][:, c * Q:(c + 1) * Q],
                                          net.ident[0:P, 0:P])
                    mm.then_inc(s_turned, 1)

                def body(t, b, first):
                    pe.wait_ge(s_copied, t + 1)
                    if not first:
                        pe.wait_ge(s_finished, t - 1)
                    products(pe, cols[b], product[b]).then_inc(s_product, 1)
                pe.wait_ge(s_w, 16 * loads)
                for_tiles(pe, T, body, ahead=((1, turn),))

            @block.vector
            def _(dve):
                def copy(t, b, turn):
                    dve.wait_ge(s_turned, t + 1)
                    dve.tensor_copy(cols[b % 2][:, :, :].rearrange("p c n -> p (c n)"),
                                    turned[b % 2][:, 0:chunks * P]).then_inc(s_copied, 1)

                def body(t, b, turn):
                    dve.wait_ge(s_product, t + 1)
                    if store and b % STORE == 0 and not is_zero(turn):
                        dve.wait_ge(s_stored[b // STORE], 16 * turn)
                    step = Chain(dve, s_step, t * steps)
                    row = store[1][b // STORE][:, b % STORE, :] if store else None
                    finish(dve, step, t, row, product[b % 2]).then_inc(s_finished, 1)
                    assert step.n == steps
                dve.wait_ge(s_w, 16 * loads)
                for_tiles(dve, T, body, ahead=((1, copy),), ring=2 * STORE, turns=True)


def loader(*items):
    def load(sp, ph, sem):
        n = 0
        if sp is None:
            ph.net.got = {}
            for name, shape, _ in items:
                ph.net.got[name] = ph.sb(name, shape)
        for name, _, pairs in items:
            for to, of in pairs(ph.net.got[name]):
                n += 1
                if sp is not None:
                    sp.dma_start(to, of).then_inc(sem, 16)
        return n
    return load


def row_of(vector, parts=P):
    return vector.unsqueeze(0).broadcast_to([parts, vector.shape[0]])


def in_chunks(w):
    return w.rearrange("(c p) n -> p c n", p=Q)



def experts(net, buf, outb, exp_row):
    nc, a = net.nc, net.a
    xm = net.acc_view(D)
    with ExitStack() as ctx:
        def sb(name, shape, dt=F32):
            return ctx.enter_context(nc.sbuf_tensor(f"moe_{name}", shape, dt))

        mask = sb("mask", [P, T, X_EXP])
        val = sb("val", [P, T, 2])
        exp_of = sb("exp_of", [P, T, 2])
        rank = sb("rank", [P, T, 2])
        gate = sb("gate", [P, T, 2])
        valid = sb("valid", [P, T, 2])
        put = sb("put", [P, T, 2], I32)
        get = sb("get", [P, T, 2], I32)
        exp_tab = sb("exp_tab", [1, MT], I32)

        s_idle = nc.alloc_semaphore("route_idle")
        logits, top, top_i = sb("logits", [P, X_EXP]), sb("top", [P, 8]), sb("top_i", [P, 8], U32)

        def stage(act, t, rows):
            return act.activation(rows[:, :], node_row(xm, t), ACT.Copy)

        def products(pe, cols, po):
            for c in (0, 1):
                mm = pe.matmul(po[0:P, 0:X_EXP], cols[:, c, :], net.got["wg"][:, c, :], start=(c == 0), stop=(c == 1))
            return mm

        def finish(dve, step, t, row, po):
            step(dve.tensor_tensor(logits[:, :], po[0:P, 0:X_EXP], net.got["bg"][:, :], ALU.add))
            carry_wait(dve, s_idle)
            step(dve.max(top[:, :], logits[:, :]))
            carry_wait(dve, s_idle)
            step(dve.max_index(top_i[:, :], top[:, :], logits[:, :]))
            dve.tensor_copy(node_row(val, t), top[:, 0:2])
            e = node_row(exp_of, t)
            step(dve.tensor_copy(e, top_i[:, 0:2]))
            m = node_row(mask, t)
            step(dve.tensor_scalar(m, net.iota_i[0:P, 0:X_EXP], exp_of[:, ds(t, 1), 0], None, ALU.is_equal))
            return dve.scalar_tensor_tensor(m, net.iota_i[0:P, 0:X_EXP], exp_of[:, ds(t, 1), 1], m,
                                            ALU.is_equal, ALU.add)

        node_stage(net, "route", 2, loader(
            ("wg", [Q, 2, X_EXP], lambda w: [(w[:, :, :], in_chunks(a["L0_gnn_Wg"]))]),
            ("bg", [P, X_EXP], lambda w: [(w[:, :], row_of(a["L0_gnn_bg"]))])), stage, products, finish, steps=5)

        with net.phase("rank") as ph:
            carry, place, junk = ph.sb("carry", [P, X_EXP]), ph.sb("place", [P, X_EXP]), ph.sb("junk", [P, 2, X_EXP])
            counts, col, coli = ph.sb("counts", [P, X_EXP]), ph.sb("col", [X_EXP, 8]), ph.sb("coli", [X_EXP, 1], I32)
            past, tiles_bc, start = ph.sb("past", [X_EXP, MT]), ph.sb("tiles_bc", [X_EXP, P]), ph.sb("start", [P, X_EXP])
            place_of, diff = ph.sb("place_of", [P, T, 2]), ph.sb("diff", [P, T])
            pick = net.acc[:, T * D:T * D + 2 * T * X_EXP].rearrange("p (n e) -> p n e", e=X_EXP)
            s_rank, s_used, s_step = ph.sem("rank"), ph.sem("used"), ph.sem("step")
            s_counts, s_cnt, s_tiles, s_end, s_past = (ph.sem("counts"), ph.sem("cnt"), ph.sem("tiles"),
                                                       ph.sem("end"), ph.sem("past"))
            s_rows, s_diff, s_exp, s_zero = ph.sem("rows"), ph.sem("diff"), ph.sem("exp"), ph.sem("zero")
            small, exp_h, start_h = net.bank[2], net.bank[3], net.bank[4]
            with ph.block() as block:
                @block.tensor
                def _(pe):
                    def body(t, b, first):
                        if not first:
                            pe.wait_ge(s_used, t - 1)
                        m = node_row(mask, t)
                        pe.matmul(net.bank[b][0:P, 0:X_EXP], net.tri[0:P, 0:P], m, start=True, stop=True)
                        pe.matmul(net.bank[b][0:P, X_EXP:2 * X_EXP], net.ones[0:P, 0:P], m,
                                  start=True, stop=True).then_inc(s_rank, 1)
                    for_tiles(pe, T, body)
                    pe.wait_ge(s_counts, 1)
                    pe.matmul(small[0:X_EXP, 0:1], counts[:, :], net.ones[0:P, 0:1], start=True, stop=True).then_inc(s_cnt, 1)
                    pe.wait_ge(s_tiles, 1)
                    pe.matmul(small[0:X_EXP, 1:2], net.tri[0:X_EXP, 0:X_EXP], col[:, 1:2], start=True, stop=True)
                    pe.matmul(start_h[0:P, 0:X_EXP], tiles_bc[:, :], net.tri[0:X_EXP, 0:X_EXP],
                              start=True, stop=True).then_inc(s_end, 1)
                    pe.wait_ge(s_past, 1)
                    pe.matmul(exp_h[0:1, 0:MT], net.ones[0:X_EXP, 0:1], past[:, :], start=True, stop=True).then_inc(s_rows, 1)

                @block.scalar
                def _(act):
                    act.wait_ge(s_diff, 1)
                    act.activation(gate[:, :, 1], diff[:, :], ACT.Exp).then_inc(s_exp, 1)

                @block.vector
                def _(dve):
                    dve.tensor_tensor(diff[:, :], val[:, :, 1], val[:, :, 0], ALU.subtract).then_inc(s_diff, 1)
                    dve.memset(carry[:, :], 0.0).then_inc(s_zero, 1)
                    dve.wait_ge(s_zero, 1)

                    def body(t, b, first):
                        step = Chain(dve, s_step, t)
                        dve.wait_ge(s_rank, t + 1)
                        if not (isinstance(t, int) and t == 0):
                            dve.wait_ge(s_used, t)
                        step(dve.tensor_tensor(place[:, :], net.bank[b][0:P, 0:X_EXP], carry[:, :], ALU.add))
                        for k in (0, 1):
                            dve.scalar_tensor_tensor(junk[:, k, :], net.iota_i[0:P, 0:X_EXP], exp_of[:, ds(t, 1), k],
                                                     place[:, :], ALU.is_equal, ALU.mult,
                                                     accum_out=rank[:, ds(t, 1), k])
                        dve.tensor_tensor(carry[:, :], net.bank[b][0:P, X_EXP:2 * X_EXP], carry[:, :],
                                          ALU.add).then_inc(s_used, 1)
                    for_tiles(dve, T, body)
                    step = Chain(dve, s_step, T)
                    dve.tensor_reduce(counts[:, :], mask[:, :, :].rearrange("p t e -> p e t"), AX_X, ALU.add).then_inc(s_counts, 1)
                    dve.wait_ge(s_cnt, 1)
                    step(dve.tensor_scalar(col[:, 0:1], small[0:X_EXP, 0:1], float(CAP), None, ALU.min))
                    ceil_div(step, dve, col[:, 1:2], col[:, 0:1], Q, coli[:, :], col[:, 2:3])
                    dve.tensor_scalar(tiles_bc[:, :], net.ones[0:X_EXP, 0:P], col[:, 1:2], None, ALU.mult).then_inc(s_tiles, 1)
                    dve.wait_ge(s_end, 1)
                    step(dve.tensor_tensor(col[:, 4:5], small[0:X_EXP, 1:2], col[:, 1:2], ALU.add))
                    dve.tensor_scalar(past[:, :], net.iota_i[0:X_EXP, 0:MT], col[:, 4:5], None, ALU.is_ge).then_inc(s_past, 1)
                    step(dve.tensor_scalar(start[:, :], start_h[0:P, 0:X_EXP], float(Q), None, ALU.mult))
                    dve.wait_ge(s_rows, 1)
                    dve.tensor_scalar(exp_tab[:, :], exp_h[0:1, 0:MT], float(X_EXP - 1), None, ALU.min)
                    chosen = exp_of[:, :, :].rearrange("p t k -> p (t k)")
                    wide = [P, 2 * T, X_EXP]
                    step(dve.tensor_tensor(pick, bc(chosen, 2, wide), bc(net.iota_i[0:P, 0:X_EXP], 1, wide), ALU.is_equal))
                    step(dve.tensor_tensor(pick, pick, bc(start[:, :], 1, wide), ALU.mult))
                    step(dve.tensor_reduce(place_of[:, :, :].rearrange("p t k -> p (t k)"), pick, AX_X, ALU.add))
                    step(dve.tensor_tensor(place_of[:, :, :], place_of[:, :, :], rank[:, :, :], ALU.add))
                    step(dve.tensor_scalar(valid[:, :, :], rank[:, :, :], float(CAP), None, ALU.is_lt))
                    step(dve.tensor_tensor(get[:, :, :], place_of[:, :, :], valid[:, :, :], ALU.mult))
                    step(dve.tensor_scalar(rank[:, :, :], valid[:, :, :], -1e6, 1e6, ALU.mult, ALU.add))
                    step(dve.tensor_tensor(put[:, :, :], place_of[:, :, :], rank[:, :, :], ALU.add))
                    dve.wait_ge(s_exp, 1)
                    step(dve.tensor_scalar(gate[:, :, 0], gate[:, :, 1], 1.0, None, ALU.add))
                    step(dve.reciprocal(gate[:, :, 0], gate[:, :, 0]))
                    step(dve.tensor_tensor(gate[:, :, 1], gate[:, :, 1], gate[:, :, 0], ALU.mult))
                    dve.tensor_tensor(gate[:, :, :], gate[:, :, :], valid[:, :, :], ALU.mult)

        with net.phase("send") as ph:
            row = [ph.sb(f"row{b}", [P, D]) for b in (0, 1)]
            to = [ph.sb(f"to{b}", [P, 2], I32) for b in (0, 1)]
            s_idle = ph.sem("idle")
            s_row, s_to, s_sent = ph.sem("row"), ph.sem("to"), [ph.sem("sent0"), ph.sem("sent1")]
            with ph.block() as block:
                @block.scalar
                def _(act):
                    def body(t, b, first):
                        if not first:
                            act.wait_ge(s_sent[b], (t - b) * 16)
                        act.activation(row[b][:, :], node_row(xm, t), ACT.Copy).then_inc(s_row, 1)
                    for_tiles(act, T, body)

                @block.vector
                def _(dve):
                    def body(t, b, first):
                        if not first:
                            dve.wait_ge(s_sent[b], (t - b) * 16)
                        dve.tensor_copy(to[b][:, :].bitcast(F32), node_row(put, t).bitcast(F32)).then_inc(s_to, 1)
                    for_tiles(dve, T, body)

                @block.gpsimd
                def _(pool):
                    def body(t, b, first):
                        pool.wait_ge(s_row, t + 1)
                        pool.wait_ge(s_to, t + 1)
                        carry_wait(pool, s_idle)
                        for k in (0, 1):
                            pool.indirect_dma_start(
                                out=buf[:, :], out_offset=bass.IndirectOffsetOnAxis(ap=to[b][:, k:k + 1], axis=0),
                                in_=row[b][:, :], in_offset=None, bounds_check=TOK_ROWS - 1, oob_is_err=False,
                            ).then_inc(s_sent[b], 16)
                    for_tiles(pool, T, body)
                    for b in (0, 1):
                        pool.wait_ge(s_sent[b], 16 * T)

        with net.phase("ffn") as ph:
            R = RING = 6
            KD, KH = D // Q, HID // Q
            free = net.acc_full[:, T * D:2 * T * D]
            w1 = [free[:, r * D * HID // Q:(r + 1) * D * HID // Q].rearrange("p (c n) -> p c n", c=KD) for r in range(R)]
            w2 = [free[:, (R + r) * D * HID // Q:(R + r + 1) * D * HID // Q].rearrange("p (c n) -> p c n", c=KH)
                  for r in range(R)]
            b1 = [ph.sb(f"b1_{r}", [Q, KH]) for r in range(R)]
            b2 = [ph.sb(f"b2_{r}", [Q, D]) for r in range(R)]
            rows = [ph.sb(f"rows{r}", [Q, D]) for r in range(R)]
            cols = [ph.sb(f"cols{r}", [Q, KD, Q]) for r in (0, 1)]
            hid = [ph.sb(f"hid{r}", [Q, KH, Q]) for r in (0, 1)]
            res = [ph.sb(f"res{r}", [Q, D]) for r in (0, 1)]
            turned, hidden, product = net.bank[0:2], net.bank[2:4], net.bank[4:6]
            s_w = [ph.sem(f"w{r}") for r in range(R)]
            s_in = [ph.sem(f"in{r}") for r in range(R)]
            s_turned, s_copied, s_hidden, s_gelu = ph.sem("turned"), ph.sem("copied"), ph.sem("hidden"), ph.sem("gelu")
            s_product, s_res, s_stored = ph.sem("product"), ph.sem("res"), [ph.sem("st0"), ph.sem("st1")]
            with ph.block() as block:
                @block.sync
                def _(sp):
                    def body(t, b, first):
                        e = sp.value_load(exp_tab[0:1, ds(t, 1)], min_val=0, max_val=X_EXP - 1)
                        r = b % R
                        if not (first and b < R):
                            sp.wait_ge(s_product, t - R + 1)
                        sp.dma_start(w1[r][:, :, :].rearrange("p c n -> p (c n)"),
                                     a["L0_gnn_w1"][ds(e, 1)].rearrange("e (p c) n -> p (e c n)", c=KD)).then_inc(s_w[r], 16)
                        sp.dma_start(w2[r][:, :, :].rearrange("p c n -> p (c n)"),
                                     a["L0_gnn_w2"][ds(e, 1)].rearrange("e (p c) n -> p (e c n)", c=KH)).then_inc(s_w[r], 32)
                    for_tiles(sp, MT, body, ring=RING)

                @block.gpsimd
                def _(pool):
                    def body(t, b, first):
                        e = pool.value_load(exp_tab[0:1, ds(t, 1)], min_val=0, max_val=X_EXP - 1)
                        r = b % R
                        if not (first and b < R):
                            pool.wait_ge(s_res, t - R + 1)
                        pool.dma_start(rows[r][:, :], buf[ds(Q * t, Q), :]).then_inc(s_in[r], 16)
                        pool.dma_start(b1[r][:, :], a["L0_gnn_b1"][ds(e, 1)].rearrange("e (p c) -> p (e c)", c=KH)).then_inc(s_in[r], 16)
                        pool.dma_start(b2[r][:, :], a["L0_gnn_b2"][ds(e, 1)].broadcast_to([Q, D])).then_inc(s_in[r], 16)
                    for_tiles(pool, MT, body, ring=RING)

                def loaded(eng, sem, each, t, b):
                    eng.wait_ge(sem[b], each // R * (t - b) + each)

                @block.tensor
                def _(pe):
                    def turn(t, b, first):
                        loaded(pe, s_in, 48, t, b)
                        if not (first and b < 2):
                            pe.wait_ge(s_copied, t - 1)
                        for c in range(KD):
                            mm = pe.transpose(turned[b % 2][:, c * Q:(c + 1) * Q], rows[b % R][:, c:D:KD], net.ident[:, :])
                        mm.then_inc(s_turned, 1)

                    def up(t, b, first):
                        loaded(pe, s_w, 48, t, b)
                        pe.wait_ge(s_copied, t + 1)
                        if not (first and b < 2):
                            pe.wait_ge(s_gelu, t - 1)
                        for j in range(KH):
                            for c in range(KD):
                                mm = pe.matmul(hidden[b % 2][:, j * Q:(j + 1) * Q], w1[b % R][:, c, j:HID:KH],
                                               cols[b % 2][:, c, :], start=(c == 0), stop=(c == KD - 1))
                        mm.then_inc(s_hidden, 1)

                    def down(t, b, first):
                        pe.wait_ge(s_gelu, t + 1)
                        if not (first and b < 2):
                            pe.wait_ge(s_res, t - 1)
                        for j in range(KH):
                            mm = pe.matmul(product[b % 2][:, 0:D], hid[b % 2][:, j, :], w2[b % R][:, j, :],
                                           start=(j == 0), stop=(j == KH - 1))
                        mm.then_inc(s_product, 1)
                    for_tiles(pe, MT, down, ahead=((2, turn), (1, up)), ring=RING)

                @block.scalar
                def _(act):
                    def body(t, b, first):
                        act.wait_ge(s_hidden, t + 1)
                        loaded(act, s_in, 48, t, b)
                        if not (first and b < 2):
                            act.wait_ge(s_product, t - 1)
                        for j in range(KH):
                            ins = act.activation(hid[b % 2][:, j, :], hidden[b % 2][:, j * Q:(j + 1) * Q], ACT.Gelu,
                                                 bias=b1[b % R][:, j:j + 1])
                        ins.then_inc(s_gelu, 1)

                    def store(t, b, first):
                        act.wait_ge(s_res, t + 1)
                        act.dma_start(outb[ds(Q * t, Q), :], res[b % 2][:, :]).then_inc(s_stored[b % 2], 16)
                    for_tiles(act, MT, store, ahead=((1, body),), ring=RING)
                    for b in (0, 1):
                        act.wait_ge(s_stored[b], 16 * (MT // 2))

                @block.vector
                def _(dve):
                    def copy(t, b, first):
                        dve.wait_ge(s_turned, t + 1)
                        if not (first and b < 2):
                            dve.wait_ge(s_hidden, t - 1)
                        dve.tensor_copy(cols[b % 2][:, :, :].rearrange("p c n -> p (c n)"),
                                        turned[b % 2][:, 0:D]).then_inc(s_copied, 1)

                    def body(t, b, first):
                        dve.wait_ge(s_product, t + 1)
                        loaded(dve, s_in, 48, t, b)
                        if not (first and b < 2):
                            dve.wait_ge(s_stored[b % 2], 8 * (t - b % 2))
                        dve.tensor_tensor(res[b % 2][:, :], product[b % 2][:, 0:D], b2[b % R][:, :], ALU.add).then_inc(s_res, 1)
                    for_tiles(dve, MT, body, ahead=((2, copy),), ring=RING)

        with net.phase("take") as ph:
            R = 2
            got = [[ph.sb(f"got{b}{k}", [P, D]) for k in (0, 1)] for b in (0, 1)]
            of = [ph.sb(f"of{b}", [P, 2], I32) for b in (0, 1)]
            s_idle = ph.sem("idle")
            s_of, s_got, s_y, s_step = ph.sem("of"), [ph.sem("got0"), ph.sem("got1")], ph.sem("y"), ph.sem("step")
            with ph.block() as block:
                @block.gpsimd
                def _(pool):
                    def body(t, b, first):
                        pool.wait_ge(s_of, t + 1)
                        carry_wait(pool, s_idle)
                        for k in (0, 1):
                            pool.indirect_dma_start(
                                out=got[b][k][:, :], out_offset=None, in_=outb[:, :],
                                in_offset=bass.IndirectOffsetOnAxis(ap=of[b][:, k:k + 1], axis=0),
                            ).then_inc(s_got[b], 16)
                    for_tiles(pool, T, body)

                @block.vector
                def _(dve):
                    def ahead(t, b, first):
                        if not first:
                            dve.wait_ge(s_y, t - 1)
                        dve.tensor_copy(of[b][:, :].bitcast(F32), node_row(get, t).bitcast(F32)).then_inc(s_of, 1)

                    def body(t, b, first):
                        dve.wait_ge(s_got[b], (t - b) * 16 + 32)
                        step = Chain(dve, s_step, t)
                        y = node_row(xm, t)
                        step(dve.scalar_tensor_tensor(y, got[b][0][:, :], gate[:, ds(t, 1), 0], y, ALU.mult, ALU.add))
                        dve.scalar_tensor_tensor(y, got[b][1][:, :], gate[:, ds(t, 1), 1], y,
                                                 ALU.mult, ALU.add).then_inc(s_y, 1)
                    for_tiles(dve, T, body, ahead=((1, ahead),))


def batch_norm(net):
    a = net.a
    y = net.acc_view(D)
    sq = net.acc[:, T * D:2 * T * D].rearrange("p (t d) -> p t d", d=D)
    by_column = "p t d -> p d t"
    with net.phase("bn") as ph:
        part, mean, scale = ph.sb("part", [P, D]), ph.sb("mean", [P, D]), ph.sb("scale", [P, D])
        gamma, beta = ph.sb("gamma", [P, D]), ph.sb("beta", [P, D])
        s_w, s_part, s_all, s_step, s_yc, s_sq = (ph.sem("w"), ph.sem("part"), ph.sem("all"), ph.sem("step"),
                                                  ph.sem("yc"), ph.sem("sq"))
        s_var, s_root = ph.sem("var"), ph.sem("root")
        wide = [P, T, D]
        with ph.block() as block:
            @block.sync
            def _(sp):
                sp.dma_start(gamma[:, :], row_of(a["L0_gnn_gamma"])).then_inc(s_w, 16)
                sp.dma_start(beta[:, :], row_of(a["L0_gnn_beta"])).then_inc(s_w, 16)

            @block.tensor
            def _(pe):
                for k in (0, 1):
                    pe.wait_ge(s_part, k + 1)
                    pe.matmul(net.bank[k][0:P, 0:D], net.ones[0:P, 0:P], part[:, :], start=True, stop=True).then_inc(s_all, 1)

            @block.scalar
            def _(act):
                act.wait_ge(s_yc, 1)
                act.activation(sq, y, ACT.Square).then_inc(s_sq, 1)
                act.wait_ge(s_var, 1)
                act.activation(scale[:, :], scale[:, :], ACT.Sqrt).then_inc(s_root, 1)

            @block.vector
            def _(dve):
                step = Chain(dve, s_step)
                dve.tensor_reduce(part[:, :], y.rearrange(by_column), AX_X, ALU.add).then_inc(s_part, 1)
                dve.wait_ge(s_all, 1)
                step(dve.tensor_scalar(mean[:, :], net.bank[0][0:P, 0:D], 1.0 / N, None, ALU.mult))
                dve.tensor_tensor(y, y, bc(mean[:, :], 1, wide), ALU.subtract).then_inc(s_yc, 1)
                dve.wait_ge(s_sq, 1)
                dve.tensor_reduce(part[:, :], sq.rearrange(by_column), AX_X, ALU.add).then_inc(s_part, 1)
                dve.wait_ge(s_all, 2)
                dve.tensor_scalar(scale[:, :], net.bank[1][0:P, 0:D], 1.0 / N, BN_EPS, ALU.mult, ALU.add).then_inc(s_var, 1)
                dve.wait_ge(s_root, 1)
                step(dve.reciprocal(scale[:, :], scale[:, :]))
                dve.wait_ge(s_w, 32)
                step(dve.tensor_tensor(scale[:, :], scale[:, :], gamma[:, :], ALU.mult))
                step(dve.tensor_tensor(y, y, bc(scale[:, :], 1, wide), ALU.mult))
                step(dve.tensor_tensor(y, y, bc(beta[:, :], 1, wide), ALU.add))
                step(dve.tensor_tensor(net.x[:, :, :], net.x[:, :, :], y, ALU.add))



PAIRS = 3 * 3 * 8
BL = 8

def tensor_product_edges(net, table):
    nc, a = net.nc, net.a
    acc = net.acc_view(2 * D)
    R = 8
    with net.phase("tp") as ph:
        attr = [ph.sb(f"attr{r}", [Q, 4]) for r in range(R)]
        scal = [ph.sb(f"scal{r}", [PAIRS, WIN], BF16) for r in range(R)]
        fc1, fc2 = ph.sb("fc1", [8, MUL]), ph.sb("fc2", [MUL, 4, MUL])
        fc1_parts = [ph.sb(f"fc1_part{k}", [8, MUL], BF16) for k in range(3)]
        fc1_pairs = ph.sb("fc1_pairs", [PAIRS, MUL], BF16)
        hid = [ph.sb(f"hid{r}", [MUL, WIN]) for r in (0, 1)]
        src = [ph.sb(f"src{r}", [Q, D]) for r in range(R)]
        idx = [ph.sb(f"idx{r}", [Q, 2], I32) for r in range(R // 2)]
        hot = [ph.sb(f"hot{r}", [Q, P]) for r in range(R)]
        hots = [ph.sb(f"hots{r}", [Q, 4, P]) for r in (0, 1)]
        msg = [ph.sb(f"msg{r}", [Q, BL, MUL]) for r in (0, 1)]
        s_fc, s_fcs, s_attr = ph.sem("fc"), ph.sem("fcs"), [ph.sem(f"attr{r}") for r in range(R)]
        s_fc1, s_pairs = ph.sem("fc1"), ph.sem("pairs")
        s_idx, s_src, s_idle = ph.sem("idx"), [ph.sem(f"src{r}") for r in range(R)], ph.sem("idle")
        s_z, s_hid, s_w = ph.sem("z"), ph.sem("hid"), ph.sem("w")
        s_hot, s_hots, s_msg, s_sum, s_add = ph.sem("hot"), ph.sem("hots"), ph.sem("msg"), ph.sem("sum"), ph.sem("add")
        s_zero = ph.sem("zero")
        zb, wb, ab = net.bank[0:2], net.bank[2:4], net.bank[4:8]
        LOADS = {0: 2, 2: 4, 6: 2}
        fc2_of = (0, 2, 3, 1)

        def fresh(first, b, n):
            return first and b < n

        with ph.block() as block:
            @block.sync
            def _(sp):
                sp.dma_start(fc1[:, :], a["L3_gnn_fc_w1"][:, :]).then_inc(s_fc, 16)
                for k, of in enumerate(fc2_of):
                    sp.dma_start(fc2[:, k, :], a["L3_gnn_fc_w2"][:, of * MUL:(of + 1) * MUL]).then_inc(s_fc, 16)
                sp.wait_ge(s_fc1, 5)
                for k in range(3):
                    for m in range(3):
                        row = 8 * (3 * k + m)
                        sp.dma_start(fc1_pairs[row:row + 8, :], fc1_parts[k][:, :]).then_inc(s_pairs, 16)

                first_edges = [None] * R

                def body(w, b, first):
                    if b == 0:
                        first_edges[:] = load_values(sp, net.win_tab[0:1, ds(WINDOWS + w, R)], E)
                    e0 = first_edges[b]
                    if not fresh(first, b, R):
                        sp.wait_ge(s_sum, w - R + 1)
                    sp.dma_start(attr[b][:, :], net.attr[ds(e0, WIN), :]).then_inc(s_attr[b], 16)
                    of = net.scal_parts.rearrange("m k n -> (m k) n")[:, ds(e0, WIN)]
                    sp.dma_start(scal[b][:, :], of.unsqueeze(0).broadcast_to([3, PAIRS // 3, WIN])).then_inc(s_attr[b], 16)
                for_tiles(sp, WINDOWS, body, ring=R)

            @block.gpsimd
            def _(pool):
                def body(w, b, first):
                    if b % 2 == 0:
                        pool.wait_ge(s_idx, w + 2)
                        carry_wait(pool, s_idle)
                    pool.indirect_dma_start(
                        out=src[b][:, :], out_offset=None, in_=table[:, :],
                        in_offset=bass.IndirectOffsetOnAxis(ap=idx[b // 2][:, b % 2:b % 2 + 1], axis=0)).then_inc(s_src[b], 16)
                for_tiles(pool, WINDOWS, body, ring=R)

            @block.scalar
            def _(act):
                def hidden(w, b, first):
                    act.wait_ge(s_z, w + 1)
                    if not fresh(first, b, 2):
                        act.wait_ge(s_w, w - 1)
                    act.activation(hid[b % 2][:, :], zb[b % 2][0:MUL, 0:WIN], ACT.Silu, scale=8 ** -0.5).then_inc(s_hid, 1)

                def body(w, b, first):
                    act.wait_ge(s_hot, w + 1)
                    act.wait_ge(s_attr[b], 4 * (w - b) + 32)
                    if not fresh(first, b, 2):
                        act.wait_ge(s_sum, w - 1)
                    for c in range(4):
                        ins = act.activation(hots[b % 2][:, c, :], hot[b][:, :], ACT.Copy, scale=attr[b][:, c:c + 1])
                    ins.then_inc(s_hots, 1)
                for_tiles(act, WINDOWS, body, ahead=((1, hidden),), ring=R)

            @block.tensor
            def _(pe):
                def first_product(w, b, first):
                    pe.wait_ge(s_attr[b], 4 * (w - b) + 32)
                    if not fresh(first, b, 2):
                        pe.wait_ge(s_hid, w - 1)
                    pe.matmul(zb[b % 2][0:MUL, 0:WIN], fc1_pairs[:, :], scal[b][:, :], start=True, stop=True).then_inc(s_z, 1)

                def second_product(w, b, first):
                    pe.wait_ge(s_hid, w + 1)
                    if not fresh(first, b, 2):
                        pe.wait_ge(s_msg, w - 1)
                    pe.matmul(wb[b % 2][:, 0:4 * MUL], hid[b % 2][:, :], fc2[:, :, :].rearrange("p b n -> p (b n)"),
                              start=True, stop=True).then_inc(s_w, 1)

                def body(w, b, first):
                    if not fresh(first, b, 4):
                        pe.wait_ge(s_add, w - 3)
                    pe.wait_ge(s_msg, w + 1)
                    pe.wait_ge(s_hots, w + 1)
                    m, h = msg[b % 2], hots[b % 2]
                    out = ab[b % 4][0:P, :].rearrange("p (b n) -> p b n", n=MUL)
                    pe.matmul(out[:, 0:4, :], h[:, 0, :], m[:, 0:4, :], start=True, stop=False, skip_group_check=True)
                    for c in range(3):
                        mm = pe.matmul(out[:, 4 + c:8:3 - c, :], h[:, 1 + c, :], m[:, 4:6 + c:1 + c, :],
                                       start=False, stop=(c == 2), skip_group_check=True)
                    mm.then_inc(s_sum, 1)
                pe.wait_ge(s_fc, 16 * 5)
                pe.wait_ge(s_fcs, 2)
                pe.wait_ge(s_pairs, 16 * 9)
                for_tiles(pe, WINDOWS, body, ahead=((2, first_product), (1, second_product)), ring=R)

            @block.vector
            def _(dve):
                dve.memset(net.acc[:, :], 0.0).then_inc(s_zero, 1)
                dve.wait_ge(s_fc, 16 * 5)
                step = Chain(dve, s_fc1)
                for k in range(3):
                    step(dve.tensor_copy(fc1_parts[k][:, :], fc1[:, :]))
                    if k < 2:
                        step(dve.tensor_tensor(fc1[:, :], fc1[:, :], fc1_parts[k][:, :], ALU.subtract))
                dve.tensor_scalar(fc2[:, 0:3, :], fc2[:, 0:3, :], 1.679 * MUL ** -0.5, None, ALU.mult).then_inc(s_fcs, 1)
                dve.tensor_scalar(fc2[:, 3, :], fc2[:, 3, :], 1.679 * MUL ** -0.5 * 3 ** -0.5, None, ALU.mult).then_inc(s_fcs, 1)

                def stage(w, b, first):
                    if b % 2 == 0:
                        if not fresh(first, b, R):
                            dve.wait_ge(s_sum, w - R + 2)
                        dve.tensor_copy(idx[b // 2][:, :].bitcast(F32),
                                        net.src_w[:, ds(w, 2)].bitcast(F32)).then_inc(s_idx, 2)
                    dve.tensor_scalar(hot[b][:, :], net.iota_i[:, 0:P], net.dst_w[:, ds(w, 1)], None,
                                      ALU.is_equal).then_inc(s_hot, 1)

                tiles = {}

                def add(w, tile, bank, very_first):
                    dve.wait_ge(s_sum, w + 1)
                    if not very_first:
                        dve.wait_ge(s_add, w)
                    row = node_row(acc, tile)
                    dve.tensor_tensor(row, row, bank[0:P, :], ALU.add).then_inc(s_add, 1)

                def body(w, b, first):
                    dve.wait_ge(s_src[b], 2 * (w - b) + 16)
                    dve.wait_ge(s_w, w + 1)
                    if not fresh(first, b, 2):
                        dve.wait_ge(s_sum, w - 1)
                    m = msg[b % 2][:, :, :]
                    wv = wb[b % 2][:, 0:4 * MUL].rearrange("p (b n) -> p b n", n=MUL)
                    sv = src[b][:, :].rearrange("p (b n) -> p b n", n=MUL)
                    dve.tensor_tensor(m[:, 0:8:4, :], wv[:, 0:2, :], sv[:, 0:1, :].broadcast_to([Q, 2, MUL]), ALU.mult)
                    quad = m.rearrange("p (g k) n -> p g k n", g=2)[:, :, 1:4, :]
                    dve.tensor_tensor(quad, bc(wv[:, 2:4, :], 2, [Q, 2, 3, MUL]),
                                      bc(sv[:, 1:4, :], 1, [Q, 2, 3, MUL]), ALU.mult).then_inc(s_msg, 1)
                    if not fresh(first, b, 2):
                        if b in LOADS:
                            loaded = load_values(dve, net.win_tab[0:1, ds(w - 2, LOADS[b])], T - 1)
                            tiles.update({b + k: tile for k, tile in enumerate(loaded)})
                        add(w - 2, tiles[b], ab[(b - 2) % 4], fresh(first, b, 3))
                dve.wait_ge(s_zero, 1)
                for_tiles(dve, WINDOWS, body, ahead=((4, stage),), ring=R)
                last = load_values(dve, net.win_tab[0:1, WINDOWS - 2:WINDOWS], T - 1)
                for k, w in enumerate((WINDOWS - 2, WINDOWS - 1)):
                    add(w, last[k], ab[w % 4], False)


def gnn_kernel(nc, a, out):
    with ExitStack() as ctx:
        net = Net(nc, ctx, a)
        table0, table1 = dram(nc, "table0", [N, D]), dram(nc, "table1", [N, D])
        table2, table3 = dram(nc, "table2", [N, D // 2]), dram(nc, "table3", [N, D])
        buf, outb = dram(nc, "token_rows", [TOK_ROWS, D]), dram(nc, "expert_rows", [TOK_ROWS, D])
        prepare(net, buf)
        group_edges(net)
        load_windows(net)
        acc256, acc128, acc512 = net.acc_view(D), net.acc_view(D // 2), net.acc_view(2 * D)

        def relu_norm(act, t, rows):
            return act.activation(rows, node_row(net.x, t), ACT.Relu, bias=net.nmr[:, ds(t, 1)],
                                  scale=net.rstd[:, ds(t, 1)])

        def four_products(pe, cols, po):
            for c in range(4):
                mm = pe.matmul(po[0:P, 0:D], cols[:, c, :], net.got["w"][:, c, :], start=(c == 0), stop=(c == 3))
            return mm

        def factors0(step, dve, act, s1, s2):
            if act:
                act.activation(net.rb[:, :], net.deg_out[:, :], ACT.Sqrt).then_inc(s1, 1)
            else:
                dve.wait_ge(s1, 1)
                step(dve.reciprocal(net.rb[:, :], net.rb[:, :]))
                step(dve.tensor_tensor(net.rc[:, :], net.rb[:, :], net.nmr[:, :], ALU.mult))
                step(dve.tensor_tensor(net.ra[:, :], net.rb[:, :], net.rstd[:, :], ALU.mult))
        layer_stats(net, "ln0", factors0)
        write_table(net, "tab0", table0, net.ra, net.rc)

        aggregate(net, "agg0", table0, D, degrees=True)
        root_of_degree(net)

        acc257 = net.acc_view(D + 1)

        def stage0(act, t, rows, of=acc257):
            act.activation(rows[:, 0:D], node_row(of, t)[:, 0:D], ACT.Copy, scale=net.rb[:, ds(t, 1)])
            return relu_norm(act, t, rows[:, D:2 * D])

        def finish0(dve, step, t, row, po):
            row = node_row(acc256, t)
            step(dve.tensor_tensor(row, po[0:P, 0:D], net.got["b1"][:, :], ALU.add))
            return dve.tensor_tensor(row, row, net.got["b2"][:, :], ALU.add)
        node_stage(net, "node0", 4, loader(
            ("w", [Q, 4, D], lambda w: [(w[:, 0:2, :], in_chunks(a["L0_gnn_W_gc"])), (w[:, 2:4, :], in_chunks(a["L0_gnn_W_res"]))]),
            ("b1", [P, D], lambda w: [(w[:, :], row_of(a["L0_gnn_b_gc"]))]),
            ("b2", [P, D], lambda w: [(w[:, :], row_of(a["L0_gnn_b_res"]))])), stage0, four_products, finish0, steps=1)
        experts(net, buf, outb, None)
        batch_norm(net)

        def factors1(step, dve, act, s1, s2):
            if dve:
                step(dve.tensor_scalar(net.rb[:, :], net.deg_in[:, :], 1.0, None, ALU.max))
                step(dve.reciprocal(net.rb[:, :], net.rb[:, :]))
        layer_stats(net, "ln1", factors1)
        write_table(net, "tab1", table1, net.rstd, net.nmr)
        aggregate(net, "agg1", table1, D, split=True)

        def finish1(dve, step, t, row, po):
            row = node_row(net.x, t)
            step(dve.tensor_tensor(row, po[0:P, 0:D], row, ALU.add))
            return dve.tensor_tensor(row, row, net.got["b"][:, :], ALU.add)
        node_stage(net, "node1", 4, loader(
            ("w", [Q, 4, D], lambda w: [(w[:, 0:2, :], in_chunks(a["L1_w_neigh_t"])), (w[:, 2:4, :], in_chunks(a["L1_w_self_t"]))]),
            ("b", [P, D], lambda w: [(w[:, :], row_of(a["L1_gnn_b_self"]))])), lambda act, t, rows: stage0(act, t, rows, acc256), four_products, finish1, steps=1)

        half = D // 2
        own = net.acc[:, T * half:2 * T * half].rearrange("p (t d) -> p t d", d=half)

        def factors2(step, dve, act, s1, s2):
            if act:
                act.wait_ge(s2, 1)
                act.activation(net.ra[:, :], net.ra[:, :], ACT.Sqrt).then_inc(s1, 1)
            else:
                dve.tensor_scalar(net.ra[:, :], net.deg_in[:, :], 1.0, None, ALU.add).then_inc(s2, 1)
                dve.wait_ge(s1, 1)
                step(dve.reciprocal(net.ra[:, :], net.ra[:, :]))
        layer_stats(net, "ln2", factors2)
        with ExitStack() as c2:
            out2 = [c2.enter_context(nc.sbuf_tensor(f"out2_{b}", [P, STORE, half], F32)) for b in (0, 1)]

            def stage2(act, t, rows):
                return relu_norm(act, t, rows[:, :])

            def products2(pe, cols, po):
                for c in (0, 1):
                    mm = pe.matmul(po[0:P, 0:half], cols[:, c, :], net.got["w"][:, c, :], start=(c == 0), stop=(c == 1))
                return mm

            def finish2(dve, step, t, row, po):
                dve.tensor_scalar(node_row(own, t), po[0:P, 0:half], net.ra[:, ds(t, 1)], None, ALU.mult)
                return dve.tensor_scalar(row, po[0:P, 0:half], net.ra[:, ds(t, 1)], None, ALU.mult)

            node_stage(net, "node2", 2, loader(
                ("w", [Q, 2, half], lambda w: [(w[:, :, :], in_chunks(a["L2_gnn_W_conv"]))])),
                stage2, products2, finish2, steps=0, store=(table2, out2))
        aggregate(net, "agg2", table2, half)
        with ExitStack() as c2:
            b_conv = c2.enter_context(nc.sbuf_tensor("b_conv", [P, half], F32))
            scale_and_bias(net, acc128, own, b_conv)

        def stage2b(act, t, rows):
            return act.activation(rows[:, :], node_row(acc128, t), ACT.Copy)

        def products2b(pe, cols, po):
            return pe.matmul(po[0:P, 0:D], cols[:, 0, :], net.got["w"][:, 0, :], start=True, stop=True)
        node_stage(net, "node2b", 1, loader(
            ("w", [Q, 1, D], lambda w: [(w[:, 0, :], a["L2_gnn_W_lin"][:, :])]),
            ("b", [P, D], lambda w: [(w[:, :], row_of(a["L2_gnn_b_lin"]))])), stage2b, products2b, finish1, steps=1)

        inv_mul = MUL ** -0.5
        c_s, c_x = float(np.sin(np.pi / 8)), float(np.cos(np.pi / 8))

        def factors3(step, dve, act, s1, s2):
            if dve:
                step(dve.tensor_scalar(net.ra[:, :], net.rc[:, :], inv_mul, None, ALU.mult))
                step(dve.tensor_scalar(net.rb[:, :], net.rc[:, :], c_s * inv_mul, None, ALU.mult))
                step(dve.tensor_scalar(net.rc[:, :], net.rc[:, :], c_x * (2 * MUL) ** -0.5 * 20.0 ** -0.5, None, ALU.mult))
        load_node_attr(net)
        layer_stats(net, "ln3", factors3)
        parts = "p (u c) -> p c u"
        with ExitStack() as c3:
            out3 = [c3.enter_context(nc.sbuf_tensor(f"out3_{b}", [P, STORE, D], F32)) for b in (0, 1)]

            def stage3(act, t, rows):
                relu_norm3 = dict(bias=net.nmr[:, ds(t, 1)], scale=net.rstd[:, ds(t, 1)])
                xr = node_row(net.x, t)
                act.activation(rows[:, 0:MUL], xr[:, 0:MUL], ACT.Relu, **relu_norm3)
                return act.activation(rows[:, MUL:D].rearrange("p (c u) -> p c u", c=3),
                                      xr[:, MUL:D].rearrange(parts, c=3), ACT.Relu, **relu_norm3)

            def products3(pe, cols, po):
                w = net.got["w"]
                for c in (0, 1):
                    pe.matmul(po[0:P, c * Q:(c + 1) * Q], cols[:, c, :], w[:, c, :], start=(c == 0), stop=True,
                              skip_group_check=True)
                    mm = pe.matmul(po[0:P, D + c * Q:D + (c + 1) * Q], cols[:, c, :], w[:, 2 + c, :], start=False,
                                   stop=True, skip_group_check=True)
                return mm

            def finish3(dve, step, t, row, po):
                dve.tensor_scalar(row, po[0:P, 0:D], net.ra[:, ds(t, 1)], None, ALU.mult)
                xr = node_row(net.x, t)
                dve.scalar_tensor_tensor(xr[:, 0:MUL], po[0:P, D:D + MUL], net.rb[:, ds(t, 1)], xr[:, 0:MUL],
                                         ALU.mult, ALU.add)
                x1 = xr[:, MUL:D].rearrange(parts, c=3)
                return dve.scalar_tensor_tensor(x1, po[0:P, D + MUL:2 * D].rearrange("p (c u) -> p c u", c=3),
                                                net.rb[:, ds(t, 1)], x1, ALU.mult, ALU.add)

            node_stage(net, "node3", 2, loader(("w", [Q, 4, Q], lambda w: [
                (w[:, k, :], a["L3_w_pairs"][k]) for k in range(4)])), stage3, products3, finish3, steps=0, store=(table3, out3))
        tensor_product_edges(net, table3)

        with ExitStack() as c4:
            out4 = [c4.enter_context(nc.sbuf_tensor(f"out4_{b}", [P, STORE, D], F32)) for b in (0, 1)]

            def stage4(act, t, rows):
                of = node_row(acc512, t).rearrange("p (b u) -> p b u", u=MUL)
                to = rows[:, :].rearrange("p (b u) -> p b u", u=MUL)
                act.activation(to[:, 0, :], of[:, 0, :], ACT.Copy)
                act.activation(to[:, 1, :], of[:, 7, :], ACT.Copy)
                act.activation(to[:, 2:8:2, :], of[:, 4:7, :], ACT.Copy)
                return act.activation(to[:, 3:8:2, :], of[:, 1:4, :], ACT.Copy)

            def products4(pe, cols, po):
                w = net.got["w"]
                for c in range(4):
                    mm = pe.matmul(po[0:P, c * MUL:(c + 1) * MUL], cols[:, c, :], w[:, min(c, 1), :], start=(c == 0),
                                   stop=True, skip_group_check=True)
                return mm

            def finish4(dve, step, t, row, po):
                xr = node_row(net.x, t)
                sc = net.rc[:, ds(t, 1)]
                dve.scalar_tensor_tensor(row[:, 0:MUL], po[0:P, 0:MUL], sc, xr[:, 0:MUL], ALU.mult, ALU.add)
                return dve.scalar_tensor_tensor(row[:, MUL:D].rearrange(parts, c=3),
                                                po[0:P, MUL:D].rearrange("p (c u) -> p c u", c=3), sc,
                                                xr[:, MUL:D].rearrange(parts, c=3), ALU.mult, ALU.add)

            node_stage(net, "node4", 4, loader(("w", [Q, 2, MUL], lambda w: [
                (w[MUL * h:MUL * (h + 1), k, :], a["L3_gnn_lin2_w" + n][:, :])
                for k, h, n in ((0, 0, "00"), (0, 1, "01"), (1, 0, "10"), (1, 1, "11"))])),
                stage4, products4, finish4, steps=0, store=(out, out4))


def root_of_degree(net):
    degree = net.acc_view(D + 1)[:, :, D]
    with net.phase("root") as ph:
        s_clip, s_root, s_step = ph.sem("clip"), ph.sem("root"), ph.sem("step")
        with ph.block() as block:
            @block.vector
            def _(dve):
                dve.tensor_copy(net.deg_in[:, :], degree)
                dve.tensor_scalar(net.rb[:, :], degree, 1.0, None, ALU.max).then_inc(s_clip, 1)
                dve.wait_ge(s_root, 1)
                dve.reciprocal(net.rb[:, :], net.rb[:, :]).then_inc(s_step, 1)

            @block.scalar
            def _(act):
                act.wait_ge(s_clip, 1)
                act.activation(net.rb[:, :], net.rb[:, :], ACT.Sqrt).then_inc(s_root, 1)


def scale_and_bias(net, acc, own, b_conv):
    half = D // 2
    with net.phase("gcn") as ph:
        s_w, s_step = ph.sem("w"), ph.sem("step")
        with ph.block() as block:
            @block.sync
            def _(sp):
                sp.dma_start(b_conv[:, :], row_of(net.a["L2_gnn_b_conv"])).then_inc(s_w, 16)

            @block.vector
            def _(dve):
                step = Chain(dve, s_step)
                wide = [P, T, half]
                step(dve.tensor_tensor(acc, acc, own, ALU.add))
                step(dve.tensor_tensor(acc, acc, bc(net.ra[:, :], 2, wide), ALU.mult))
                dve.wait_ge(s_w, 16)
                step(dve.tensor_tensor(acc, acc, bc(b_conv[:, :], 1, wide), ALU.add))


def load_node_attr(net):
    with net.phase("attr") as ph:
        s_w, s_t = ph.sem("w"), ph.sem("t")
        rows = ph.sb("rows", [T, P])
        with ph.block() as block:
            @block.sync
            def _(sp):
                sp.dma_start(rows[:, :], net.a["node_vec1"].rearrange("(t p) k -> t (p k)", p=P)).then_inc(s_w, 16)

            @block.tensor
            def _(pe):
                pe.wait_ge(s_w, 16)
                pe.transpose(net.bank[0][0:P, 0:T], rows[:, :], net.ident[0:T, 0:T]).then_inc(s_t, 1)

            @block.vector
            def _(dve):
                dve.wait_ge(s_t, 1)
                dve.tensor_copy(net.rc[:, :], net.bank[0][0:P, 0:T])


_OUT_SHAPE = (N, D)


def kernel(**inputs):
    import concourse.bacc as _bacc
    from concourse.bass_utils import run_bass_kernel_spmd as _run

    src, dst = np.asarray(inputs["src"]), np.asarray(inputs["dst"])
    arrays = {}
    edge_index = np.full((EPAD, 2), -1, np.int32)
    edge_index[:E, 0], edge_index[:E, 1] = src, dst
    edge_index[E:, 0] = 0
    arrays["edge_index"] = edge_index
    arrays["edge_attr"] = np.zeros((EPAD, 4), np.float32)
    arrays["edge_attr"][:E] = inputs["edge_attr_4"]
    arrays["edge_scal_t"] = np.zeros((8, EPAD), np.float32)
    arrays["edge_scal_t"][:, :E] = np.asarray(inputs["edge_attr_8"]).T
    arrays["L1_w_neigh_t"] = np.ascontiguousarray(np.asarray(inputs["L1_gnn_w_neigh"]).T)
    arrays["L1_w_self_t"] = np.ascontiguousarray(np.asarray(inputs["L1_gnn_w_self"]).T)
    arrays["L3_w_pairs"] = np.zeros((4, 2 * MUL, 2 * MUL), np.float32)
    for k, (top, low) in enumerate((("lin1_w0", "lin1_w1"), ("lin1_w1", "lin1_w1"), ("sc_w0", "sc_w1"), ("sc_w1", "sc_w1"))):
        arrays["L3_w_pairs"][k, :MUL, :MUL] = inputs["L3_gnn_" + top]
        arrays["L3_w_pairs"][k, MUL:, MUL:] = inputs["L3_gnn_" + low]
    laid_out = ("edge_attr_4", "L1_gnn_w_neigh", "L1_gnn_w_self", "L3_gnn_sc_w0", "L3_gnn_sc_w1",
                "L3_gnn_lin1_w0", "L3_gnn_lin1_w1")
    for name in inputs:
        if name not in laid_out:
            arrays[name] = np.ascontiguousarray(inputs[name])
    nc = _bacc.Bacc("TRN2", target_bir_lowering=False, num_devices=1)
    a = {name: nc.dram_tensor(f"in_{name}_dram", v.shape, mybir.dt.from_np(v.dtype), kind="ExternalInput").ap()
         for name, v in arrays.items()}
    out = nc.dram_tensor("out_0_dram", _OUT_SHAPE, F32, kind="ExternalOutput").ap()
    gnn_kernel(nc, a, out)
    r = _run(nc, [{f"in_{k}_dram": v for k, v in arrays.items()}], core_ids=[0])
    return r.results[0]["out_0_dram"]
```

```python
from contextlib import ExitStack

import numpy as np

import concourse.bass as bass
from concourse import mybir

F32 = mybir.dt.float32
I32 = mybir.dt.int32
U32 = mybir.dt.uint32
BF16 = mybir.dt.bfloat16
ALU = mybir.AluOpType
ACT = mybir.ActivationFunctionType
AX_X = mybir.AxisListType.X
ds = bass.ds

N = 6250
E = 100000
D = 256
P = 125
T = N // P
Q = 128
WIN = 128
WPI = 16
WINDOWS = -(-((E + T * (WIN - 1)) // WIN) // WPI) * WPI
STEPS = WINDOWS // WPI
SPLIT = -(-8 * (E + WIN) // (Q * STEPS))
EPAD = SPLIT * STEPS * Q // 8
GROUPS_W = 8
WG = WINDOWS // GROUPS_W
EC = E // P
X_EXP = 64
HID = 512
CAP = 1024
MT = -(-((2 * N + X_EXP * (Q - 1)) // Q) // 6) * 6
TOK_ROWS = MT * Q
MUL = 64
LN_EPS = 1e-5
BN_EPS = 1e-5
assert N == P * T and E == P * EC and T % 2 == 0 and WINDOWS == WG * GROUPS_W and WG <= Q
assert EPAD >= E + WIN and 8 * EPAD == SPLIT * STEPS * Q


class Chain:

    def __init__(self, eng, sem, base=0):
        self.eng, self.sem, self.base, self.n = eng, sem, base, 0

    def __call__(self, ins):
        self.n += 1
        ins.then_inc(self.sem, 1)
        self.eng.wait_ge(self.sem, self.base + self.n)


def for_tiles(eng, count, body, ahead=(), ring=2, turns=False):
    def call(f, t, b, turn):
        f(t, b, turn if turns else is_zero(turn))

    def step(t, b, turn, last_b):
        for lead, f in ahead:
            if last_b is None or last_b + lead < ring:
                call(f, t + lead, (b + lead) % ring, turn + (b + lead) // ring)
        call(body, t, b, turn)

    for lead in sorted({k for k, _ in ahead}, reverse=True):
        for k, f in ahead:
            if k == lead:
                for t in range(k):
                    call(f, t, t % ring, 0)
    for t in range(ring):
        step(t, t, 0, None)
    if count > 2 * ring:
        with eng.Fori(1, count // ring - 1) as i:
            for b in range(ring):
                step(ring * i + b, b, i, None)
    for b in range(ring):
        step(count - ring + b, b, count // ring - 1, b)


def load_values(eng, row, most):
    return eng.bass.values_load_multi_w_load_instructions(row, engines=[eng.engine], min_val=0, max_val=most)[1]


def is_zero(turn):
    return isinstance(turn, int) and turn == 0


def carry_wait(eng, sem):
    eng.sem_inc(sem, 1)


def dram(nc, name, shape, dt=F32):
    return nc.dram_tensor(name, shape, dt, kind="Internal").ap()


def bc(ap, axis, shape):
    return ap.unsqueeze(axis).broadcast_to(shape)


class Net:

    def __init__(self, nc, ctx, a):
        self.nc, self.a = nc, a

        def sb(name, shape, dt=F32):
            return ctx.enter_context(nc.sbuf_tensor(name, shape, dt))

        self.x = sb("x_res", [P, T, D])
        self.acc_full = sb("acc", [Q, T * 2 * D])
        self.acc = self.acc_full[0:P, :]
        self.src_w = sb("src_w", [Q, WINDOWS], I32)
        self.dst_w = sb("dst_w", [Q, WINDOWS])
        self.win_tab = sb("win_tab", [1, 2 * WINDOWS], I32)
        self.ident = sb("ident", [Q, Q])
        self.iota_i = sb("iota_i", [Q, MT])
        self.first_edge = sb("first_edge", [WG, GROUPS_W], I32)
        self.base_col = sb("base_col", [WG, GROUPS_W])
        self.below = sb("below", [P, T])
        self.flag = sb("flag", [1, 1], I32)
        self.edges = dram(nc, "edges", [EPAD, 2], I32)
        self.attr = dram(nc, "attr", [EPAD, 4])
        self.scal_t = dram(nc, "scal_t", [8, EPAD])
        self.b2_parts = dram(nc, "b2_parts", [3, X_EXP, D], BF16)
        self.scal_parts = dram(nc, "scal_parts", [3, 8, EPAD], BF16)
        self.ones = sb("ones", [Q, Q])
        self.tri = sb("tri", [Q, Q])
        self.deg_out = sb("deg_out", [P, T])
        self.deg_in = sb("deg_in", [P, T])
        self.ra = sb("ra", [P, T])
        self.rb = sb("rb", [P, T])
        self.rc = sb("rc", [P, T])
        self.stats = sb("stats", [P, T, 6])
        self.mv = sb("mv", [P, T, 2])
        self.rstd = sb("rstd", [P, T])
        self.nmr = sb("nmr", [P, T])
        self.eps = sb("eps", [Q, 1])
        self.bank = [ctx.enter_context(nc.psum_tensor(f"bank{i}", [Q, 512], F32)) for i in range(8)]
        self.used = []

    def acc_view(self, width):
        return self.acc[:, 0:T * width].rearrange("p (t d) -> p t d", d=width)

    def phase(self, name):
        return Phase(self, name)


class Phase:

    def __init__(self, net, name):
        self.net, self.nc, self.name = net, net.nc, name
        self.ctx = ExitStack()
        if len(net.used) > 120:
            self.nc.clear_and_free_semaphores(net.used)
            self.nc.all_engine_barrier()
            net.used = []

    def __enter__(self):
        return self

    def __exit__(self, *e):
        return self.ctx.__exit__(*e)

    def sb(self, name, shape, dt=F32):
        return self.ctx.enter_context(self.nc.sbuf_tensor(f"{self.name}_{name}", shape, dt))

    def sem(self, name):
        sem = self.nc.alloc_semaphore(f"{self.name}_{name}")
        self.net.used.append(sem)
        return sem

    def block(self):
        return self.nc.Block()



def ceil_div(step, dve, out, x, divisor, whole, over):
    step(dve.tensor_scalar(out, x, 1.0 / divisor, None, ALU.mult))
    step(dve.tensor_copy(whole, out))
    step(dve.tensor_copy(over, whole))
    step(dve.tensor_tensor(out, out, over, ALU.subtract))
    step(dve.tensor_scalar(out, out, 0.0, None, ALU.is_gt))
    step(dve.tensor_tensor(out, out, over, ALU.add))


def split_parts(step, dve, parts, whole):
    for k in range(3):
        step(dve.tensor_copy(parts[k], whole))
        if k < 2:
            step(dve.tensor_tensor(whole, whole, parts[k], ALU.subtract))


def split_node(step, dve, ids, tile, lane, whole):
    step(dve.tensor_copy(lane, ids))
    step(dve.tensor_scalar(whole, lane, 1.0 / P, None, ALU.mult))
    step(dve.tensor_copy(tile, whole))
    step(dve.scalar_tensor_tensor(lane, tile, -float(P), lane, ALU.mult, ALU.add))
    low = whole.bitcast(F32)
    step(dve.tensor_scalar(low, lane, 0.0, None, ALU.is_lt))
    step(dve.tensor_tensor(tile, tile, low, ALU.subtract))
    step(dve.scalar_tensor_tensor(lane, low, float(P), lane, ALU.mult, ALU.add))
    step(dve.tensor_scalar(low, lane, float(P), None, ALU.is_ge))
    step(dve.tensor_tensor(tile, tile, low, ALU.add))
    step(dve.scalar_tensor_tensor(lane, low, -float(P), lane, ALU.mult, ALU.add))


def prepare(net, buf):
    a = net.a
    COLS = 8
    with net.phase("prep") as ph:
        base = net.acc
        ids = [base[:, k * EC:(k + 1) * EC].bitcast(I32) for k in (0, 1)]
        next_dst = base[:, 2 * EC:3 * EC].bitcast(I32)
        tiles, lanes = base[:, 3 * EC:4 * EC], base[:, 4 * EC:5 * EC]
        whole = base[:, 5 * EC:6 * EC].bitcast(I32)
        dst_f, next_f = base[:, 6 * EC:7 * EC], base[:, 7 * EC:8 * EC]
        junk = base[:, 8 * EC:9 * EC]
        SCRATCH = 16
        scratch = [base[:, (9 + k) * EC:(10 + k) * EC] for k in range(SCRATCH)]
        tiles_bf, lanes_bf = ph.sb("tiles_bf", [P, EC], BF16), ph.sb("lanes_bf", [P, EC], BF16)
        iota_bf = ph.sb("iota_bf", [P, P], BF16)
        lane_hot = [ph.sb(f"lane_hot{k}", [P, COLS, P], BF16) for k in (0, 1)]
        tile_hot = [ph.sb(f"tile_hot{k}", [P, COLS, T], BF16) for k in (0, 1)]
        zero_bf = ph.sb("zero_bf", [P, P], BF16)
        CLEAR = 18
        zero, s_clear = ph.sb("zero", [Q, CLEAR * D]), ph.sem("clear")
        bounds = ph.sb("bounds", [P, T])
        b2, s_b2, s_b2_split = ph.sb("b2", [X_EXP, D]), ph.sem("b2"), ph.sem("b2_split")
        b2_parts = [ph.sb(f"b2_part{k}", [X_EXP, D], BF16) for k in range(3)]
        below, count = net.below, ph.sb("count", [P, T])
        bad = ph.sb("bad", [P, 1])
        col = ph.sb("col", [T, 8])
        coli = ph.sb("coli", [T, 1], I32)
        past = ph.sb("past", [T, WINDOWS])
        edge_row = base[0:1, 9 * EC:9 * EC + WINDOWS]
        first_col = ph.sb("first_col", [WG, GROUPS_W])
        number = ph.sb("number", [WG, GROUPS_W])
        iota_w = ph.sb("iota_w", [T, WINDOWS])
        s_const, s_x, s_ids = ph.sem("const"), ph.sem("x"), [ph.sem("src"), ph.sem("dst")]
        s_step, s_hot, s_used, s_hist = ph.sem("step"), ph.sem("hot"), ph.sem("used"), ph.sem("hist")
        s_below, s_cnt, s_pairs, s_end = ph.sem("below"), ph.sem("cnt"), ph.sem("pairs"), ph.sem("end")
        s_edge = ph.sem("edge")
        s_past, s_sum, s_copies, s_zero = ph.sem("past"), ph.sem("sum"), ph.sem("copies"), ph.sem("zero")
        hist, tile_h, first_h = net.bank[0], net.bank[1:3], net.bank[3:5]
        small, by_window = net.bank[5], net.bank[6]
        HALF = WINDOWS // 2

        with ph.block() as block:
            @block.gpsimd
            def _(pool):
                pool.memset(net.ones[:, :], 1.0).then_inc(s_const, 1)
                pool.memset(net.eps[:, :], LN_EPS).then_inc(s_const, 1)
                pool.memset(zero[:, :], 0.0).then_inc(s_zero, 1)
                pool.iota(iota_w[:, :], [[1, WINDOWS]], base=0, channel_multiplier=0,
                          allow_small_or_imprecise_dtypes=True).then_inc(s_const, 1)
                pool.iota(net.iota_i[:, :], [[1, MT]], base=0, channel_multiplier=0,
                          allow_small_or_imprecise_dtypes=True).then_inc(s_const, 1)
                pool.iota(number[:, :], [[WIN * WG, GROUPS_W]], base=0, channel_multiplier=WIN,
                          allow_small_or_imprecise_dtypes=True).then_inc(s_const, 1)
                pool.wait_ge(s_const, 5)
                pool.affine_select(out=net.ident[:, :], in_=net.ones[:, :], compare_op=ALU.is_equal, fill=0.0,
                                   base=0, pattern=[[-1, Q]], channel_multiplier=1).then_inc(s_const, 1)
                pool.affine_select(out=net.tri[:, :], in_=net.ones[:, :], compare_op=ALU.is_ge, fill=0.0,
                                   base=-1, pattern=[[1, Q]], channel_multiplier=-1).then_inc(s_const, 1)

            @block.sync
            def _(sp):
                dst, tail = a["dst"], (P - 1) * EC
                sp.dma_start(ids[1], dst.rearrange("(p c) -> p c", c=EC)).then_inc(s_ids[1], 16)
                sp.dma_start(next_dst[0:P - 1, :],
                             dst[1:tail + 1].rearrange("(p c) -> p c", c=EC)).then_inc(s_ids[1], 16)
                sp.dma_start(next_dst[P - 1:P, 0:EC - 1], dst[tail + 1:E].unsqueeze(0)).then_inc(s_ids[1], 16)
                sp.dma_start(next_dst[P - 1:P, EC - 1:EC], dst[E - 1:E].unsqueeze(0)).then_inc(s_ids[1], 16)
                sp.dma_start(ids[0], a["src"].rearrange("(p c) -> p c", c=EC)).then_inc(s_ids[0], 16)
                sp.dma_start(net.x[:, :, :], a["x"].rearrange("(t p) d -> p t d", p=P)).then_inc(s_x, 16)
                sp.dma_start(b2[:, :], a["L0_gnn_b2"][:, :]).then_inc(s_b2, 16)
                sp.wait_ge(s_zero, 2)
                for g in range(MT // CLEAR):
                    sp.dma_start(buf[CLEAR * Q * g:CLEAR * Q * (g + 1), :].rearrange("(p r) d -> p (r d)", p=Q),
                                 zero[:, :]).then_inc(s_clear, 16)
                sp.wait_ge(s_b2_split, 5)
                for k in range(3):
                    sp.dma_start(net.b2_parts[k], b2_parts[k][:, :]).then_inc(s_clear, 16)
                sp.wait_ge(s_clear, 16 * (MT // CLEAR) + 48)
                sp.wait_ge(s_x, 16)

            @block.scalar
            def _(act):
                act.wait_ge(s_ids[1], 64)
                for to, of, rows in ((net.edges, a["edge_index"], 208), (net.attr, a["edge_attr"], 208)):
                    act.dma_start(to.rearrange("(r n) k -> r (n k)", r=rows),
                                  of.rearrange("(r n) k -> r (n k)", r=rows)).then_inc(s_copies, 16)
                act.dma_start(net.scal_t.rearrange("k (r n) -> (k r) n", r=32),
                              a["edge_scal_t"].rearrange("k (r n) -> (k r) n", r=32)).then_inc(s_copies, 16)
                act.wait_ge(s_copies, 48)

            @block.vector
            def _(dve):
                step = Chain(dve, s_step)
                dve.memset(zero_bf[:, :], 0.0).then_inc(s_zero, 1)
                dve.wait_ge(s_const, 7)
                dve.tensor_copy(iota_bf[:, :], net.iota_i[0:P, 0:P])
                step(dve.tensor_scalar(bounds[:, :], net.iota_i[0:P, 0:T], float(P), float(P), ALU.mult, ALU.add))
                dve.wait_ge(s_ids[1], 64)
                dve.tensor_copy(next_f, next_dst)
                step(dve.tensor_copy(dst_f, ids[1]))
                for b in range(T):
                    if b >= SCRATCH:
                        dve.wait_ge(s_below, b - SCRATCH + 1)
                    dve.tensor_scalar(scratch[b % SCRATCH], dst_f, bounds[:, b:b + 1], 0.0, ALU.is_lt, ALU.add,
                                      accum_out=below[:, b:b + 1]).then_inc(s_below, 1)
                dve.wait_ge(s_below, T)
                dve.tensor_copy(count[:, 0:1], below[:, 0:1])
                dve.tensor_tensor(count[:, 1:T], below[:, 1:T], below[:, 0:T - 1], ALU.subtract)
                step(dve.tensor_tensor(junk, dst_f, next_f, ALU.is_gt))
                dve.tensor_reduce(bad[:, :], junk, AX_X, ALU.add).then_inc(s_below, 1)
                dve.wait_ge(s_cnt, 2)
                dve.tensor_copy(net.flag[:, :], small[0:1, 2:3])
                step(dve.tensor_copy(col[:, 0:1], small[0:T, 0:1]))
                ceil_div(step, dve, col[:, 1:2], col[:, 0:1], WIN, coli[:, :], col[:, 2:3])
                dve.scalar_tensor_tensor(col[:, 3:4], col[:, 1:2], -float(WIN), col[:, 0:1],
                                         ALU.mult, ALU.add).then_inc(s_pairs, 1)
                dve.wait_ge(s_end, 1)
                step(dve.tensor_tensor(col[:, 4:5], small[0:T, 1:2], col[:, 1:2], ALU.add))
                dve.tensor_scalar(past[:, :], iota_w[:, :], col[:, 4:5], None, ALU.is_ge).then_inc(s_past, 1)
                dve.wait_ge(s_sum, 4 + 2 * GROUPS_W)
                for k in (0, 1):
                    of = slice(k * HALF, (k + 1) * HALF)
                    dve.tensor_scalar(net.win_tab[0:1, of], tile_h[k][0:1, 0:HALF], float(T - 1), None, ALU.min)
                    dve.scalar_tensor_tensor(edge_row[:, of],
                                             iota_w[0:1, of], float(WIN), first_h[k][0:1, 0:HALF],
                                             ALU.mult, ALU.add).then_inc(s_edge, 1)
                dve.wait_ge(s_edge, 2)
                dve.tensor_scalar(net.win_tab[0:1, WINDOWS:2 * WINDOWS], edge_row[:, :], float(E), None, ALU.min)
                step(dve.tensor_tensor(first_col[:, :], number[:, :], by_window[0:WG, 0:GROUPS_W], ALU.add))
                dve.tensor_scalar(net.first_edge[:, :], first_col[:, :], float(E), None, ALU.min)
                dve.tensor_scalar(net.base_col[:, :], by_window[0:WG, GROUPS_W:2 * GROUPS_W], float(T - 1), float(P),
                                  ALU.min, ALU.mult)
                dve.wait_ge(s_b2, 16)
                split_parts(Chain(dve, s_b2_split), dve, [part[:, :] for part in b2_parts], b2[:, :])
                dve.wait_ge(s_ids[0], 16)
                split_node(step, dve, ids[0], tiles, lanes, whole)
                dve.tensor_copy(tiles_bf[:, :], tiles)
                step(dve.tensor_copy(lanes_bf[:, :], lanes))
                with dve.Fori(0, EC // COLS // 2) as g:
                    for k in (0, 1):
                        dve.wait_ge(s_used, 2 * g + 1 + k)
                        cols = ds(COLS * (2 * g + k), COLS)
                        dve.tensor_tensor(lane_hot[k][:, :, :], bc(lanes_bf[:, cols], 2, [P, COLS, P]),
                                          bc(iota_bf[:, :], 1, [P, COLS, P]), ALU.is_equal).then_inc(s_hot, 1)
                        dve.tensor_tensor(tile_hot[k][:, :, :], bc(tiles_bf[:, cols], 2, [P, COLS, T]),
                                          bc(iota_bf[:, 0:T], 1, [P, COLS, T]), ALU.is_equal).then_inc(s_hot, 1)
                dve.wait_ge(s_hist, 1)
                dve.tensor_scalar(net.deg_out[:, :], hist[0:P, 0:T], 1.0, None, ALU.max)

            @block.tensor
            def _(pe):
                pe.wait_ge(s_const, 7)
                pe.wait_ge(s_below, T + 1)
                pe.matmul(small[0:T, 0:1], count[:, :], net.ones[0:P, 0:1], start=True, stop=True).then_inc(s_cnt, 1)
                pe.matmul(small[0:1, 2:3], bad[:, :], net.ones[0:P, 0:1], start=True, stop=True).then_inc(s_cnt, 1)
                pe.wait_ge(s_pairs, 1)
                pe.matmul(small[0:T, 1:2], net.tri[0:T, 0:T], col[:, 1:2], start=True, stop=True).then_inc(s_end, 1)
                pe.wait_ge(s_past, 1)
                for k in (0, 1):
                    of = past[:, k * HALF:(k + 1) * HALF]
                    pe.matmul(tile_h[k][0:1, 0:HALF], net.ones[0:T, 0:1], of, start=True, stop=True).then_inc(s_sum, 1)
                    pe.matmul(first_h[k][0:1, 0:HALF], col[:, 3:4], of, start=True, stop=True).then_inc(s_sum, 1)
                for g in range(GROUPS_W):
                    of = past[:, WG * g:WG * (g + 1)]
                    pe.matmul(by_window[0:WG, g:g + 1], of, col[:, 3:4], start=True, stop=True).then_inc(s_sum, 1)
                    pe.matmul(by_window[0:WG, GROUPS_W + g:GROUPS_W + g + 1], of, net.ones[0:T, 0:1],
                              start=True, stop=True).then_inc(s_sum, 1)
                pe.wait_ge(s_zero, 2)
                pe.matmul(hist[0:P, 0:T], zero_bf[:, :], zero_bf[:, 0:T], start=True, stop=False,
                          skip_group_check=True).then_inc(s_used, 2)
                with pe.Fori(0, EC // COLS // 2) as g:
                    for k in (0, 1):
                        pe.wait_ge(s_hot, 4 * g + 2 + 2 * k)
                        for j in range(COLS):
                            mm = pe.matmul(hist[0:P, 0:T], lane_hot[k][:, j, :], tile_hot[k][:, j, :],
                                           start=False, stop=False, skip_group_check=True)
                        mm.then_inc(s_used, 1)
                pe.matmul(hist[0:P, 0:T], zero_bf[:, :], zero_bf[:, 0:T], start=False, stop=True,
                          skip_group_check=True).then_inc(s_hist, 1)


def group_edges(net):
    nc, a = net.nc, net.a
    base = net.acc
    dst = base[:, EC:2 * EC].bitcast(I32)
    tiles, lanes = base[:, 2 * EC:3 * EC], base[:, 3 * EC:4 * EC]
    whole, place = base[:, 4 * EC:5 * EC].bitcast(I32), base[:, 5 * EC:6 * EC]
    scal_rows = dram(nc, "scal_rows", [E, 8])
    of_column = "(p c) k -> p c k"
    sources = (a["edge_index"][0:E].rearrange(of_column, c=EC), a["edge_attr"][0:E].rearrange(of_column, c=EC),
               a["edge_attr_8"].rearrange(of_column, c=EC))
    targets = (net.edges, net.attr, scal_rows)
    with net.phase("group") as ph:
        count, offset, junk = ph.sb("count", [P, T]), ph.sb("offset", [P, T]), ph.sb("junk", [P, T])
        to = [ph.sb(f"to{b}", [P, 1], I32) for b in (0, 1)]
        rec = [(ph.sb(f"ids{b}", [P, 2], I32), ph.sb(f"attr{b}", [P, 4]), ph.sb(f"scal{b}", [P, 8])) for b in (0, 1)]
        rows = [ph.sb(f"rows{b}", [P, 8]) for b in (0, 1)]
        cols = [ph.sb(f"cols{b}", [8, P]) for b in (0, 1)]
        s_step, s_count, s_offset, s_place = ph.sem("step"), ph.sem("count"), ph.sem("offset"), ph.sem("place")
        s_rec, s_to, s_sent = [ph.sem("rec0"), ph.sem("rec1")], ph.sem("to"), [ph.sem("sent0"), ph.sem("sent1")]
        s_idle, s_grouped, s_rows = ph.sem("idle"), ph.sem("grouped"), [ph.sem("rows0"), ph.sem("rows1")]
        s_turned, s_flat, s_stored = ph.sem("turned"), ph.sem("flat"), [ph.sem("stored0"), ph.sem("stored1")]

        def unordered(eng):
            return eng.If(eng.value_load(net.flag[0:1, 0:1], min_val=0, max_val=E) > 0)

        with ph.block() as block:
            @block.vector
            def _(dve):
                with unordered(dve):
                    step = Chain(dve, s_step)
                    split_node(step, dve, dst, tiles, lanes, whole)
                    step(dve.tensor_copy(count[:, 0:1], net.below[:, 0:1]))
                    dve.tensor_tensor(count[:, 1:T], net.below[:, 1:T], net.below[:, 0:T - 1],
                                      ALU.subtract).then_inc(s_count, 1)
                    dve.wait_ge(s_offset, 1)
                    dve.tensor_copy(offset[:, :], net.bank[0][0:P, 0:T]).then_inc(s_place, 1)
                    with dve.Fori(0, EC) as c:
                        dve.wait_ge(s_place, 2 * c + 1)
                        dve.scalar_tensor_tensor(junk[:, :], net.iota_i[0:P, 0:T], tiles[:, ds(c, 1)], offset[:, :],
                                                 ALU.is_equal, ALU.mult,
                                                 accum_out=place[:, ds(c, 1)]).then_inc(s_place, 1)
                        dve.wait_ge(s_place, 2 * c + 2)
                        dve.scalar_tensor_tensor(offset[:, :], net.iota_i[0:P, 0:T], tiles[:, ds(c, 1)], offset[:, :],
                                                 ALU.is_equal, ALU.add).then_inc(s_place, 1)
                    dve.wait_ge(s_place, 2 * EC + 1)

                    def stage(t, b, first):
                        if not first:
                            dve.wait_ge(s_sent[b], (t - b) * 24)
                        dve.tensor_copy(to[b][:, :], place[:, ds(t, 1)]).then_inc(s_to, 1)
                    for_tiles(dve, EC, stage)

                    def copy(t, b, first):
                        dve.wait_ge(s_turned, t + 1)
                        if not first:
                            dve.wait_ge(s_stored[b], (t - b) * 8)
                        dve.tensor_copy(cols[b][:, :], net.bank[b][0:8, 0:P]).then_inc(s_flat, 1)
                    for_tiles(dve, EC, copy)

            @block.tensor
            def _(pe):
                with unordered(pe):
                    pe.wait_ge(s_count, 1)
                    pe.matmul(net.bank[0][0:P, 0:T], net.tri[0:P, 0:P], count[:, :], start=True, stop=False,
                              skip_group_check=True)
                    pe.matmul(net.bank[0][0:P, 1:T], net.ones[0:P, 0:P], net.below[:, 0:T - 1], start=False, stop=True,
                              skip_group_check=True).then_inc(s_offset, 1)

                    def turn(t, b, first):
                        pe.wait_ge(s_rows[b], (t - b) * 8 + 16)
                        if not first:
                            pe.wait_ge(s_flat, t - 1)
                        pe.transpose(net.bank[b][0:8, 0:P], rows[b][:, :], net.ident[0:P, 0:P]).then_inc(s_turned, 1)
                    for_tiles(pe, EC, turn)

            @block.sync
            def _(sp):
                with unordered(sp):
                    def load(t, b, first):
                        if not first:
                            sp.wait_ge(s_sent[b], (t - b) * 24)
                        for r, of in zip(rec[b], sources):
                            sp.dma_start(r[:, :], of[:, ds(t, 1), :].rearrange("p c k -> p (c k)")).then_inc(s_rec[b], 16)
                    for_tiles(sp, EC, load)

                    def load_rows(t, b, first):
                        if not first:
                            sp.wait_ge(s_turned, t - 1)
                        sp.dma_start(rows[b][:, :], scal_rows[ds(P * t, P), :]).then_inc(s_rows[b], 16)
                    sp.wait_ge(s_grouped, 1)
                    for_tiles(sp, EC, load_rows)

            @block.gpsimd
            def _(pool):
                with unordered(pool):
                    def send(t, b, first):
                        pool.wait_ge(s_to, t + 1)
                        pool.wait_ge(s_rec[b], (t - b) * 24 + 48)
                        carry_wait(pool, s_idle)
                        for r, target in zip(rec[b], targets):
                            pool.indirect_dma_start(
                                out=target[:, :], out_offset=bass.IndirectOffsetOnAxis(ap=to[b][:, 0:1], axis=0),
                                in_=r[:, :], in_offset=None, bounds_check=E - 1, oob_is_err=False).then_inc(s_sent[b], 16)
                    for_tiles(pool, EC, send)
                    for b in (0, 1):
                        pool.wait_ge(s_sent[b], 24 * EC)
                    pool.sem_inc(s_grouped, 1)

            @block.scalar
            def _(act):
                with unordered(act):
                    def store(t, b, first):
                        act.wait_ge(s_flat, t + 1)
                        act.dma_start(net.scal_t[:, ds(P * t, P)], cols[b][:, :]).then_inc(s_stored[b], 16)
                    for_tiles(act, EC, store)
                    for b in (0, 1):
                        act.wait_ge(s_stored[b], 8 * EC)


def load_windows(net):
    with net.phase("windows") as ph:
        got = [ph.sb(f"got{g}", [WG, 2 * WIN], I32) for g in range(GROUPS_W)]
        src = [ph.sb(f"src{g}", [WG, WIN]) for g in range(GROUPS_W)]
        dst = [ph.sb(f"dst{g}", [WG, WIN]) for g in range(GROUPS_W)]
        s_got, s_flat, s_turned = ph.sem("got"), ph.sem("flat"), ph.sem("turned")
        of_src, of_dst = net.bank[0:2], net.bank[2:4]
        with ph.block() as block:
            @block.gpsimd
            def _(pool):
                for g in range(GROUPS_W):
                    pool.indirect_dma_start(
                        out=got[g][:, :], out_offset=None, in_=net.edges[:, :],
                        in_offset=bass.IndirectOffsetOnAxis(ap=net.first_edge[:, g:g + 1], axis=0)).then_inc(s_got, 16)

            @block.vector
            def _(dve):
                dve.wait_ge(s_got, 16 * GROUPS_W)
                for g in range(GROUPS_W):
                    dve.tensor_copy(src[g][:, :], got[g][:, 0::2]).then_inc(s_flat, 1)
                    dve.tensor_scalar(dst[g][:, :], got[g][:, 1::2], net.base_col[:, g:g + 1], None,
                                      ALU.subtract).then_inc(s_flat, 1)
                dve.wait_ge(s_turned, 2 * GROUPS_W)
                half = WINDOWS // 2
                for k in (0, 1):
                    dve.tensor_copy(net.src_w[:, k * half:(k + 1) * half], of_src[k][:, 0:half])
                    dve.tensor_copy(net.dst_w[:, k * half:(k + 1) * half], of_dst[k][:, 0:half])

            @block.tensor
            def _(pe):
                for g in range(GROUPS_W):
                    pe.wait_ge(s_flat, 2 * g + 2)
                    k, c = divmod(g, GROUPS_W // 2)
                    for of, to in ((src[g], of_src[k]), (dst[g], of_dst[k])):
                        pe.transpose(to[:, WG * c:WG * (c + 1)], of[:, :], net.ident[0:WG, 0:WG]).then_inc(s_turned, 1)



def row_stats(net, dve, t):
    return dve.bn_stats(node_row(net.stats, t), node_row(net.x, t))


def layer_stats(net, tag, factors, measured=False):
    with net.phase(tag) as ph:
        s_stat, s_step, s_var, s_root = ph.sem("stat"), ph.sem("step"), ph.sem("var"), ph.sem("root")
        s_own, s_own2 = ph.sem("own"), ph.sem("own2")
        with ph.block() as block:
            @block.vector
            def _(dve):
                if not measured:
                    with dve.Fori(0, T // STORE) as g:
                        for k in range(STORE):
                            row_stats(net, dve, STORE * g + k).then_inc(s_stat, 1)
                    dve.wait_ge(s_stat, T)
                for t in range(T):
                    dve.bn_aggr(net.mv[:, t, :], net.stats[:, t, :]).then_inc(s_var, 1)
                step = Chain(dve, s_step)
                dve.wait_ge(s_root, 1)
                step(dve.reciprocal(net.rstd[:, :], net.rstd[:, :]))
                step(dve.scalar_tensor_tensor(net.nmr[:, :], net.mv[:, :, 0], -1.0, net.rstd[:, :],
                                              ALU.mult, ALU.mult))
                factors(step, dve, None, s_own, s_own2)

            @block.scalar
            def _(act):
                act.wait_ge(s_var, T)
                act.activation(net.rstd[:, :], net.mv[:, :, 1], ACT.Sqrt, bias=net.eps[0:P, :]).then_inc(s_root, 1)
                factors(None, None, act, s_own, s_own2)


def node_row(view, t):
    return view[:, ds(t, 1), :].rearrange("p a d -> p (a d)")


STORE = 5


def tiles_of(table, first):
    return table[ds(P * first, P * STORE), :].rearrange("(t p) d -> p t d", p=P)


def write_table(net, tag, table, scale, bias):
    with net.phase(tag) as ph:
        row = [ph.sb(f"row{b}", [P, STORE, D]) for b in (0, 1)]
        s_row, s_out = ph.sem("row"), [ph.sem("out0"), ph.sem("out1")]
        with ph.block() as block:
            @block.scalar
            def _(act):
                def body(g, b, first):
                    if not first:
                        act.wait_ge(s_out[b], (g - b) * 8)
                    for k in range(STORE):
                        t = STORE * g + k
                        ins = act.activation(row[b][:, k, :], node_row(net.x, t), ACT.Relu, bias=bias[:, ds(t, 1)],
                                             scale=scale[:, ds(t, 1)])
                    ins.then_inc(s_row, 1)
                for_tiles(act, T // STORE, body)

            @block.sync
            def _(sp):
                def body(g, b, first):
                    sp.wait_ge(s_row, g + 1)
                    sp.dma_start(tiles_of(table, STORE * g), row[b][:, :, :]).then_inc(s_out[b], 16)
                for_tiles(sp, T // STORE, body)
                for b in (0, 1):
                    sp.wait_ge(s_out[b], 16 * (T // STORE // 2))



def aggregate(net, tag, table, width, degrees=False, split=False, clear=True):
    sums = width + 1 if degrees else width
    acc = net.acc_view(sums)
    GROUPS = 4
    PER = WPI // GROUPS
    LEAD = 2
    BANKS = LEAD * PER
    with net.phase(tag) as ph:
        msg = [ph.sb(f"msg{r}", [Q, sums]) for r in range(WPI)]
        hot = [ph.sb(f"hot{r}", [Q, P]) for r in range(WPI)]
        idx = [ph.sb(f"idx{g}", [Q, PER], I32) for g in range(GROUPS)]
        s_idx, s_idle = ph.sem("idx"), ph.sem("idle")
        s_msg = [ph.sem(f"msg{r}") for r in range(WPI)]
        s_hot, s_sum, s_add, s_clear = ph.sem("hot"), ph.sem("sum"), ph.sem("add"), ph.sem("clear")
        s_ones = ph.sem("ones")
        if split:
            whole = ph.sb("whole", [Q, SPLIT])
            parts = [ph.sb(f"part{k}", [Q, SPLIT], BF16) for k in range(3)]
            s_whole, s_parts, s_split = ph.sem("whole"), ph.sem("parts"), ph.sem("split")
            flat_in = net.scal_t.rearrange("k n -> (k n)").rearrange("(p c) -> p c", p=Q)
            flat_out = [net.scal_parts[k].rearrange("k n -> (k n)").rearrange("(p c) -> p c", p=Q) for k in range(3)]
        with ph.block() as block:
            @block.gpsimd
            def _(pool):
                if degrees:
                    for r in range(WPI):
                        pool.memset(msg[r][:, width:sums], 1.0).then_inc(s_ones, 1)
                with pool.Fori(0, STEPS) as i:
                    for g in range(GROUPS):
                        pool.wait_ge(s_idx, GROUPS * i + g + 1)
                        carry_wait(pool, s_idle)
                        for r in range(PER):
                            pool.indirect_dma_start(
                                out=msg[PER * g + r][:, 0:width], out_offset=None, in_=table[:, :],
                                in_offset=bass.IndirectOffsetOnAxis(ap=idx[g][:, r:r + 1], axis=0),
                            ).then_inc(s_msg[PER * g + r], 16)

            @block.vector
            def _(dve):
                def stage(i, r):
                    g = r // PER
                    if r % PER == 0:
                        dve.wait_ge(s_sum, WPI * i + PER * g + PER)
                        dve.tensor_copy(idx[g][:, :].bitcast(F32),
                                        net.src_w[:, ds(WPI * i + PER * g, PER)].bitcast(F32)).then_inc(s_idx, 1)
                    dve.tensor_scalar(hot[r][:, :], net.iota_i[:, 0:P], net.dst_w[:, ds(WPI * i + r, 1)], None,
                                      ALU.is_equal).then_inc(s_hot, 1)

                def add(i, w, tile):
                    dve.wait_ge(s_sum, WPI * i + w + 1 + WPI)
                    dve.wait_ge(s_add, WPI * i + w + 1)
                    row = node_row(acc, tile)
                    dve.tensor_tensor(row, row, net.bank[w % BANKS][0:P, 0:sums], ALU.add).then_inc(s_add, 1)

                def split_step(i, k):
                    if k == 0:
                        dve.wait_ge(s_whole, 16 * i + 16)
                        dve.wait_ge(s_parts, 48 * i + 48)
                    else:
                        dve.wait_ge(s_split, 5 * i + 5 + k)
                    if k % 2 == 0:
                        ins = dve.tensor_copy(parts[k // 2][:, :], whole[:, :])
                    else:
                        ins = dve.tensor_tensor(whole[:, :], whole[:, :], parts[k // 2][:, :], ALU.subtract)
                    ins.then_inc(s_split, 1)

                def steps(i, last):
                    tiles = load_values(dve, net.win_tab[0:1, ds(WPI * i, WPI)], T - 1)
                    for w in range(WPI):
                        add(i, w, tiles[w])
                        if w + BANKS < WPI:
                            stage(i, w + BANKS)
                        elif not last:
                            stage(i + 1, w + BANKS - WPI)
                        if split and 1 <= w <= 9 and w % 2:
                            split_step(i, w // 2)

                if clear:
                    dve.memset(net.acc[:, 0:T * sums], 0.0).then_inc(s_clear, 1)
                dve.sem_inc(s_add, 1)
                for r in range(BANKS):
                    stage(0, r)
                if clear:
                    dve.wait_ge(s_clear, 1)
                with dve.Fori(0, STEPS - 1) as i:
                    steps(i, False)
                steps(STEPS - 1, True)

            @block.tensor
            def _(pe):
                if degrees:
                    pe.wait_ge(s_ones, WPI)
                pe.sem_inc(s_sum, WPI)
                with pe.Fori(0, STEPS) as i:
                    for w in range(WPI):
                        pe.wait_ge(s_hot, WPI * i + w + 1)
                        pe.wait_ge(s_msg[w], 16 * i + 16)
                        pe.matmul(net.bank[w % BANKS][0:P, 0:sums], hot[w][:, :], msg[w][:, :],
                                  start=True, stop=True).then_inc(s_sum, 1)

            if split:
                @block.sync
                def _(sp):
                    sp.sem_inc(s_split, 5)
                    sp.sem_inc(s_parts, 48)
                    with sp.Fori(0, STEPS) as i:
                        sp.wait_ge(s_split, 5 * i + 5)
                        sp.dma_start(whole[:, :], flat_in[:, ds(SPLIT * i, SPLIT)]).then_inc(s_whole, 16)

                @block.scalar
                def _(act):
                    with act.Fori(0, STEPS) as i:
                        act.wait_ge(s_split, 5 * i + 10)
                        for k in range(3):
                            act.dma_start(flat_out[k][:, ds(SPLIT * i, SPLIT)], parts[k][:, :]).then_inc(s_parts, 16)
                    act.wait_ge(s_parts, 48 * STEPS + 48)



def node_stage(net, tag, chunks, load, stage, products, finish, steps=0, store=None):
    with net.phase(tag) as ph:
        rows = [ph.sb(f"rows{b}", [P, chunks * Q]) for b in (0, 1)]
        cols = [ph.sb(f"cols{b}", [Q, chunks, P]) for b in (0, 1)]
        turned, product = net.bank[0:2], net.bank[2:4]
        s_w, s_staged, s_turned, s_copied = ph.sem("w"), ph.sem("staged"), ph.sem("turned"), ph.sem("copied")
        s_product, s_finished, s_step = ph.sem("product"), ph.sem("finished"), ph.sem("step")
        s_stored = [ph.sem("stored0"), ph.sem("stored1")]
        loads = load(None, ph, None)
        with ph.block() as block:
            @block.sync
            def _(sp):
                load(sp, ph, s_w)
                if store:
                    def body(g, b, first):
                        sp.wait_ge(s_finished, STORE * g + STORE)
                        sp.dma_start(tiles_of(store[0], STORE * g), store[1][b][:, :, :]).then_inc(s_stored[b], 16)
                    for_tiles(sp, T // STORE, body)
                    for b in (0, 1):
                        sp.wait_ge(s_stored[b], 16 * (T // STORE // 2))

            @block.scalar
            def _(act):
                def body(t, b, first):
                    if not first:
                        act.wait_ge(s_turned, t - 1)
                    stage(act, t, rows[b]).then_inc(s_staged, 1)
                for_tiles(act, T, body)

            @block.tensor
            def _(pe):
                def turn(t, b, first):
                    pe.wait_ge(s_staged, t + 1)
                    for c in range(chunks):
                        mm = pe.transpose(turned[b][:, c * P:(c + 1) * P], rows[b][:, c * Q:(c + 1) * Q],
                                          net.ident[0:P, 0:P])
                    mm.then_inc(s_turned, 1)

                def body(t, b, first):
                    pe.wait_ge(s_copied, t + 1)
                    if not first:
                        pe.wait_ge(s_finished, t - 1)
                    products(pe, cols[b], product[b]).then_inc(s_product, 1)
                pe.wait_ge(s_w, 16 * loads)
                for_tiles(pe, T, body, ahead=((1, turn),))

            @block.vector
            def _(dve):
                def copy(t, b, turn):
                    dve.wait_ge(s_turned, t + 1)
                    to, of = cols[b % 2][:, :, :].rearrange("p c n -> p (c n)"), turned[b % 2][:, 0:chunks * P]
                    if "bias" in net.got:
                        ins = dve.tensor_scalar(to, of, net.got["bias"][:, :], None, ALU.add)
                    else:
                        ins = dve.tensor_copy(to, of)
                    ins.then_inc(s_copied, 1)

                def body(t, b, turn):
                    dve.wait_ge(s_product, t + 1)
                    if store and b % STORE == 0 and not is_zero(turn):
                        dve.wait_ge(s_stored[b // STORE], 16 * turn)
                    step = Chain(dve, s_step, t * steps)
                    row = store[1][b // STORE][:, b % STORE, :] if store else None
                    finish(dve, step, t, row, product[b % 2]).then_inc(s_finished, 1)
                    assert step.n == steps
                dve.wait_ge(s_w, 16 * loads)
                for_tiles(dve, T, body, ahead=((1, copy),), ring=2 * STORE, turns=True)


def loader(*items):
    def load(sp, ph, sem):
        n = 0
        if sp is None:
            ph.net.got = {}
            for name, shape, _ in items:
                ph.net.got[name] = ph.sb(name, shape)
        for name, _, pairs in items:
            for to, of in pairs(ph.net.got[name]):
                n += 1
                if sp is not None:
                    sp.dma_start(to, of).then_inc(sem, 16)
        return n
    return load


def row_of(vector, parts=P):
    return vector.unsqueeze(0).broadcast_to([parts, vector.shape[0]])


def in_chunks(w):
    return w.rearrange("(c p) n -> p c n", p=Q)



def experts(net, buf, outb):
    nc, a = net.nc, net.a
    xm = net.acc_view(D)
    with ExitStack() as ctx:
        def sb(name, shape, dt=F32):
            return ctx.enter_context(nc.sbuf_tensor(f"moe_{name}", shape, dt))

        mask = sb("mask", [P, T, X_EXP])
        top = sb("top", [P, T, 8])
        top_i = sb("top_i", [P, T, 8], U32)
        exp_of = sb("exp_of", [P, T, 2])
        rank = sb("rank", [P, T, 2])
        gate = sb("gate", [P, T, 2])
        valid = sb("valid", [P, T, 2])
        put = sb("put", [P, T, 2], I32)
        get = sb("get", [P, T, 2], I32)
        exp_tab = sb("exp_tab", [1, MT], I32)

        free = net.acc[:, T * D:2 * T * D]
        logits = free[:, 3 * T * X_EXP:4 * T * X_EXP].rearrange("p (t e) -> p t e", e=X_EXP)

        def stage(act, t, rows):
            return act.activation(rows[:, :], node_row(xm, t), ACT.Copy)

        def products(pe, cols, po):
            for c in (0, 1):
                mm = pe.matmul(po[0:P, 0:X_EXP], cols[:, c, :], net.got["wg"][:, c, :], start=(c == 0), stop=(c == 1))
            return mm

        def finish(dve, step, t, row, po):
            return dve.tensor_tensor(node_row(logits, t), po[0:P, 0:X_EXP], net.got["bg"][:, :], ALU.add)

        node_stage(net, "route", 2, loader(
            ("wg", [Q, 2, X_EXP], lambda w: [(w[:, :, :], in_chunks(a["L0_gnn_Wg"]))]),
            ("bg", [P, X_EXP], lambda w: [(w[:, :], row_of(a["L0_gnn_bg"]))])), stage, products, finish, steps=0)

        with net.phase("rank") as ph:
            counts, col, coli = ph.sb("counts", [P, X_EXP]), ph.sb("col", [X_EXP, 8]), ph.sb("coli", [X_EXP, 1], I32)
            past, tiles_bc, start = ph.sb("past", [X_EXP, MT]), ph.sb("tiles_bc", [X_EXP, P]), ph.sb("start", [P, X_EXP])
            place_of, diff = ph.sb("place_of", [P, T, 2]), ph.sb("diff", [P, T])
            pick = free[:, 0:2 * T * X_EXP].rearrange("p (n e) -> p n e", e=X_EXP)
            place = free[:, 2 * T * X_EXP:3 * T * X_EXP]
            total = free[:, 3 * T * X_EXP:4 * T * X_EXP]
            before = ph.sb("before", [P, T, X_EXP])
            scaled = [before[:, :, :], total.rearrange("p (t e) -> p t e", e=X_EXP)]
            CHUNK = 8
            chunks = [(k, slice(X_EXP * t, X_EXP * min(t + CHUNK, T))) for k, t in enumerate(range(0, T, CHUNK))]
            s_rank, s_place, s_total, s_step = ph.sem("rank"), ph.sem("place"), ph.sem("total"), ph.sem("step")
            s_top, s_mask = ph.sem("top"), ph.sem("mask")
            s_counts, s_cnt, s_tiles, s_end, s_past = (ph.sem("counts"), ph.sem("cnt"), ph.sem("tiles"),
                                                       ph.sem("end"), ph.sem("past"))
            s_rows, s_diff, s_exp, s_zero = ph.sem("rows"), ph.sem("diff"), ph.sem("exp"), ph.sem("zero")
            small, exp_h, start_h = net.bank[2], net.bank[3], net.bank[4]
            with ph.block() as block:
                @block.tensor
                def _(pe):
                    flat = mask[:, :, :].rearrange("p t e -> p (t e)")
                    pe.wait_ge(s_mask, 1)
                    for k, of in chunks:
                        n = of.stop - of.start
                        if k >= 4:
                            pe.wait_ge(s_place, k - 3)
                            pe.wait_ge(s_total, k - 3)
                        pe.matmul(net.bank[2 * (k % 4)][0:P, 0:n], net.tri[0:P, 0:P], flat[:, of], start=True, stop=True)
                        pe.matmul(net.bank[2 * (k % 4) + 1][0:P, 0:n], net.ones[0:P, 0:P], flat[:, of],
                                  start=True, stop=True).then_inc(s_rank, 1)
                    pe.wait_ge(s_place, len(chunks))
                    pe.wait_ge(s_total, len(chunks))
                    pe.wait_ge(s_counts, 1)
                    pe.matmul(small[0:X_EXP, 0:1], counts[:, :], net.ones[0:P, 0:1], start=True, stop=True).then_inc(s_cnt, 1)
                    pe.wait_ge(s_tiles, 1)
                    pe.matmul(small[0:X_EXP, 1:2], net.tri[0:X_EXP, 0:X_EXP], col[:, 1:2], start=True, stop=True)
                    pe.matmul(start_h[0:P, 0:X_EXP], tiles_bc[:, :], net.tri[0:X_EXP, 0:X_EXP],
                              start=True, stop=True).then_inc(s_end, 1)
                    pe.wait_ge(s_past, 1)
                    pe.matmul(exp_h[0:1, 0:MT], net.ones[0:X_EXP, 0:1], past[:, :], start=True, stop=True).then_inc(s_rows, 1)

                @block.scalar
                def _(act):
                    for k, of in chunks:
                        act.wait_ge(s_rank, k + 1)
                        act.activation(total[:, of], net.bank[2 * (k % 4) + 1][0:P, 0:of.stop - of.start],
                                       ACT.Copy).then_inc(s_total, 1)
                    act.wait_ge(s_diff, 1)
                    act.activation(gate[:, :, 1], diff[:, :], ACT.Exp).then_inc(s_exp, 1)

                @block.vector
                def _(dve):
                    for t in range(T):
                        dve.max(top[:, t, :], logits[:, t, :]).then_inc(s_top, 1)
                    dve.wait_ge(s_top, T)
                    for t in range(T):
                        dve.max_index(top_i[:, t, :], top[:, t, :], logits[:, t, :]).then_inc(s_top, 1)
                    dve.tensor_tensor(diff[:, :], top[:, :, 1], top[:, :, 0], ALU.subtract).then_inc(s_diff, 1)
                    dve.memset(before[:, 0, :], 0.0).then_inc(s_zero, 1)
                    dve.wait_ge(s_top, 2 * T)
                    step = Chain(dve, s_step)
                    step(dve.tensor_copy(exp_of[:, :, :], top_i[:, :, 0:2]))
                    chosen = exp_of[:, :, :].rearrange("p t k -> p (t k)")
                    wide = [P, 2 * T, X_EXP]
                    step(dve.tensor_tensor(pick, bc(chosen, 2, wide), bc(net.iota_i[0:P, 0:X_EXP], 1, wide), ALU.is_equal))
                    pick_of = pick.rearrange("p (t k) e -> p t k e", k=2)
                    dve.tensor_tensor(mask[:, :, :], pick_of[:, :, 0, :], pick_of[:, :, 1, :], ALU.add).then_inc(s_mask, 1)
                    dve.wait_ge(s_mask, 1)
                    for k, of in chunks:
                        dve.wait_ge(s_rank, k + 1)
                        dve.tensor_copy(place[:, of], net.bank[2 * (k % 4)][0:P, 0:of.stop - of.start]).then_inc(s_place, 1)
                    dve.tensor_reduce(counts[:, :], mask[:, :, :].rearrange("p t e -> p e t"), AX_X, ALU.add).then_inc(s_counts, 1)
                    dve.wait_ge(s_zero, 1)
                    for t in range(T - 1):
                        if t % CHUNK == 0:
                            dve.wait_ge(s_total, t // CHUNK + 1)
                        step(dve.tensor_tensor(before[:, t + 1, :], before[:, t, :], total[:, X_EXP * t:X_EXP * (t + 1)], ALU.add))
                    places = place.rearrange("p (t e) -> p t e", e=X_EXP)
                    step(dve.tensor_tensor(places, places, before[:, :, :], ALU.add))
                    for k in (0, 1):
                        dve.tensor_tensor(scaled[k], pick_of[:, :, k, :], places, ALU.mult).then_inc(s_step, 1)
                    for k in (0, 1):
                        dve.wait_ge(s_step, step.n + k + 1)
                        dve.tensor_reduce(rank[:, :, k], scaled[k], AX_X, ALU.add)
                    step = Chain(dve, s_step, step.n + 2)
                    dve.wait_ge(s_cnt, 1)
                    step(dve.tensor_scalar(col[:, 0:1], small[0:X_EXP, 0:1], float(CAP), None, ALU.min))
                    ceil_div(step, dve, col[:, 1:2], col[:, 0:1], Q, coli[:, :], col[:, 2:3])
                    dve.tensor_scalar(tiles_bc[:, :], net.ones[0:X_EXP, 0:P], col[:, 1:2], None, ALU.mult).then_inc(s_tiles, 1)
                    dve.wait_ge(s_end, 1)
                    step(dve.tensor_tensor(col[:, 4:5], small[0:X_EXP, 1:2], col[:, 1:2], ALU.add))
                    dve.tensor_scalar(past[:, :], net.iota_i[0:X_EXP, 0:MT], col[:, 4:5], None, ALU.is_ge).then_inc(s_past, 1)
                    step(dve.tensor_scalar(start[:, :], start_h[0:P, 0:X_EXP], float(Q), None, ALU.mult))
                    dve.wait_ge(s_rows, 1)
                    dve.tensor_scalar(exp_tab[:, :], exp_h[0:1, 0:MT], float(X_EXP - 1), None, ALU.min)
                    step(dve.tensor_tensor(pick, pick, bc(start[:, :], 1, wide), ALU.mult))
                    step(dve.tensor_reduce(place_of[:, :, :].rearrange("p t k -> p (t k)"), pick, AX_X, ALU.add))
                    step(dve.tensor_tensor(place_of[:, :, :], place_of[:, :, :], rank[:, :, :], ALU.add))
                    step(dve.tensor_scalar(valid[:, :, :], rank[:, :, :], float(CAP), None, ALU.is_lt))
                    step(dve.tensor_tensor(get[:, :, :], place_of[:, :, :], valid[:, :, :], ALU.mult))
                    step(dve.tensor_scalar(rank[:, :, :], valid[:, :, :], -1e6, 1e6, ALU.mult, ALU.add))
                    step(dve.tensor_tensor(put[:, :, :], place_of[:, :, :], rank[:, :, :], ALU.add))
                    dve.wait_ge(s_exp, 1)
                    step(dve.tensor_scalar(gate[:, :, 0], gate[:, :, 1], 1.0, None, ALU.add))
                    step(dve.reciprocal(gate[:, :, 0], gate[:, :, 0]))
                    step(dve.tensor_tensor(gate[:, :, 1], gate[:, :, 1], gate[:, :, 0], ALU.mult))
                    dve.tensor_tensor(gate[:, :, :], gate[:, :, :], valid[:, :, :], ALU.mult)

        with net.phase("send") as ph:
            row = [ph.sb(f"row{b}", [P, D]) for b in (0, 1)]
            to = [ph.sb(f"to{b}", [P, 2], I32) for b in (0, 1)]
            s_idle = ph.sem("idle")
            s_row, s_to, s_sent = ph.sem("row"), ph.sem("to"), [ph.sem("sent0"), ph.sem("sent1")]
            with ph.block() as block:
                @block.scalar
                def _(act):
                    def body(t, b, first):
                        if not first:
                            act.wait_ge(s_sent[b], (t - b) * 16)
                        act.activation(row[b][:, :], node_row(xm, t), ACT.Copy).then_inc(s_row, 1)
                    for_tiles(act, T, body)

                @block.vector
                def _(dve):
                    def body(t, b, first):
                        if not first:
                            dve.wait_ge(s_sent[b], (t - b) * 16)
                        dve.tensor_copy(to[b][:, :].bitcast(F32), node_row(put, t).bitcast(F32)).then_inc(s_to, 1)
                    for_tiles(dve, T, body)

                @block.gpsimd
                def _(pool):
                    def body(t, b, first):
                        pool.wait_ge(s_row, t + 1)
                        pool.wait_ge(s_to, t + 1)
                        carry_wait(pool, s_idle)
                        for k in (0, 1):
                            pool.indirect_dma_start(
                                out=buf[:, :], out_offset=bass.IndirectOffsetOnAxis(ap=to[b][:, k:k + 1], axis=0),
                                in_=row[b][:, :], in_offset=None, bounds_check=TOK_ROWS - 1, oob_is_err=False,
                            ).then_inc(s_sent[b], 16)
                    for_tiles(pool, T, body)
                    for b in (0, 1):
                        pool.wait_ge(s_sent[b], 16 * T)

        with net.phase("ffn") as ph:
            R = RING = 6
            KD, KH = D // Q, HID // Q
            free = net.acc_full[:, T * D:2 * T * D]
            w1 = [free[:, r * D * HID // Q:(r + 1) * D * HID // Q].rearrange("p (c n) -> p c n", c=KD) for r in range(R)]
            w2 = [free[:, (R + r) * D * HID // Q:(R + r + 1) * D * HID // Q].rearrange("p (c n) -> p c n", c=KH)
                  for r in range(R)]
            b1 = ph.sb("b1", [Q, X_EXP, KH])
            b2 = [ph.sb(f"b2_{r}", [3, D], BF16) for r in range(R)]
            ones = ph.sb("ones", [3, Q], BF16)
            s_b1, s_ones = ph.sem("b1"), ph.sem("ones")
            rows = [ph.sb(f"rows{r}", [Q, D]) for r in range(R)]
            cols = [ph.sb(f"cols{r}", [Q, KD, Q]) for r in (0, 1)]
            hid = [ph.sb(f"hid{r}", [Q, KH, Q]) for r in (0, 1)]
            res = [ph.sb(f"res{r}", [Q, D]) for r in (0, 1)]
            turned, hidden, product = net.bank[0:2], net.bank[2:4], net.bank[4:6]
            s_w = [ph.sem(f"w{r}") for r in range(R)]
            s_in = [ph.sem(f"in{r}") for r in range(R)]
            s_turned, s_copied, s_hidden, s_gelu = ph.sem("turned"), ph.sem("copied"), ph.sem("hidden"), ph.sem("gelu")
            s_product, s_res, s_stored = ph.sem("product"), ph.sem("res"), [ph.sem("st0"), ph.sem("st1")]
            with ph.block() as block:
                @block.sync
                def _(sp):
                    sp.dma_start(b1[:, :, :], a["L0_gnn_b1"].rearrange("e (p j) -> p e j", j=KH)).then_inc(s_b1, 16)

                    def body(t, b, turn):
                        e = sp.value_load(exp_tab[0:1, ds(t, 1)], min_val=0, max_val=X_EXP - 1)
                        r = b % R
                        if not is_zero(turn):
                            sp.wait_ge(s_product, t - R + 1)
                        sp.dma_start(w1[r][:, :, :].rearrange("p c n -> p (c n)"),
                                     a["L0_gnn_w1"][ds(e, 1)].rearrange("e (p c) n -> p (e c n)", c=KD)).then_inc(s_w[r], 16)
                        sp.dma_start(w2[r][:, :, :].rearrange("p c n -> p (c n)"),
                                     a["L0_gnn_w2"][ds(e, 1)].rearrange("e (p c) n -> p (e c n)", c=KH)).then_inc(s_w[r], 16)
                    for_tiles(sp, MT, body, ring=RING, turns=True)

                @block.gpsimd
                def _(pool):
                    def body(t, b, turn):
                        e = pool.value_load(exp_tab[0:1, ds(t, 1)], min_val=0, max_val=X_EXP - 1)
                        r = b % R
                        if not is_zero(turn):
                            pool.wait_ge(s_product, t - R + 1)
                        pool.dma_start(rows[r][:, :], buf[ds(Q * t, Q), :]).then_inc(s_in[r], 16)
                        pool.dma_start(b2[r][:, :], net.b2_parts[:, ds(e, 1), :].rearrange("k e d -> k (e d)")).then_inc(s_in[r], 16)
                    for_tiles(pool, MT, body, ring=RING, turns=True)

                def loaded(eng, sem, b, turn):
                    eng.wait_ge(sem[b], 32 * turn + 32)

                @block.tensor
                def _(pe):
                    def turn(t, b, turn):
                        loaded(pe, s_in, b, turn)
                        if not (is_zero(turn) and b < 2):
                            pe.wait_ge(s_copied, t - 1)
                        for c in range(KD):
                            mm = pe.transpose(turned[b % 2][:, c * Q:(c + 1) * Q], rows[b % R][:, c:D:KD], net.ident[:, :])
                        mm.then_inc(s_turned, 1)

                    def up(t, b, turn):
                        loaded(pe, s_w, b, turn)
                        pe.wait_ge(s_copied, t + 1)
                        if not (is_zero(turn) and b < 2):
                            pe.wait_ge(s_gelu, t - 1)
                        for j in range(KH):
                            for c in range(KD):
                                mm = pe.matmul(hidden[b % 2][:, j * Q:(j + 1) * Q], w1[b % R][:, c, j:HID:KH],
                                               cols[b % 2][:, c, :], start=(c == 0), stop=(c == KD - 1))
                        mm.then_inc(s_hidden, 1)

                    def down(t, b, turn):
                        pe.wait_ge(s_gelu, t + 1)
                        if not (is_zero(turn) and b < 2):
                            pe.wait_ge(s_res, t - 1)
                        for j in range(KH):
                            pe.matmul(product[b % 2][:, 0:D], hid[b % 2][:, j, :], w2[b % R][:, j, :],
                                           start=(j == 0), stop=False)
                        pe.matmul(product[b % 2][:, 0:D], ones[:, :], b2[b % R][:, :], start=False,
                                  stop=True).then_inc(s_product, 1)
                    pe.wait_ge(s_ones, 1)
                    for_tiles(pe, MT, down, ahead=((2, turn), (1, up)), ring=RING, turns=True)

                @block.scalar
                def _(act):
                    def body(t, b, turn):
                        act.wait_ge(s_hidden, t + 1)
                        e = act.value_load(exp_tab[0:1, ds(t, 1)], min_val=0, max_val=X_EXP - 1)
                        if not (is_zero(turn) and b < 2):
                            act.wait_ge(s_product, t - 1)
                        for j in range(KH):
                            ins = act.activation(hid[b % 2][:, j, :], hidden[b % 2][:, j * Q:(j + 1) * Q], ACT.Gelu,
                                                 bias=b1[:, ds(e, 1), j])
                        ins.then_inc(s_gelu, 1)

                    def store(t, b, turn):
                        act.wait_ge(s_res, t + 1)
                        act.dma_start(outb[ds(Q * t, Q), :], res[b % 2][:, :]).then_inc(s_stored[b % 2], 16)
                    act.wait_ge(s_b1, 16)
                    for_tiles(act, MT, store, ahead=((1, body),), ring=RING, turns=True)
                    for b in (0, 1):
                        act.wait_ge(s_stored[b], 16 * (MT // 2))

                @block.vector
                def _(dve):
                    dve.memset(ones[:, :], 1.0).then_inc(s_ones, 1)

                    def copy(t, b, turn):
                        dve.wait_ge(s_turned, t + 1)
                        if not (is_zero(turn) and b < 2):
                            dve.wait_ge(s_hidden, t - 1)
                        dve.tensor_copy(cols[b % 2][:, :, :].rearrange("p c n -> p (c n)"),
                                        turned[b % 2][:, 0:D]).then_inc(s_copied, 1)

                    def body(t, b, turn):
                        dve.wait_ge(s_product, t + 1)
                        if not (is_zero(turn) and b < 2):
                            dve.wait_ge(s_stored[b % 2], 8 * (t - b % 2))
                        dve.tensor_copy(res[b % 2][:, :], product[b % 2][:, 0:D]).then_inc(s_res, 1)
                    for_tiles(dve, MT, body, ahead=((2, copy),), ring=RING, turns=True)

        with net.phase("take") as ph:
            R = 5
            got = [[ph.sb(f"got{b}{k}", [P, D]) for k in (0, 1)] for b in range(R)]
            of = [ph.sb(f"of{b}", [P, 2], I32) for b in range(R)]
            s_idle = ph.sem("idle")
            s_of, s_got, s_y, s_step = ph.sem("of"), [ph.sem(f"got{b}") for b in range(R)], ph.sem("y"), ph.sem("step")
            with ph.block() as block:
                @block.gpsimd
                def _(pool):
                    def body(t, b, turn):
                        pool.wait_ge(s_of, t + 1)
                        carry_wait(pool, s_idle)
                        for k in (0, 1):
                            pool.indirect_dma_start(
                                out=got[b][k][:, :], out_offset=None, in_=outb[:, :],
                                in_offset=bass.IndirectOffsetOnAxis(ap=of[b][:, k:k + 1], axis=0),
                            ).then_inc(s_got[b], 16)
                    for_tiles(pool, T, body, ring=R, turns=True)

                @block.vector
                def _(dve):
                    def ahead(t, b, turn):
                        if not is_zero(turn):
                            dve.wait_ge(s_y, t - R + 1)
                        dve.tensor_copy(of[b][:, :].bitcast(F32), node_row(get, t).bitcast(F32)).then_inc(s_of, 1)

                    def body(t, b, turn):
                        dve.wait_ge(s_got[b], 32 * turn + 32)
                        step = Chain(dve, s_step, t)
                        y = node_row(xm, t)
                        step(dve.scalar_tensor_tensor(y, got[b][0][:, :], gate[:, ds(t, 1), 0], y, ALU.mult, ALU.add))
                        dve.scalar_tensor_tensor(y, got[b][1][:, :], gate[:, ds(t, 1), 1], y,
                                                 ALU.mult, ALU.add).then_inc(s_y, 1)
                    for_tiles(dve, T, body, ahead=((4, ahead),), ring=R, turns=True)

                @block.tensor
                def _(pe):
                    def body(t, b, turn):
                        pe.wait_ge(s_y, t + 1)
                        pe.matmul(net.bank[0][0:P, 0:D], net.ones[0:P, 0:P], node_row(xm, t),
                                  start=is_zero(t), stop=is_zero(t - (T - 1)))
                    for_tiles(pe, T, body, ring=R, turns=True)


def batch_norm(net):
    a = net.a
    y = net.acc_view(D)
    sq = net.acc[:, T * D:2 * T * D].rearrange("p (t d) -> p t d", d=D)
    PART = 10
    parts = [slice(t, t + PART) for t in range(0, T, PART)]
    with net.phase("bn") as ph:
        mean, scale = ph.sb("mean", [P, D]), ph.sb("scale", [P, D])
        gamma, beta = ph.sb("gamma", [P, D]), ph.sb("beta", [P, D])
        s_w, s_all, s_step, s_yc, s_sq = ph.sem("w"), ph.sem("all"), ph.sem("step"), ph.sem("yc"), ph.sem("sq")
        s_var, s_root, s_beta = ph.sem("var"), ph.sem("root"), ph.sem("beta")
        wide = [P, PART, D]
        with ph.block() as block:
            @block.sync
            def _(sp):
                sp.dma_start(gamma[:, :], row_of(a["L0_gnn_gamma"])).then_inc(s_w, 16)
                sp.dma_start(beta[:, :], row_of(a["L0_gnn_beta"])).then_inc(s_w, 16)

            @block.tensor
            def _(pe):
                for t in range(T):
                    if t % PART == 0:
                        pe.wait_ge(s_sq, t // PART + 1)
                    mm = pe.matmul(net.bank[1][0:P, 0:D], net.ones[0:P, 0:P], sq[:, t, :], start=(t == 0), stop=(t == T - 1))
                mm.then_inc(s_all, 1)

            @block.scalar
            def _(act):
                for k, part in enumerate(parts):
                    act.wait_ge(s_yc, k + 1)
                    act.activation(sq[:, part, :], y[:, part, :], ACT.Square).then_inc(s_sq, 1)
                act.wait_ge(s_var, 1)
                act.activation(scale[:, :], scale[:, :], ACT.Sqrt).then_inc(s_root, 1)

            @block.gpsimd
            def _(pool):
                pool.wait_ge(s_w, 32)
                for part in parts:
                    pool.tensor_tensor(net.x[:, part, :], net.x[:, part, :], bc(beta[:, :], 1, wide), ALU.add).then_inc(s_beta, 1)

            @block.vector
            def _(dve):
                step = Chain(dve, s_step)
                step(dve.tensor_scalar(mean[:, :], net.bank[0][0:P, 0:D], 1.0 / N, None, ALU.mult))
                for part in parts:
                    dve.tensor_tensor(y[:, part, :], y[:, part, :], bc(mean[:, :], 1, wide), ALU.subtract).then_inc(s_yc, 1)
                dve.wait_ge(s_all, 1)
                dve.tensor_scalar(scale[:, :], net.bank[1][0:P, 0:D], 1.0 / N, BN_EPS, ALU.mult, ALU.add).then_inc(s_var, 1)
                dve.wait_ge(s_root, 1)
                step(dve.reciprocal(scale[:, :], scale[:, :]))
                dve.wait_ge(s_w, 32)
                step(dve.tensor_tensor(scale[:, :], scale[:, :], gamma[:, :], ALU.mult))
                for part in parts:
                    dve.tensor_tensor(y[:, part, :], y[:, part, :], bc(scale[:, :], 1, wide), ALU.mult).then_inc(s_step, 1)
                for k, part in enumerate(parts):
                    dve.wait_ge(s_step, step.n + k + 1)
                    dve.wait_ge(s_beta, k + 1)
                    dve.tensor_tensor(net.x[:, part, :], net.x[:, part, :], y[:, part, :], ALU.add)



PAIRS = 3 * 3 * 8
BL = 8

def tensor_product_edges(net, table):
    a = net.a
    acc = net.acc_view(2 * D)
    R = 8
    with net.phase("tp") as ph:
        attr = [ph.sb(f"attr{r}", [Q, 4]) for r in range(R)]
        scal = [ph.sb(f"scal{r}", [PAIRS, WIN], BF16) for r in range(R)]
        fc1, fc2 = ph.sb("fc1", [8, MUL]), ph.sb("fc2", [MUL, 4, MUL])
        fc1_parts = [ph.sb(f"fc1_part{k}", [8, MUL], BF16) for k in range(3)]
        fc1_pairs = ph.sb("fc1_pairs", [PAIRS, MUL], BF16)
        hid = [ph.sb(f"hid{r}", [MUL, WIN]) for r in (0, 1)]
        src = [ph.sb(f"src{r}", [Q, D]) for r in range(R)]
        idx = [ph.sb(f"idx{r}", [Q, 2], I32) for r in range(R // 2)]
        hot = [ph.sb(f"hot{r}", [Q, P]) for r in range(R)]
        hots = [ph.sb(f"hots{r}", [Q, 4, P]) for r in range(4)]
        msg = [ph.sb(f"msg{r}", [Q, BL, MUL]) for r in range(4)]
        s_fc, s_fcs, s_attr = ph.sem("fc"), ph.sem("fcs"), [ph.sem(f"attr{r}") for r in range(R)]
        s_fc1, s_pairs = ph.sem("fc1"), ph.sem("pairs")
        s_idx, s_src, s_idle = ph.sem("idx"), [ph.sem(f"src{r}") for r in range(R)], ph.sem("idle")
        s_z, s_hid, s_w = ph.sem("z"), ph.sem("hid"), ph.sem("w")
        s_hot, s_hots, s_msg, s_sum, s_add = ph.sem("hot"), ph.sem("hots"), ph.sem("msg"), ph.sem("sum"), ph.sem("add")
        s_zero = ph.sem("zero")
        zb, wb, ab = net.bank[0:2], net.bank[2:4], net.bank[4:8]
        LOADS = {0: 2, 2: 4, 6: 2}
        fc2_of = (0, 2, 3, 1)

        def fresh(first, b, n):
            return first and b < n

        with ph.block() as block:
            @block.sync
            def _(sp):
                sp.dma_start(fc1[:, :], a["L3_gnn_fc_w1"][:, :]).then_inc(s_fc, 16)
                for k, of in enumerate(fc2_of):
                    sp.dma_start(fc2[:, k, :], a["L3_gnn_fc_w2"][:, of * MUL:(of + 1) * MUL]).then_inc(s_fc, 16)
                sp.wait_ge(s_fc1, 5)
                for k in range(3):
                    for m in range(3):
                        row = 8 * (3 * k + m)
                        sp.dma_start(fc1_pairs[row:row + 8, :], fc1_parts[k][:, :]).then_inc(s_pairs, 16)

                first_edges = [None] * R

                def body(w, b, first):
                    if b == 0:
                        first_edges[:] = load_values(sp, net.win_tab[0:1, ds(WINDOWS + w, R)], E)
                    e0 = first_edges[b]
                    if not fresh(first, b, R):
                        sp.wait_ge(s_sum, w - R + 1)
                    sp.dma_start(attr[b][:, :], net.attr[ds(e0, WIN), :]).then_inc(s_attr[b], 16)
                    of = net.scal_parts.rearrange("m k n -> (m k) n")[:, ds(e0, WIN)]
                    sp.dma_start(scal[b][:, :], of.unsqueeze(0).broadcast_to([3, PAIRS // 3, WIN])).then_inc(s_attr[b], 16)
                for_tiles(sp, WINDOWS, body, ring=R)

            @block.gpsimd
            def _(pool):
                def body(w, b, first):
                    if b % 2 == 0:
                        pool.wait_ge(s_idx, w + 2)
                        carry_wait(pool, s_idle)
                    pool.indirect_dma_start(
                        out=src[b][:, :], out_offset=None, in_=table[:, :],
                        in_offset=bass.IndirectOffsetOnAxis(ap=idx[b // 2][:, b % 2:b % 2 + 1], axis=0)).then_inc(s_src[b], 16)
                for_tiles(pool, WINDOWS, body, ring=R)

            @block.scalar
            def _(act):
                def hidden(w, b, first):
                    act.wait_ge(s_z, w + 1)
                    if not fresh(first, b, 2):
                        act.wait_ge(s_w, w - 1)
                    act.activation(hid[b % 2][:, :], zb[b % 2][0:MUL, 0:WIN], ACT.Silu, scale=8 ** -0.5).then_inc(s_hid, 1)

                def body(w, b, first):
                    act.wait_ge(s_hot, w + 1)
                    act.wait_ge(s_attr[b], 4 * (w - b) + 32)
                    if not fresh(first, b, 4):
                        act.wait_ge(s_sum, w - 3)
                    for c in range(4):
                        ins = act.activation(hots[b % 4][:, c, :], hot[b][:, :], ACT.Copy, scale=attr[b][:, c:c + 1])
                    ins.then_inc(s_hots, 1)
                for_tiles(act, WINDOWS, body, ahead=((2, hidden),), ring=R)

            @block.tensor
            def _(pe):
                def first_product(w, b, first):
                    pe.wait_ge(s_attr[b], 4 * (w - b) + 32)
                    if not fresh(first, b, 2):
                        pe.wait_ge(s_hid, w - 1)
                    pe.matmul(zb[b % 2][0:MUL, 0:WIN], fc1_pairs[:, :], scal[b][:, :], start=True, stop=True).then_inc(s_z, 1)

                def second_product(w, b, first):
                    pe.wait_ge(s_hid, w + 1)
                    if not fresh(first, b, 2):
                        pe.wait_ge(s_msg, w - 1)
                    pe.matmul(wb[b % 2][:, 0:4 * MUL], hid[b % 2][:, :], fc2[:, :, :].rearrange("p b n -> p (b n)"),
                              start=True, stop=True).then_inc(s_w, 1)

                def body(w, b, first):
                    if not fresh(first, b, 4):
                        pe.wait_ge(s_add, w - 3)
                    pe.wait_ge(s_msg, w + 1)
                    pe.wait_ge(s_hots, w + 1)
                    m, h = msg[b % 4], hots[b % 4]
                    out = ab[b % 4][0:P, :].rearrange("p (b n) -> p b n", n=MUL)
                    pe.matmul(out[:, 0:4, :], h[:, 0, :], m[:, 0:4, :], start=True, stop=False, skip_group_check=True)
                    for c in range(3):
                        mm = pe.matmul(out[:, 4 + c:8:3 - c, :], h[:, 1 + c, :], m[:, 4:6 + c:1 + c, :],
                                       start=False, stop=(c == 2), skip_group_check=True)
                    mm.then_inc(s_sum, 1)
                pe.wait_ge(s_fc, 16 * 5)
                pe.wait_ge(s_fcs, 2)
                pe.wait_ge(s_pairs, 16 * 9)
                for_tiles(pe, WINDOWS, body, ahead=((3, first_product), (2, second_product)), ring=R)

            @block.vector
            def _(dve):
                dve.memset(net.acc[:, :], 0.0).then_inc(s_zero, 1)
                dve.wait_ge(s_fc, 16 * 5)
                split_parts(Chain(dve, s_fc1), dve, [part[:, :] for part in fc1_parts], fc1[:, :])
                dve.tensor_scalar(fc2[:, 0:3, :], fc2[:, 0:3, :], 1.679 * MUL ** -0.5, None, ALU.mult).then_inc(s_fcs, 1)
                dve.tensor_scalar(fc2[:, 3, :], fc2[:, 3, :], 1.679 * MUL ** -0.5 * 3 ** -0.5, None, ALU.mult).then_inc(s_fcs, 1)

                def stage(w, b, first):
                    if b % 2 == 0:
                        if not fresh(first, b, R):
                            dve.wait_ge(s_sum, w - R + 2)
                        dve.tensor_copy(idx[b // 2][:, :].bitcast(F32),
                                        net.src_w[:, ds(w, 2)].bitcast(F32)).then_inc(s_idx, 2)
                    dve.tensor_scalar(hot[b][:, :], net.iota_i[:, 0:P], net.dst_w[:, ds(w, 1)], None,
                                      ALU.is_equal).then_inc(s_hot, 1)

                tiles = {}

                def add(w, tile, bank, very_first):
                    dve.wait_ge(s_sum, w + 1)
                    if not very_first:
                        dve.wait_ge(s_add, w)
                    row = node_row(acc, tile)
                    dve.tensor_tensor(row, row, bank[0:P, :], ALU.add).then_inc(s_add, 1)

                def body(w, b, first):
                    dve.wait_ge(s_src[b], 2 * (w - b) + 16)
                    dve.wait_ge(s_w, w + 1)
                    if not fresh(first, b, 4):
                        dve.wait_ge(s_sum, w - 3)
                    m = msg[b % 4][:, :, :]
                    wv = wb[b % 2][:, 0:4 * MUL].rearrange("p (b n) -> p b n", n=MUL)
                    sv = src[b][:, :].rearrange("p (b n) -> p b n", n=MUL)
                    dve.tensor_tensor(m[:, 0:8:4, :], wv[:, 0:2, :], sv[:, 0:1, :].broadcast_to([Q, 2, MUL]), ALU.mult)
                    quad = m.rearrange("p (g k) n -> p g k n", g=2)[:, :, 1:4, :]
                    dve.tensor_tensor(quad, bc(wv[:, 2:4, :], 2, [Q, 2, 3, MUL]),
                                      bc(sv[:, 1:4, :], 1, [Q, 2, 3, MUL]), ALU.mult).then_inc(s_msg, 1)
                    if not fresh(first, b, 2):
                        if b in LOADS:
                            loaded = load_values(dve, net.win_tab[0:1, ds(w - 2, LOADS[b])], T - 1)
                            tiles.update({b + k: tile for k, tile in enumerate(loaded)})
                        add(w - 2, tiles[b], ab[(b - 2) % 4], fresh(first, b, 3))
                dve.wait_ge(s_zero, 1)
                for_tiles(dve, WINDOWS, body, ahead=((4, stage),), ring=R)
                last = load_values(dve, net.win_tab[0:1, WINDOWS - 2:WINDOWS], T - 1)
                for k, w in enumerate((WINDOWS - 2, WINDOWS - 1)):
                    add(w, last[k], ab[w % 4], False)


def gnn_kernel(nc, a, out):
    with ExitStack() as ctx:
        net = Net(nc, ctx, a)
        table0, table1 = dram(nc, "table0", [N, D]), dram(nc, "table1", [N, D])
        table2, table3 = dram(nc, "table2", [N, D // 2]), dram(nc, "table3", [N, D])
        buf, outb = dram(nc, "token_rows", [TOK_ROWS, D]), dram(nc, "expert_rows", [TOK_ROWS, D])
        prepare(net, buf)
        group_edges(net)
        load_windows(net)
        acc256, acc128, acc512 = net.acc_view(D), net.acc_view(D // 2), net.acc_view(2 * D)

        def relu_norm(act, t, rows):
            return act.activation(rows, node_row(net.x, t), ACT.Relu, bias=net.nmr[:, ds(t, 1)],
                                  scale=net.rstd[:, ds(t, 1)])

        def four_products(pe, cols, po):
            for c in range(4):
                mm = pe.matmul(po[0:P, 0:D], cols[:, c, :], net.got["w"][:, c, :], start=(c == 0), stop=(c == 3))
            return mm

        def factors0(step, dve, act, s1, s2):
            if act:
                act.activation(net.rb[:, :], net.deg_out[:, :], ACT.Sqrt).then_inc(s1, 1)
            else:
                dve.wait_ge(s1, 1)
                step(dve.reciprocal(net.rb[:, :], net.rb[:, :]))
                step(dve.tensor_tensor(net.rc[:, :], net.rb[:, :], net.nmr[:, :], ALU.mult))
                step(dve.tensor_tensor(net.ra[:, :], net.rb[:, :], net.rstd[:, :], ALU.mult))
        layer_stats(net, "ln0", factors0)
        write_table(net, "tab0", table0, net.ra, net.rc)

        aggregate(net, "agg0", table0, D, degrees=True)
        root_of_degree(net)

        acc257 = net.acc_view(D + 1)

        def stage0(act, t, rows, of=acc257):
            act.activation(rows[:, 0:D], node_row(of, t)[:, 0:D], ACT.Copy, scale=net.rb[:, ds(t, 1)])
            return relu_norm(act, t, rows[:, D:2 * D])

        def finish0(dve, step, t, row, po):
            row = node_row(acc256, t)
            step(dve.tensor_tensor(row, po[0:P, 0:D], net.got["b1"][:, :], ALU.add))
            return dve.tensor_tensor(row, row, net.got["b2"][:, :], ALU.add)
        node_stage(net, "node0", 4, loader(
            ("w", [Q, 4, D], lambda w: [(w[:, 0:2, :], in_chunks(a["L0_gnn_W_gc"])), (w[:, 2:4, :], in_chunks(a["L0_gnn_W_res"]))]),
            ("b1", [P, D], lambda w: [(w[:, :], row_of(a["L0_gnn_b_gc"]))]),
            ("b2", [P, D], lambda w: [(w[:, :], row_of(a["L0_gnn_b_res"]))])), stage0, four_products, finish0, steps=1)
        experts(net, buf, outb)
        batch_norm(net)

        def factors1(step, dve, act, s1, s2):
            if dve:
                step(dve.tensor_scalar(net.rb[:, :], net.deg_in[:, :], 1.0, None, ALU.max))
                step(dve.reciprocal(net.rb[:, :], net.rb[:, :]))
        layer_stats(net, "ln1", factors1)
        write_table(net, "tab1", table1, net.rstd, net.nmr)
        aggregate(net, "agg1", table1, D, split=True)

        def finish1(dve, step, t, row, po):
            row = node_row(net.x, t)
            step(dve.tensor_tensor(row, po[0:P, 0:D], row, ALU.add))
            step(dve.tensor_tensor(row, row, net.got["b"][:, :], ALU.add))
            return row_stats(net, dve, t)
        node_stage(net, "node1", 4, loader(
            ("w", [Q, 4, D], lambda w: [(w[:, 0:2, :], in_chunks(a["L1_w_neigh_t"])), (w[:, 2:4, :], in_chunks(a["L1_w_self_t"]))]),
            ("b", [P, D], lambda w: [(w[:, :], row_of(a["L1_gnn_b_self"]))])), lambda act, t, rows: stage0(act, t, rows, acc256), four_products, finish1, steps=2)

        half = D // 2

        def factors2(step, dve, act, s1, s2):
            if act:
                act.wait_ge(s2, 1)
                act.activation(net.ra[:, :], net.ra[:, :], ACT.Sqrt).then_inc(s1, 1)
            else:
                dve.tensor_scalar(net.ra[:, :], net.deg_in[:, :], 1.0, None, ALU.add).then_inc(s2, 1)
                dve.wait_ge(s1, 1)
                step(dve.reciprocal(net.ra[:, :], net.ra[:, :]))
        layer_stats(net, "ln2", factors2, measured=True)
        with ExitStack() as c2:
            out2 = [c2.enter_context(nc.sbuf_tensor(f"out2_{b}", [P, STORE, half], F32)) for b in (0, 1)]

            def stage2(act, t, rows):
                return relu_norm(act, t, rows[:, :])

            def products2(pe, cols, po):
                for c in (0, 1):
                    mm = pe.matmul(po[0:P, 0:half], cols[:, c, :], net.got["w"][:, c, :], start=(c == 0), stop=(c == 1))
                return mm

            def finish2(dve, step, t, row, po):
                dve.tensor_scalar(node_row(acc128, t), po[0:P, 0:half], net.ra[:, ds(t, 1)], None, ALU.mult)
                return dve.tensor_scalar(row, po[0:P, 0:half], net.ra[:, ds(t, 1)], None, ALU.mult)

            node_stage(net, "node2", 2, loader(
                ("w", [Q, 2, half], lambda w: [(w[:, :, :], in_chunks(a["L2_gnn_W_conv"]))])),
                stage2, products2, finish2, steps=0, store=(table2, out2))
        aggregate(net, "agg2", table2, half, clear=False)

        def stage2b(act, t, rows):
            return act.activation(rows[:, :], node_row(acc128, t), ACT.Copy, scale=net.ra[:, ds(t, 1)])

        def products2b(pe, cols, po):
            return pe.matmul(po[0:P, 0:D], cols[:, 0, :], net.got["w"][:, 0, :], start=True, stop=True)
        node_stage(net, "node2b", 1, loader(
            ("w", [Q, 1, D], lambda w: [(w[:, 0, :], a["L2_gnn_W_lin"][:, :])]),
            ("bias", [Q, 1], lambda w: [(w[:, :], a["L2_gnn_b_conv"].unsqueeze(1))]),
            ("b", [P, D], lambda w: [(w[:, :], row_of(a["L2_gnn_b_lin"]))])), stage2b, products2b, finish1, steps=2)

        inv_mul = MUL ** -0.5
        c_s, c_x = float(np.sin(np.pi / 8)), float(np.cos(np.pi / 8))

        def factors3(step, dve, act, s1, s2):
            if dve:
                step(dve.tensor_scalar(net.ra[:, :], net.rc[:, :], inv_mul, None, ALU.mult))
                step(dve.tensor_scalar(net.rb[:, :], net.rc[:, :], c_s * inv_mul, None, ALU.mult))
                step(dve.tensor_scalar(net.rc[:, :], net.rc[:, :], c_x * (2 * MUL) ** -0.5 * 20.0 ** -0.5, None, ALU.mult))
        load_node_attr(net)
        layer_stats(net, "ln3", factors3, measured=True)
        parts = "p (u c) -> p c u"
        with ExitStack() as c3:
            out3 = [c3.enter_context(nc.sbuf_tensor(f"out3_{b}", [P, STORE, D], F32)) for b in (0, 1)]

            def stage3(act, t, rows):
                relu_norm3 = dict(bias=net.nmr[:, ds(t, 1)], scale=net.rstd[:, ds(t, 1)])
                xr = node_row(net.x, t)
                act.activation(rows[:, 0:MUL], xr[:, 0:MUL], ACT.Relu, **relu_norm3)
                return act.activation(rows[:, MUL:D].rearrange("p (c u) -> p c u", c=3),
                                      xr[:, MUL:D].rearrange(parts, c=3), ACT.Relu, **relu_norm3)

            def products3(pe, cols, po):
                w = net.got["w"]
                for c in (0, 1):
                    pe.matmul(po[0:P, c * Q:(c + 1) * Q], cols[:, c, :], w[:, c, :], start=(c == 0), stop=True,
                              skip_group_check=True)
                    mm = pe.matmul(po[0:P, D + c * Q:D + (c + 1) * Q], cols[:, c, :], w[:, 2 + c, :], start=False,
                                   stop=True, skip_group_check=True)
                return mm

            def finish3(dve, step, t, row, po):
                dve.tensor_scalar(row, po[0:P, 0:D], net.ra[:, ds(t, 1)], None, ALU.mult)
                xr = node_row(net.x, t)
                dve.scalar_tensor_tensor(xr[:, 0:MUL], po[0:P, D:D + MUL], net.rb[:, ds(t, 1)], xr[:, 0:MUL],
                                         ALU.mult, ALU.add)
                x1 = xr[:, MUL:D].rearrange(parts, c=3)
                return dve.scalar_tensor_tensor(x1, po[0:P, D + MUL:2 * D].rearrange("p (c u) -> p c u", c=3),
                                                net.rb[:, ds(t, 1)], x1, ALU.mult, ALU.add)

            node_stage(net, "node3", 2, loader(("w", [Q, 4, Q], lambda w: [
                (w[:, k, :], a["L3_w_pairs"][k]) for k in range(4)])), stage3, products3, finish3, steps=0, store=(table3, out3))
        tensor_product_edges(net, table3)

        with ExitStack() as c4:
            out4 = [c4.enter_context(nc.sbuf_tensor(f"out4_{b}", [P, STORE, D], F32)) for b in (0, 1)]

            def stage4(act, t, rows):
                of = node_row(acc512, t).rearrange("p (b u) -> p b u", u=MUL)
                to = rows[:, :].rearrange("p (b u) -> p b u", u=MUL)
                act.activation(to[:, 0, :], of[:, 0, :], ACT.Copy)
                act.activation(to[:, 1, :], of[:, 7, :], ACT.Copy)
                act.activation(to[:, 2:8:2, :], of[:, 4:7, :], ACT.Copy)
                return act.activation(to[:, 3:8:2, :], of[:, 1:4, :], ACT.Copy)

            def products4(pe, cols, po):
                w = net.got["w"]
                for c in range(4):
                    mm = pe.matmul(po[0:P, c * MUL:(c + 1) * MUL], cols[:, c, :], w[:, min(c, 1), :], start=(c == 0),
                                   stop=True, skip_group_check=True)
                return mm

            def finish4(dve, step, t, row, po):
                xr = node_row(net.x, t)
                sc = net.rc[:, ds(t, 1)]
                dve.scalar_tensor_tensor(row[:, 0:MUL], po[0:P, 0:MUL], sc, xr[:, 0:MUL], ALU.mult, ALU.add)
                return dve.scalar_tensor_tensor(row[:, MUL:D].rearrange(parts, c=3),
                                                po[0:P, MUL:D].rearrange("p (c u) -> p c u", c=3), sc,
                                                xr[:, MUL:D].rearrange(parts, c=3), ALU.mult, ALU.add)

            node_stage(net, "node4", 4, loader(("w", [Q, 2, MUL], lambda w: [
                (w[MUL * h:MUL * (h + 1), k, :], a["L3_gnn_lin2_w" + n][:, :])
                for k, h, n in ((0, 0, "00"), (0, 1, "01"), (1, 0, "10"), (1, 1, "11"))])),
                stage4, products4, finish4, steps=0, store=(out, out4))


def root_of_degree(net):
    degree = net.acc_view(D + 1)[:, :, D]
    with net.phase("root") as ph:
        s_clip, s_root, s_step = ph.sem("clip"), ph.sem("root"), ph.sem("step")
        with ph.block() as block:
            @block.vector
            def _(dve):
                dve.tensor_copy(net.deg_in[:, :], degree)
                dve.tensor_scalar(net.rb[:, :], degree, 1.0, None, ALU.max).then_inc(s_clip, 1)
                dve.wait_ge(s_root, 1)
                dve.reciprocal(net.rb[:, :], net.rb[:, :]).then_inc(s_step, 1)

            @block.scalar
            def _(act):
                act.wait_ge(s_clip, 1)
                act.activation(net.rb[:, :], net.rb[:, :], ACT.Sqrt).then_inc(s_root, 1)


def load_node_attr(net):
    with net.phase("attr") as ph:
        s_w, s_t = ph.sem("w"), ph.sem("t")
        rows = ph.sb("rows", [T, P])
        with ph.block() as block:
            @block.sync
            def _(sp):
                sp.dma_start(rows[:, :], net.a["node_vec1"].rearrange("(t p) k -> t (p k)", p=P)).then_inc(s_w, 16)

            @block.tensor
            def _(pe):
                pe.wait_ge(s_w, 16)
                pe.transpose(net.bank[0][0:P, 0:T], rows[:, :], net.ident[0:T, 0:T]).then_inc(s_t, 1)

            @block.vector
            def _(dve):
                dve.wait_ge(s_t, 1)
                dve.tensor_copy(net.rc[:, :], net.bank[0][0:P, 0:T])


_OUT_SHAPE = (N, D)


def kernel(**inputs):
    import concourse.bacc as _bacc
    from concourse.bass_utils import run_bass_kernel_spmd as _run

    src, dst = np.asarray(inputs["src"]), np.asarray(inputs["dst"])
    arrays = {}
    edge_index = np.full((EPAD, 2), -1, np.int32)
    edge_index[:E, 0], edge_index[:E, 1] = src, dst
    edge_index[E:, 0] = 0
    arrays["edge_index"] = edge_index
    arrays["edge_attr"] = np.zeros((EPAD, 4), np.float32)
    arrays["edge_attr"][:E] = inputs["edge_attr_4"]
    arrays["edge_scal_t"] = np.zeros((8, EPAD), np.float32)
    arrays["edge_scal_t"][:, :E] = np.asarray(inputs["edge_attr_8"]).T
    arrays["L1_w_neigh_t"] = np.ascontiguousarray(np.asarray(inputs["L1_gnn_w_neigh"]).T)
    arrays["L1_w_self_t"] = np.ascontiguousarray(np.asarray(inputs["L1_gnn_w_self"]).T)
    arrays["L3_w_pairs"] = np.zeros((4, 2 * MUL, 2 * MUL), np.float32)
    for k, (top, low) in enumerate((("lin1_w0", "lin1_w1"), ("lin1_w1", "lin1_w1"), ("sc_w0", "sc_w1"), ("sc_w1", "sc_w1"))):
        arrays["L3_w_pairs"][k, :MUL, :MUL] = inputs["L3_gnn_" + top]
        arrays["L3_w_pairs"][k, MUL:, MUL:] = inputs["L3_gnn_" + low]
    laid_out = ("edge_attr_4", "L1_gnn_w_neigh", "L1_gnn_w_self", "L3_gnn_sc_w0", "L3_gnn_sc_w1",
                "L3_gnn_lin1_w0", "L3_gnn_lin1_w1")
    for name in inputs:
        if name not in laid_out:
            arrays[name] = np.ascontiguousarray(inputs[name])
    nc = _bacc.Bacc("TRN2", target_bir_lowering=False, num_devices=1)
    a = {name: nc.dram_tensor(f"in_{name}_dram", v.shape, mybir.dt.from_np(v.dtype), kind="ExternalInput").ap()
         for name, v in arrays.items()}
    out = nc.dram_tensor("out_0_dram", _OUT_SHAPE, F32, kind="ExternalOutput").ap()
    gnn_kernel(nc, a, out)
    r = _run(nc, [{f"in_{k}_dram": v for k, v in arrays.items()}], core_ids=[0])
    return r.results[0]["out_0_dram"]
```
